# Optimizing a Trainium2 kernel written in Bass

```python
import numpy as np
import jax
import jax.numpy as jnp

def _softmax(x, axis=-1):
    return jax.nn.softmax(x, axis=axis)

def _gelu(x):
    return jax.nn.gelu(x, approximate=True)

def _silu(x):
    return jax.nn.silu(x)

def _sigmoid(x):
    return jax.nn.sigmoid(x)

def _layernorm(x, axis=-1, eps=1e-05):
    m = jnp.mean(x, axis=axis, keepdims=True)
    v = jnp.var(x, axis=axis, keepdims=True)
    return (x - m) / jnp.sqrt(v + eps)

def _scatter_add(tgt, idx, src, axis=0):
    return tgt.at[idx].add(src)

def _segment_sum(src, seg, n):
    return jax.ops.segment_sum(src, seg, n)
kernel_name = 'mk_gnn_resnorm_d4_gnn_r32_fde617'

def setup_inputs(seed: int=0):
    np.random.seed(seed)
    _w = jnp.asarray

    def _rec_inputs():
        import jax
        import jax.numpy as jnp
        _gk = jax.random.key(seed)
        x = -0.0005963 + 1.001 * jax.random.normal(jax.random.fold_in(_gk, 1), (128, 768), jnp.float32)
        _s = jax.random.randint(jax.random.fold_in(_gk, 2), (1024,), 0, 128, jnp.int32)
        _d = jax.random.randint(jax.random.fold_in(_gk, 3), (1024,), 0, 128, jnp.int32)
        _loop = jnp.arange(128, dtype=jnp.int32)
        src = jnp.concatenate([_s, _d, _loop])
        dst = jnp.concatenate([_d, _s, _loop])
        _o = jnp.argsort(dst, stable=True)
        src = src[_o]
        dst = dst[_o]
        edge_attr_256 = 0.000121155 + 1.00018 * jax.random.normal(jax.random.fold_in(_gk, 12), (2176, 256), jnp.float32)
        return (x, src, dst, edge_attr_256)
    x, src, dst, edge_attr_256 = _rec_inputs()

    def _L0_gnn_setup():
        import jax, jax.numpy as jnp
        import numpy as np
        N_NODES = 128
        N_EDGES = 4096
        D = 768
        DE = 256
        L = 3
        H = 8
        DH = D // H
        EPS = 1e-05

        def _layernorm(x, g, b):
            mu = jnp.mean(x, axis=-1, keepdims=True)
            var = jnp.var(x, axis=-1, keepdims=True)
            return (x - mu) * jax.lax.rsqrt(var + EPS) * g + b
        key = jax.random.key(seed)
        ks = jax.random.split(key, 20)
        s = 0.02
        inp = {'node_features': jax.random.normal(ks[0], (N_NODES, D), jnp.float32), 'edge_index': jax.random.randint(ks[1], (2, N_EDGES), 0, N_NODES, jnp.int64 if jax.config.x64_enabled else jnp.int32), 'edge_features': jax.random.normal(ks[2], (N_EDGES, DE), jnp.float32), 'Wn': jax.random.normal(ks[3], (D, D), jnp.float32) * s, 'bn': jnp.zeros((D,), jnp.float32), 'We': jax.random.normal(ks[4], (D, DE), jnp.float32) * s, 'be': jnp.zeros((D,), jnp.float32), 'W1': jax.random.normal(ks[5], (L, D, 2 * D), jnp.float32) * s, 'b1': jnp.zeros((L, D), jnp.float32), 'ln_g': jnp.ones((L, D), jnp.float32), 'ln_b': jnp.zeros((L, D), jnp.float32), 'W2': jax.random.normal(ks[6], (L, D, D), jnp.float32) * s, 'b2': jnp.zeros((L, D), jnp.float32), 'Wqkv': jax.random.normal(ks[7], (3 * D, D), jnp.float32) * s, 'bqkv': jnp.zeros((3 * D,), jnp.float32), 'Wo': jax.random.normal(ks[8], (D, D), jnp.float32) * s, 'bo': jnp.zeros((D,), jnp.float32)}
        return inp
    _L0_gnn_all = _L0_gnn_setup()
    _L0_gnn_in = {k: v for k, v in _L0_gnn_all.items() if k in ('Wn', 'bn', 'We', 'be', 'W1', 'b1', 'ln_g', 'ln_b', 'W2', 'b2', 'Wqkv', 'bqkv', 'Wo', 'bo')}
    del _L0_gnn_all

    def _L1_gnn_setup():
        import jax, jax.numpy as jnp
        import numpy as np
        N = 625
        DEG = 16
        E = N * DEG
        H = 12
        DIN = 64
        DOUT = 64
        NEG_SLOPE = 0.2
        key = jax.random.key(seed)
        k_h, k_src, k_w, k_al, k_ar, k_wr = jax.random.split(key, 6)
        std = 1.414 * np.sqrt(2.0 / (DIN + DOUT))
        h = jax.random.normal(k_h, (N, H * DIN), dtype=jnp.float32)
        src = jax.random.randint(k_src, (E,), 0, N, dtype=jnp.int64)
        dst = jnp.repeat(jnp.arange(N, dtype=jnp.int64), DEG)
        W = jax.random.normal(k_w, (DOUT, DIN), dtype=jnp.float32) * std
        attn_l = jax.random.normal(k_al, (1, H, DOUT), dtype=jnp.float32) * std
        attn_r = jax.random.normal(k_ar, (1, H, DOUT), dtype=jnp.float32) * std
        W_res = jax.random.normal(k_wr, (DOUT, DIN), dtype=jnp.float32) * std
        return {'h': h, 'src': src, 'dst': dst, 'W': W, 'attn_l': attn_l, 'attn_r': attn_r, 'W_res': W_res}
    _L1_gnn_all = _L1_gnn_setup()
    _L1_gnn_in = {k: v for k, v in _L1_gnn_all.items() if k in ('W', 'attn_l', 'attn_r', 'W_res')}
    del _L1_gnn_all

    def _L2_gnn_setup():
        import jax, jax.numpy as jnp
        import numpy as np
        N_NODES = 10000
        N_EDGES = 3125
        DIM = 768
        NEG_SLOPE = 0.2

        def gat_conv(x, src, dst, W, att_src, att_dst, bias, num_nodes):
            h = x @ W
            a_s = h @ att_src
            a_d = h @ att_dst
            e = jax.nn.leaky_relu(a_s[src] + a_d[dst], NEG_SLOPE)
            m = jax.ops.segment_max(e, dst, num_segments=num_nodes)
            e = jnp.exp(e - m[dst])
            denom = jax.ops.segment_sum(e, dst, num_segments=num_nodes)
            alpha = e / denom[dst]
            msg = alpha[:, None] * h[src]
            out = jax.ops.segment_sum(msg, dst, num_segments=num_nodes)
            return out + bias
        key = jax.random.key(seed)
        ks = jax.random.split(key, 12)
        s = 1.0 / np.sqrt(DIM)
        inp = {'x': jax.random.normal(ks[0], (N_NODES, DIM), dtype=jnp.float32), 'edge_index': jax.random.randint(ks[1], (2, N_EDGES), 0, N_NODES, dtype=jnp.int64), 'W1': jax.random.normal(ks[2], (DIM, DIM), dtype=jnp.float32) * s, 'att_src1': jax.random.normal(ks[3], (DIM,), dtype=jnp.float32) * s, 'att_dst1': jax.random.normal(ks[4], (DIM,), dtype=jnp.float32) * s, 'b1': jnp.zeros((DIM,), dtype=jnp.float32), 'W2': jax.random.normal(ks[5], (DIM, DIM), dtype=jnp.float32) * s, 'att_src2': jax.random.normal(ks[6], (DIM,), dtype=jnp.float32) * s, 'att_dst2': jax.random.normal(ks[7], (DIM,), dtype=jnp.float32) * s, 'b2': jnp.zeros((DIM,), dtype=jnp.float32)}
        return inp
    _L2_gnn_all = _L2_gnn_setup()
    _L2_gnn_in = {k: v for k, v in _L2_gnn_all.items() if k in ('W1', 'att_src1', 'att_dst1', 'b1', 'W2', 'att_src2', 'att_dst2', 'b2')}
    del _L2_gnn_all

    def _L3_gnn_setup():
        import jax, jax.numpy as jnp
        import numpy as np
        N_NODES = 625
        N_EDGES = 5000
        IN_DIM = 768
        HID = 256
        HEADS = 4
        OUT_DIM = 768
        LN_EPS = 1e-05

        def _add_self_loops(edge_index, n):
            loop = jnp.arange(n, dtype=edge_index.dtype)
            return jnp.concatenate([edge_index, jnp.stack([loop, loop])], axis=1)

        def gat_conv(x, edge_index, W, a_src, a_dst, bias, heads, out_ch, concat):
            n = x.shape[0]
            ei = _add_self_loops(edge_index, n)
            src, dst = (ei[0], ei[1])
            xl = (x @ W).reshape(n, heads, out_ch)
            alpha_src = jnp.einsum('nhc,hc->nh', xl, a_src)
            alpha_dst = jnp.einsum('nhc,hc->nh', xl, a_dst)
            e = jax.nn.leaky_relu(alpha_src[src] + alpha_dst[dst], 0.2)
            m = jax.ops.segment_max(e, dst, num_segments=n)
            e = jnp.exp(e - m[dst])
            s = jax.ops.segment_sum(e, dst, num_segments=n)
            alpha = e / (s[dst] + 1e-16)
            msg = xl[src] * alpha[:, :, None]
            out = jax.ops.segment_sum(msg, dst, num_segments=n)
            out = out.reshape(n, heads * out_ch) if concat else out.mean(axis=1)
            return out + bias

        def layer_norm(x, g, b):
            mu = jnp.mean(x, axis=-1, keepdims=True)
            var = jnp.var(x, axis=-1, keepdims=True)
            return (x - mu) * jax.lax.rsqrt(var + LN_EPS) * g + b
        key = jax.random.key(seed)
        ks = jax.random.split(key, 16)
        s = 0.02
        HC = HID * HEADS
        return {'x': jax.random.normal(ks[0], (N_NODES, IN_DIM), jnp.float32), 'edge_index': jax.random.randint(ks[1], (2, N_EDGES), 0, N_NODES, jnp.int64 if jax.config.jax_enable_x64 else jnp.int32), 'W1': jax.random.normal(ks[2], (IN_DIM, HC), jnp.float32) * s, 'a_src1': jax.random.normal(ks[3], (HEADS, HID), jnp.float32) * s, 'a_dst1': jax.random.normal(ks[4], (HEADS, HID), jnp.float32) * s, 'b1': jnp.zeros((HC,), jnp.float32), 'g1': jnp.ones((HC,), jnp.float32), 'be1': jnp.zeros((HC,), jnp.float32), 'Wr1': jax.random.normal(ks[5], (IN_DIM, HC), jnp.float32) * s, 'br1': jnp.zeros((HC,), jnp.float32), 'W2': jax.random.normal(ks[6], (HC, OUT_DIM), jnp.float32) * s, 'a_src2': jax.random.normal(ks[7], (1, OUT_DIM), jnp.float32) * s, 'a_dst2': jax.random.normal(ks[8], (1, OUT_DIM), jnp.float32) * s, 'b2': jnp.zeros((OUT_DIM,), jnp.float32), 'g2': jnp.ones((OUT_DIM,), jnp.float32), 'be2': jnp.zeros((OUT_DIM,), jnp.float32), 'Wr2': jax.random.normal(ks[9], (HC, OUT_DIM), jnp.float32) * s, 'br2': jnp.zeros((OUT_DIM,), jnp.float32)}
    _L3_gnn_all = _L3_gnn_setup()
    _L3_gnn_in = {k: v for k, v in _L3_gnn_all.items() if k in ('W1', 'a_src1', 'a_dst1', 'b1', 'g1', 'be1', 'Wr1', 'br1', 'W2', 'a_src2', 'a_dst2', 'b2', 'g2', 'be2', 'Wr2', 'br2')}
    del _L3_gnn_all
    return {'x': x, 'src': src, 'dst': dst, 'edge_attr_256': edge_attr_256, 'L0_gnn_Wn': _L0_gnn_in['Wn'], 'L0_gnn_bn': _L0_gnn_in['bn'], 'L0_gnn_We': _L0_gnn_in['We'], 'L0_gnn_be': _L0_gnn_in['be'], 'L0_gnn_W1': _L0_gnn_in['W1'], 'L0_gnn_b1': _L0_gnn_in['b1'], 'L0_gnn_ln_g': _L0_gnn_in['ln_g'], 'L0_gnn_ln_b': _L0_gnn_in['ln_b'], 'L0_gnn_W2': _L0_gnn_in['W2'], 'L0_gnn_b2': _L0_gnn_in['b2'], 'L0_gnn_Wqkv': _L0_gnn_in['Wqkv'], 'L0_gnn_bqkv': _L0_gnn_in['bqkv'], 'L0_gnn_Wo': _L0_gnn_in['Wo'], 'L0_gnn_bo': _L0_gnn_in['bo'], 'L1_gnn_W': _L1_gnn_in['W'], 'L1_gnn_attn_l': _L1_gnn_in['attn_l'], 'L1_gnn_attn_r': _L1_gnn_in['attn_r'], 'L1_gnn_W_res': _L1_gnn_in['W_res'], 'L2_gnn_W1': _L2_gnn_in['W1'], 'L2_gnn_att_src1': _L2_gnn_in['att_src1'], 'L2_gnn_att_dst1': _L2_gnn_in['att_dst1'], 'L2_gnn_b1': _L2_gnn_in['b1'], 'L2_gnn_W2': _L2_gnn_in['W2'], 'L2_gnn_att_src2': _L2_gnn_in['att_src2'], 'L2_gnn_att_dst2': _L2_gnn_in['att_dst2'], 'L2_gnn_b2': _L2_gnn_in['b2'], 'L3_gnn_W1': _L3_gnn_in['W1'], 'L3_gnn_a_src1': _L3_gnn_in['a_src1'], 'L3_gnn_a_dst1': _L3_gnn_in['a_dst1'], 'L3_gnn_b1': _L3_gnn_in['b1'], 'L3_gnn_g1': _L3_gnn_in['g1'], 'L3_gnn_be1': _L3_gnn_in['be1'], 'L3_gnn_Wr1': _L3_gnn_in['Wr1'], 'L3_gnn_br1': _L3_gnn_in['br1'], 'L3_gnn_W2': _L3_gnn_in['W2'], 'L3_gnn_a_src2': _L3_gnn_in['a_src2'], 'L3_gnn_a_dst2': _L3_gnn_in['a_dst2'], 'L3_gnn_b2': _L3_gnn_in['b2'], 'L3_gnn_g2': _L3_gnn_in['g2'], 'L3_gnn_be2': _L3_gnn_in['be2'], 'L3_gnn_Wr2': _L3_gnn_in['Wr2'], 'L3_gnn_br2': _L3_gnn_in['br2']}

def reference(x, src, dst, edge_attr_256, L0_gnn_Wn, L0_gnn_bn, L0_gnn_We, L0_gnn_be, L0_gnn_W1, L0_gnn_b1, L0_gnn_ln_g, L0_gnn_ln_b, L0_gnn_W2, L0_gnn_b2, L0_gnn_Wqkv, L0_gnn_bqkv, L0_gnn_Wo, L0_gnn_bo, L1_gnn_W, L1_gnn_attn_l, L1_gnn_attn_r, L1_gnn_W_res, L2_gnn_W1, L2_gnn_att_src1, L2_gnn_att_dst1, L2_gnn_b1, L2_gnn_W2, L2_gnn_att_src2, L2_gnn_att_dst2, L2_gnn_b2, L3_gnn_W1, L3_gnn_a_src1, L3_gnn_a_dst1, L3_gnn_b1, L3_gnn_g1, L3_gnn_be1, L3_gnn_Wr1, L3_gnn_br1, L3_gnn_W2, L3_gnn_a_src2, L3_gnn_a_dst2, L3_gnn_b2, L3_gnn_g2, L3_gnn_be2, L3_gnn_Wr2, L3_gnn_br2):
    import jax
    import jax.numpy as jnp

    def _L0_gnn_ref(node_features, edge_index, edge_features, Wn, bn, We, be, W1, b1, ln_g, ln_b, W2, b2, Wqkv, bqkv, Wo, bo):
        import jax, jax.numpy as jnp
        import numpy as np
        N_NODES = 128
        N_EDGES = 4096
        D = 768
        DE = 256
        L = 3
        H = 8
        DH = D // H
        EPS = 1e-05

        def _layernorm(x, g, b):
            mu = jnp.mean(x, axis=-1, keepdims=True)
            var = jnp.var(x, axis=-1, keepdims=True)
            return (x - mu) * jax.lax.rsqrt(var + EPS) * g + b
        n = node_features.shape[0]
        nodes = node_features @ Wn.T + bn
        edge_proj = edge_features @ We.T + be
        src, dst = (edge_index[0], edge_index[1])
        for l in range(L):
            msgs = nodes[src] + nodes[dst] + edge_proj
            agg = jax.ops.segment_sum(msgs, dst, num_segments=n)
            combined = jnp.concatenate([nodes, agg], axis=-1)
            h = combined @ W1[l].T + b1[l]
            h = _layernorm(h, ln_g[l], ln_b[l])
            h = jax.nn.relu(h)
            h = h @ W2[l].T + b2[l]
            nodes = h + nodes
        qkv = nodes @ Wqkv.T + bqkv
        q, k, v = jnp.split(qkv, 3, axis=-1)
        q = q.reshape(n, H, DH) * DH ** (-0.5)
        k = k.reshape(n, H, DH)
        v = v.reshape(n, H, DH)
        scores = jnp.einsum('nhd,mhd->hnm', q, k)
        probs = jax.nn.softmax(scores, axis=-1)
        attn = jnp.einsum('hnm,mhd->nhd', probs, v).reshape(n, D)
        attended = attn @ Wo.T + bo
        return nodes + attended

    def _L1_gnn_ref(h, src, dst, W, attn_l, attn_r, W_res):
        import jax, jax.numpy as jnp
        import numpy as np
        N = 625
        DEG = 16
        E = N * DEG
        H = 12
        DIN = 64
        DOUT = 64
        NEG_SLOPE = 0.2
        n = h.shape[0]
        hv = h.reshape(n, H, DIN)
        ft = jnp.einsum('nhd,od->nho', hv, W)
        a1 = jnp.sum(ft * attn_l, axis=-1)
        a2 = jnp.sum(ft * attn_r, axis=-1)
        e = jax.nn.leaky_relu(a1[src] + a2[dst], negative_slope=NEG_SLOPE)
        m = jax.ops.segment_max(e, dst, num_segments=n)
        m = jnp.where(jnp.isfinite(m), m, 0.0)
        w = jnp.exp(e - m[dst])
        denom = jax.ops.segment_sum(w, dst, num_segments=n)
        alpha = w / jnp.maximum(denom[dst], 1e-16)
        msg = alpha[:, :, None] * ft[src]
        agg = jax.ops.segment_sum(msg, dst, num_segments=n)
        res = jnp.einsum('nhd,od->nho', hv, W_res)
        out = jax.nn.relu((agg + res).reshape(n, H * DOUT))
        return out

    def _L2_gnn_ref(x, edge_index, W1, att_src1, att_dst1, b1, W2, att_src2, att_dst2, b2):
        import jax, jax.numpy as jnp
        import numpy as np
        N_NODES = 10000
        N_EDGES = 3125
        DIM = 768
        NEG_SLOPE = 0.2

        def gat_conv(x, src, dst, W, att_src, att_dst, bias, num_nodes):
            h = x @ W
            a_s = h @ att_src
            a_d = h @ att_dst
            e = jax.nn.leaky_relu(a_s[src] + a_d[dst], NEG_SLOPE)
            m = jax.ops.segment_max(e, dst, num_segments=num_nodes)
            e = jnp.exp(e - m[dst])
            denom = jax.ops.segment_sum(e, dst, num_segments=num_nodes)
            alpha = e / denom[dst]
            msg = alpha[:, None] * h[src]
            out = jax.ops.segment_sum(msg, dst, num_segments=num_nodes)
            return out + bias
        n = x.shape[0]
        loops = jnp.arange(n, dtype=edge_index.dtype)
        src = jnp.concatenate([edge_index[0], loops])
        dst = jnp.concatenate([edge_index[1], loops])
        h = gat_conv(x, src, dst, W1, att_src1, att_dst1, b1, n)
        h = jax.nn.relu(h)
        out = gat_conv(h, src, dst, W2, att_src2, att_dst2, b2, n)
        return out

    def _L3_gnn_ref(x, edge_index, W1, a_src1, a_dst1, b1, g1, be1, Wr1, br1, W2, a_src2, a_dst2, b2, g2, be2, Wr2, br2):
        import jax, jax.numpy as jnp
        import numpy as np
        N_NODES = 625
        N_EDGES = 5000
        IN_DIM = 768
        HID = 256
        HEADS = 4
        OUT_DIM = 768
        LN_EPS = 1e-05

        def _add_self_loops(edge_index, n):
            loop = jnp.arange(n, dtype=edge_index.dtype)
            return jnp.concatenate([edge_index, jnp.stack([loop, loop])], axis=1)

        def gat_conv(x, edge_index, W, a_src, a_dst, bias, heads, out_ch, concat):
            n = x.shape[0]
            ei = _add_self_loops(edge_index, n)
            src, dst = (ei[0], ei[1])
            xl = (x @ W).reshape(n, heads, out_ch)
            alpha_src = jnp.einsum('nhc,hc->nh', xl, a_src)
            alpha_dst = jnp.einsum('nhc,hc->nh', xl, a_dst)
            e = jax.nn.leaky_relu(alpha_src[src] + alpha_dst[dst], 0.2)
            m = jax.ops.segment_max(e, dst, num_segments=n)
            e = jnp.exp(e - m[dst])
            s = jax.ops.segment_sum(e, dst, num_segments=n)
            alpha = e / (s[dst] + 1e-16)
            msg = xl[src] * alpha[:, :, None]
            out = jax.ops.segment_sum(msg, dst, num_segments=n)
            out = out.reshape(n, heads * out_ch) if concat else out.mean(axis=1)
            return out + bias

        def layer_norm(x, g, b):
            mu = jnp.mean(x, axis=-1, keepdims=True)
            var = jnp.var(x, axis=-1, keepdims=True)
            return (x - mu) * jax.lax.rsqrt(var + LN_EPS) * g + b
        h0 = x
        h = gat_conv(x, edge_index, W1, a_src1, a_dst1, b1, HEADS, HID, True)
        h = layer_norm(h, g1, be1)
        h = jax.nn.relu(h)
        h = h + (h0 @ Wr1 + br1)
        h1 = h
        h = gat_conv(h, edge_index, W2, a_src2, a_dst2, b2, 1, OUT_DIM, False)
        h = layer_norm(h, g2, be2)
        h = h + (h1 @ Wr2 + br2)
        return h
    edge_index = jnp.stack([src, dst])
    x = _layernorm(x + _L0_gnn_ref(x, edge_index, edge_attr_256, L0_gnn_Wn, L0_gnn_bn, L0_gnn_We, L0_gnn_be, L0_gnn_W1, L0_gnn_b1, L0_gnn_ln_g, L0_gnn_ln_b, L0_gnn_W2, L0_gnn_b2, L0_gnn_Wqkv, L0_gnn_bqkv, L0_gnn_Wo, L0_gnn_bo), axis=-1)
    x = _layernorm(x + _L1_gnn_ref(x, src, dst, L1_gnn_W, L1_gnn_attn_l, L1_gnn_attn_r, L1_gnn_W_res), axis=-1)
    x = _layernorm(x + _L2_gnn_ref(x, edge_index, L2_gnn_W1, L2_gnn_att_src1, L2_gnn_att_dst1, L2_gnn_b1, L2_gnn_W2, L2_gnn_att_src2, L2_gnn_att_dst2, L2_gnn_b2), axis=-1)
    x = _layernorm(x + _L3_gnn_ref(x, edge_index, L3_gnn_W1, L3_gnn_a_src1, L3_gnn_a_dst1, L3_gnn_b1, L3_gnn_g1, L3_gnn_be1, L3_gnn_Wr1, L3_gnn_br1, L3_gnn_W2, L3_gnn_a_src2, L3_gnn_a_dst2, L3_gnn_b2, L3_gnn_g2, L3_gnn_be2, L3_gnn_Wr2, L3_gnn_br2), axis=-1)
    return x

_drawn_inputs = setup_inputs


def setup_inputs(seed=0):
    import zlib

    import numpy as np

    out = dict(_drawn_inputs(seed))
    spreads = {'L0_gnn_bn': (0.0, 0.1),
     'L0_gnn_be': (0.0, 0.1),
     'L0_gnn_b1': (0.0, 0.65),
     'L0_gnn_ln_g': (1.0, 0.2),
     'L0_gnn_ln_b': (0.0, 0.1),
     'L0_gnn_b2': (0.0, 0.1),
     'L0_gnn_bqkv': (0.0, 0.1),
     'L0_gnn_bo': (0.0, 0.1),
     'L2_gnn_b1': (0.0, 0.1),
     'L2_gnn_b2': (0.0, 0.1),
     'L3_gnn_b1': (0.0, 0.1),
     'L3_gnn_g1': (1.0, 0.2),
     'L3_gnn_be1': (0.0, 0.1),
     'L3_gnn_br1': (0.0, 0.1),
     'L3_gnn_b2': (0.0, 0.1),
     'L3_gnn_g2': (1.0, 0.2),
     'L3_gnn_be2': (0.0, 0.1),
     'L3_gnn_br2': (0.0, 0.1)}
    factors = {'L2_gnn_att_dst1': 3.257,
     'L2_gnn_att_src2': 8.0,
     'L2_gnn_att_dst2': 31.173,
     'L3_gnn_a_src1': 3.852,
     'L3_gnn_a_dst1': 8.0,
     'L3_gnn_a_src2': 3.466,
     'L3_gnn_a_dst2': 8.0}
    for name, (base, spread) in spreads.items():
        noise = np.random.default_rng([zlib.crc32(name.encode()), seed]).standard_normal(out[name].shape)
        drawn = base * np.exp(spread * noise) if base else spread * noise
        out[name] = jnp.asarray(drawn.astype(out[name].dtype))
    for name, factor in factors.items():
        out[name] = (out[name] * factor).astype(out[name].dtype)
    return out
```

```python
import concourse.bass as bass
from concourse import mybir
from contextlib import ExitStack

F32 = mybir.dt.float32
BF16 = mybir.dt.bfloat16
I32 = mybir.dt.int32
ALU = mybir.AluOpType
ACT = mybir.ActivationFunctionType
AX = mybir.AxisListType

P = 128
D = 768
DE = 256
E = 2176
EC = E // P
KC = D // P
HALF = D // 2
HC = 3
LAYERS = 3
H0, DH = 8, 96
H1, O1 = 12, 64
H3, O3 = 4, 256
D3 = H3 * O3
K3 = D3 // P
SLOPE = 0.2
EPS = 1e-5
MASKED = -1e30

UNIT = 1536
REGION = 9
RING = 2 * REGION
U_WN, U_WE, U_LAYER, U_Q, U_K, U_V, U_WO, U_C1, U_C2 = 0, 3, 9, 36, 39, 42, 45, 48, 51
U_G1, U_R1, U_G2, U_R2, U_END = 54, 58, 62, 66, 70
PRELUDE = 4


def unit_index(u):
    return u if u < PRELUDE else u - (REGION - PRELUDE)


ROWS = [
    [("bn", D)] + [("b1", LAYERS * D), ("b2", LAYERS * D)] + [("bo", D), ("c2b", D)],
    [("bqkv", 3 * D), ("g1b", D3), ("r1b", D3), ("g2b", D), ("r2b", D), ("ln2b", D)],
]
ROW_BASE = [0, 32]
ROW_LEN = [sum(n for _, n in g) for g in ROWS]
ROW_COLS = [n // P for n in ROW_LEN]
ROW_AT = {}
for _g, _rows in enumerate(ROWS):
    _at = 0
    for _name, _n in _rows:
        ROW_AT[_name] = (_g, _at)
        _at += _n

COL_BE, COL_C1B, COL_G1G, COL_G1B, COL_LNG = 0, KC, 2 * KC, 2 * KC + K3, 2 * KC + 2 * K3
COL_LNB = COL_LNG + LAYERS * KC
COLS = COL_LNB + LAYERS * KC

ATT2 = 4 * D
ATT3 = 2 * D3 + 2 * D + D


def gnn_kernel(nc, x_in, src_in, dst_in, edge_in, stream_in, cols_in, rows_in, blk_in, blka_in, att_in, out):
    ctx = ExitStack()
    with ctx:
        def sb(name, shape, dt=F32):
            return ctx.enter_context(nc.sbuf_tensor(name, shape, dt))

        sems = {}

        def sem(name):
            if name not in sems:
                sems[name] = ctx.enter_context(nc.semaphore(name))
            return sems[name]

        ring = sb("ring", [P, RING * UNIT])
        row3 = sb("row3", [P, max(ROW_LEN)], BF16)
        ones3 = sb("ones3", [P, P], BF16)
        parts = sb("parts", [P, 3, sum(ROW_COLS)], BF16)
        cols = sb("cols", [P, COLS])
        lncol = sb("lncol", [P, 2 * KC])
        ident = sb("ident", [P, P])
        identb = sb("identb", [P, P], BF16)
        onesf = sb("onesf", [P, P])
        edge_idx = sb("edge_idx", [P, 2 * EC], I32)
        edge_f = sb("edge_f", [P, 2 * EC])
        iota_i = sb("iota_i", [P, 2 * P], I32)
        cnt = sb("cnt", [P, P])
        cnt_self = sb("cnt_self", [P, P])
        cntT = sb("cntT", [P, P])
        mixT = sb("mixT", [P, P])
        mask1 = sb("mask1", [P, 4, P], BF16)
        mask2 = sb("mask2", [P, 4, P], BF16)
        deg = sb("deg", [P, 1])
        degB = sb("degB", [P, P])
        edge_sum = sb("edge_sum", [P, DE])
        edge_sumT = sb("edge_sumT", [P, 2, P])
        x = sb("x", [P, D])
        nodes = sb("nodes", [P, D])
        actT = sb("actT", [P, KC, P])
        hidT = sb("hidT", [P, K3, P])
        norm = sb("norm", [P, D3])
        h_nat = sb("h_nat", [P, D3])
        pair = sb("pair", [P, 2, D3])
        aggT = pair[:, 0, 0:D].rearrange("p (k n) -> p k n", k=KC)
        edge_term = pair[:, 1, 0:D].rearrange("p (k n) -> p k n", k=KC)
        resid = pair[:, 0, :]
        residT = pair[:, 1, :].rearrange("p (k n) -> p k n", k=K3)
        stats = sb("stats", [P, 12])
        mv = sb("mv", [P, 2])
        veps = sb("veps", [P, 1])
        mhalf = sb("mhalf", [P, 1])
        rstd = sb("rstd", [P, 1])
        small = sb("small", [P, 64])
        e4 = sb("e4", [P, 4, P])
        diag4 = sb("diag4", [P, 4, P])
        alphaT4 = sb("alphaT4", [P, 4, P])
        bd = sb("bd", [P, 2 * P])
        blk = sb("blk", [P, 2 * O1])
        blka = sb("blka", [O1, 2 * O1 + 2 * H1])
        wlr = sb("wlr", [P, 2 * H1])

        RG = 2 * H1 * P + 4 * D + 4 * H0 * P - D
        region = sb("region", [P, RG])

        def part(at, n):
            return region[:, at:at + n]
        dst_hot = part(0, EC * P).rearrange("p (k n) -> p k n", k=EC)
        src_edge = part(EC * P, EC * (P + DE)).rearrange("p (k n) -> p k n", k=EC)
        TAIL = EC * (2 * P + DE)
        rows_f, rows_r = part(TAIL, sum(ROW_COLS)), part(TAIL + sum(ROW_COLS), sum(ROW_COLS))
        colf, maskf = part(TAIL + 2 * sum(ROW_COLS), P), part(TAIL + 2 * sum(ROW_COLS) + P, 2 * P)
        assert TAIL + 2 * sum(ROW_COLS) + 3 * P <= RG
        junk = nodes[:, 0:HALF]
        w_l = part(0, H1 * P).rearrange("p (h n) -> p h n", h=H1)
        w_r = part(H1 * P, H1 * P).rearrange("p (h n) -> p h n", h=H1)
        A0 = 2 * H1 * P
        q_nat, k_nat, v_nat = (part(A0 + i * D, D) for i in range(3))
        qT, kT, prob, probT = (part(A0 + 3 * D + i * H0 * P, H0 * P).rearrange("p (h n) -> p h n", h=H0)
                               for i in range(4))
        e12 = part(A0, H1 * P).rearrange("p (h n) -> p h n", h=H1)
        alphaT12 = part(A0 + H1 * P, H1 * P).rearrange("p (h n) -> p h n", h=H1)
        att2 = part(A0 + 2 * H1 * P, ATT2)
        att3 = part(0, ATT3)
        assert ATT3 <= A0 + 2 * H1 * P and A0 + 2 * H1 * P + ATT2 <= RG and EC * (2 * P + DE) <= RG

        bank = [ctx.enter_context(nc.psum_tensor(f"bank{i}", [P, 512], F32)) for i in range(8)]
        A, T, G = bank[0:4], bank[4:6], bank[6:8]

        scratch = nc.dram_tensor("row_parts", [3, sum(ROW_LEN)], BF16).ap()
        block = ctx.enter_context(nc.Block())

        @block.sync
        def _(sp):
            sp.dma_start(x[:, :], x_in).then_inc(sem("x_in"), 16)
            sp.dma_start(edge_idx[:, 0:EC], src_in).then_inc(sem("src_in"), 16)
            sp.dma_start(edge_idx[:, EC:2 * EC], dst_in).then_inc(sem("dst_in"), 16)
            sp.dma_start(rows_f[:, :], rows_in).then_inc(sem("rows_in"), 16)
            sp.dma_start(cols[:, :], cols_in).then_inc(sem("cols_in"), 16)

            def load(row, region_at, j):
                sp.dma_start(ring[:, bass.ds(region_at + j * UNIT, UNIT)],
                             stream_in[bass.ds(row, 1), :, :].rearrange("o p n -> (o p) n")
                             ).then_inc(sem(f"weights{j}_in"), 16)

            for j in range(PRELUDE):
                load(j, 0, j)
                if j == 1:
                    sp.dma_start(src_edge[:, :, P:P + DE], edge_in).then_inc(sem("edge_in"), 16)
            for j in range(REGION):
                if j < PRELUDE:
                    sp.wait_ge(sem(f"weights{j}_in"), 16)
                load(PRELUDE + j, REGION * UNIT, j)
            sp.dma_start(blk[:, :], blk_in).then_inc(sem("blk_in"), 16)
            sp.dma_start(blka[:, :], blka_in).then_inc(sem("blka_in"), 16)
            sp.wait_ge(sem("row_parts"), 1)
            at = col = 0
            for g in range(2):
                for j in range(3):
                    sp.dma_start(scratch[j, at:at + ROW_LEN[g]].rearrange("(p c) -> p c", c=ROW_COLS[g]),
                                 parts[:, j, col:col + ROW_COLS[g]]).then_inc(sem("row_scratch"), 16)
                at += ROW_LEN[g]
                col += ROW_COLS[g]
            sp.wait_ge(sem("row_scratch"), 96)
            for g in range(2):
                sp.dma_start(row3[ROW_BASE[g]:ROW_BASE[g] + 3, 0:ROW_LEN[g]],
                             scratch[:, g * ROW_LEN[0]:g * ROW_LEN[0] + ROW_LEN[g]]).then_inc(sem("rows_ready"), 16)
            for j in range(REGION):
                if j == 0:
                    sp.wait_ge(sem("node_proj"), 1)
                elif j < 3:
                    sp.wait_ge(sem("node_proj"), 2)
                elif j == 3:
                    sp.wait_ge(sem("edge_proj"), 1)
                sp.wait_ge(sem(f"weights{j}_in"), 32 if j < PRELUDE else 16)
                load(PRELUDE + REGION + j, 0, j)
            with sp.Fori(0, LAYERS) as l:
                for j in range(REGION):
                    if j < 6:
                        sp.wait_ge(sem("hidden_proj"), 2 * l + 1 + j // 3)
                        sp.nop(nofuse=True)
                    else:
                        sp.wait_ge(sem("update_proj"), 2 * l + 1 + (1 if j > 6 else 0))
                        sp.nop(nofuse=True)
                    sp.wait_ge(sem(f"weights{j}_in"), 16 * l + (48 if j < PRELUDE else 32))
                    sp.nop(nofuse=True)
                    load(l * REGION + (PRELUDE + 2 * REGION + j), ((l + 1) % 2) * (REGION * UNIT), j)
            sp.wait_ge(sem("attended"), 2)
            for i in range(4):
                sp.dma_start(att2[:, i * D:(i + 1) * D], att_in[:, i * D:(i + 1) * D].partition_broadcast(P)
                             ).then_inc(sem("att2_in"), 16)
            for u in range(U_G1, U_END):
                j = u % REGION
                if u < U_G1 + REGION:
                    sp.wait_ge(sem(["q_proj", "k_proj", "v_proj"][j // 3]), 1 if j % 3 == 0 else 2)
                elif j < 3:
                    sp.wait_ge(sem("out_proj"), 1 if j % 3 == 0 else 2)
                elif j < 6:
                    sp.wait_ge(sem("c1_proj"), 1 if j % 3 == 0 else 2)
                else:
                    sp.wait_ge(sem("c2_proj"), 1)
                sp.wait_ge(sem(f"weights{j}_in"), 16 * (u // REGION - (0 if j < PRELUDE else 1)))
                load(unit_index(u), (u // REGION % 2) * REGION * UNIT, j)
                if j == 6 and u < U_G1 + REGION:
                    sp.wait_ge(sem("b1_agg"), 2)
                    for i in range(0, ATT3, D):
                        n = min(D, ATT3 - i)
                        sp.dma_start(att3[:, i:i + n], att_in[:, ATT2 + i:ATT2 + i + n].partition_broadcast(P)
                                     ).then_inc(sem("att3_in"), 16)
            for i in range(2):
                sp.wait_ge(sem("out_ready"), i + 1)
                sp.dma_start(out[:, i * HALF:(i + 1) * HALF], norm[:, i * HALF:(i + 1) * HALF]
                             ).then_inc(sem("out_stored"), 16)
            sp.wait_ge(sem("out_stored"), 32)

        @block.gpsimd
        def _(pool):
            pool.iota(iota_i[:, 0:P], [[1, P]], base=0, channel_multiplier=-1).then_inc(sem("iotas"), 1)
            pool.iota(iota_i[:, P:2 * P], [[1, P]], base=0, channel_multiplier=0).then_inc(sem("iotas"), 1)
            pool.memset(onesf[:, :], 1.0).then_inc(sem("constants"), 1)
            pool.memset(ones3[:, :], 1.0).then_inc(sem("constants"), 1)
            pool.memset(mhalf[:, :], -0.5).then_inc(sem("mhalf"), 1)
            pool.memset(bd[:, :], 0.0).then_inc(sem("bd_zero"), 1)
            pool.wait_ge(sem("mhalf"), 1)
            pool.wait_ge(sem("edge_sums"), 1)
            pool.memset(w_l, 0.0).then_inc(sem("w_zero"), 1)
            pool.memset(w_r, 0.0).then_inc(sem("w_zero"), 1)
            with pool.Fori(0, LAYERS + 6) as n:
                pool.wait_ge(sem("ln_var"), n + 1)
                pool.tensor_tensor(rstd[:, :], veps[:, :], mhalf[:, :], ALU.pow).then_inc(sem("ln_rstd"), 1)

        @block.tensor
        def _(pe):
            def arrived(u, j):
                pe.wait_ge(sem(f"weights{j}_in"), 16 * (u // REGION + (1 if j < PRELUDE else 0)))

            def add_row(dst, name, at, n, start=False, stop=True):
                g, off = ROW_AT[name]
                b = ROW_BASE[g]
                return pe.matmul(dst[:, 0:n], ones3[b:b + 3, :], row3[b:b + 3, bass.ds(at + off, n)],
                                 start=start, stop=stop)

            def project(u0, banks, lhsT, chunks, done, row=None, at=0, more=None, w=HALF):
                for half in range(2):
                    for k in range(chunks):
                        b = (half * chunks + k) * w
                        u = u0 + b // UNIT
                        if b % UNIT == 0 or k == 0:
                            arrived(u, u % REGION)
                        o = (u % RING) * UNIT + b % UNIT
                        mm = pe.matmul(banks[half][:, 0:w], lhsT[:, k, :], ring[:, o:o + w],
                                       start=(k == 0), stop=(k == chunks - 1 and row is None))
                    if row is not None:
                        mm = add_row(banks[half], row, at + half * w, w)
                    mm.then_inc(sem(done), 1)
                    if more is not None:
                        more(half)

            def transposes(src, banks, done, per=HC, n=KC):
                for c in range(n):
                    mm = pe.transpose(banks[c // per][:, (c % per) * P:(c % per + 1) * P],
                                      src[:, c * P:(c + 1) * P], ident[:, :])
                    if c % per == per - 1:
                        mm.then_inc(sem(done), 1)

            pe.wait_ge(sem("x_in"), 16)
            pe.wait_ge(sem("ident"), 1)
            transposes(x, T, "actT_psum")
            pe.wait_ge(sem("actT"), 2)
            pe.wait_ge(sem("constants"), 2)
            for half in range(2):
                for k in range(KC):
                    b = (half * KC + k) * HALF
                    if b % UNIT == 0:
                        arrived(b // UNIT, b // UNIT)
                    pe.matmul(A[half][:, 0:HALF], actT[:, k, :], ring[:, b:b + HALF], start=(k == 0), stop=False)
                if half == 0:
                    pe.wait_ge(sem("rows_ready"), 32)
                add_row(A[half], "bn", half * HALF, HALF).then_inc(sem("node_proj"), 1)
            pe.wait_ge(sem("one_hots"), 2)
            pe.wait_ge(sem("edge_in"), 16)
            for k in range(EC):
                mm = pe.matmul(G[0][:, 0:P + DE], dst_hot[:, k, :], src_edge[:, k, :],
                               start=(k == 0), stop=(k == EC - 1))
            mm.then_inc(sem("edge_sums"), 1)
            pe.wait_ge(sem("cnt"), 1)
            pe.wait_ge(sem("edge_sum"), 1)
            pe.transpose(T[0][:, 0:P], cnt[:, :], ident[:, :])
            pe.transpose(T[0][:, P:2 * P], edge_sum[:, 0:P], ident[:, :])
            pe.transpose(T[0][:, 2 * P:3 * P], edge_sum[:, P:2 * P], ident[:, :]).then_inc(sem("graph_T"), 1)
            pe.wait_ge(sem("cntT"), 1)
            pe.matmul(T[1][:, 0:P], onesf[:, :], cntT[:, :], start=True, stop=True).then_inc(sem("deg_rows"), 1)
            pe.wait_ge(sem("edge_sumT"), 1)
            arrived(U_WE, U_WE)
            for c in range(KC):
                for k in range(2):
                    o = U_WE * UNIT + k * D + c * P
                    mm = pe.matmul(G[c // HC][:, (c % HC) * P:(c % HC + 1) * P], ring[:, o:o + P],
                                   edge_sumT[:, k, :], start=(k == 0), stop=(k == 1))
            mm.then_inc(sem("edge_proj"), 1)
            pe.wait_ge(sem("blka_in"), 16)
            pe.matmul(A[2][:, 0:2 * H1], blka[:, 0:P], blka[:, P:P + 2 * H1], start=True, stop=True
                      ).then_inc(sem("wlr_psum"), 1)

            pe.wait_ge(sem("mixT"), 1)
            pe.wait_ge(sem("edge_term"), 1)
            pe.wait_ge(sem("wlr"), 1)
            with pe.Fori(0, LAYERS) as l:
                base = ((l + 1) % 2) * (REGION * UNIT)

                def layer_unit(j):
                    pe.wait_ge(sem(f"weights{j}_in"), 16 * l + (32 if j < PRELUDE else 16))

                for half in range(2):
                    pe.wait_ge(sem("nodes"), 2 * l + half + 1)
                    for c in range(HC):
                        cc = half * HC + c
                        mm = pe.transpose(T[half][:, c * P:(c + 1) * P], nodes[:, cc * P:(cc + 1) * P], ident[:, :])
                    mm.then_inc(sem("actT_psum"), 1)
                    for c in range(HC):
                        cc = half * HC + c
                        mm = pe.matmul(G[half][:, c * P:(c + 1) * P], nodes[:, cc * P:(cc + 1) * P], mixT[:, :],
                                       start=True, stop=True)
                    mm.then_inc(sem("agg_psum"), 1)
                for half in range(2):
                    for k in range(2 * KC):
                        if k == 0 or k == HC:
                            pe.wait_ge(sem("actT"), 2 * l + 3 + k // HC)
                        if k == KC or k == KC + HC:
                            pe.wait_ge(sem("aggT"), 2 * l + 1 + (k - KC) // HC)
                        b = (half * 2 * KC + k) * HALF
                        if b % UNIT == 0:
                            layer_unit(b // UNIT)
                        lhsT = actT[:, k, :] if k < KC else aggT[:, k - KC, :]
                        pe.matmul(A[half][:, 0:HALF], lhsT, ring[:, bass.ds(base + b, HALF)],
                                  start=(k == 0), stop=False)
                    add_row(A[half], "b1", l * D + half * HALF, HALF).then_inc(sem("hidden_proj"), 1)
                for half in range(2):
                    pe.wait_ge(sem("hidden_norm"), 2 * l + half + 1)
                    for c in range(HC):
                        cc = half * HC + c
                        mm = pe.transpose(T[half][:, c * P:(c + 1) * P], norm[:, cc * P:(cc + 1) * P], ident[:, :])
                    mm.then_inc(sem("hidT_psum"), 1)
                for half in range(2):
                    for k in range(KC):
                        if half == 0 and k == 0:
                            pe.wait_ge(sem("hidT_a"), l + 1)
                        if half == 0 and k == HC:
                            pe.wait_ge(sem("hidT_b"), l + 1)
                        b = 6 * UNIT + (half * KC + k) * HALF
                        if b % UNIT == 0:
                            layer_unit(b // UNIT)
                        pe.matmul(A[2 + half][:, 0:HALF], hidT[:, k, :], ring[:, bass.ds(base + b, HALF)],
                                  start=(k == 0), stop=False)
                    add_row(A[2 + half], "b2", l * D + half * HALF, HALF).then_inc(sem("update_proj"), 1)

            for half in range(2):
                pe.wait_ge(sem("nodes"), 2 * LAYERS + half + 1)
                for c in range(HC):
                    cc = half * HC + c
                    mm = pe.transpose(T[half][:, c * P:(c + 1) * P], nodes[:, cc * P:(cc + 1) * P], ident[:, :])
                mm.then_inc(sem("actT_psum"), 1)
            pe.wait_ge(sem("actT"), 2 * LAYERS + 4)
            project(U_Q, A[0:2], actT, KC, "q_proj", "bqkv", 0)
            project(U_K, A[2:4], actT, KC, "k_proj", "bqkv", D)

            def head_transposes(src, banks, done):
                for h in range(H0):
                    mm = pe.transpose(banks[h // 4][0:DH, (h % 4) * P:(h % 4 + 1) * P],
                                      src[:, h * DH:(h + 1) * DH], ident[:, :])
                    if h % 4 == 3:
                        mm.then_inc(sem(done), 1)

            def between(half):
                if half == 0:
                    pe.wait_ge(sem("q_nat"), 2)
                    head_transposes(q_nat, T, "qT_psum")
                    pe.wait_ge(sem("k_nat"), 2)
                    head_transposes(k_nat, A[0:2], "kT_psum")
            project(U_V, G, actT, KC, "v_proj", "bqkv", 2 * D, more=between)
            for b in range(2):
                pe.wait_ge(sem("qT"), b + 1)
                pe.wait_ge(sem("kT"), b + 1)
                for h in range(4 * b, 4 * b + 4):
                    mm = pe.matmul(A[2 + b][:, (h % 4) * P:(h % 4 + 1) * P], qT[0:DH, h, :], kT[0:DH, h, :],
                                   start=True, stop=True)
                mm.then_inc(sem("scores"), 1)
            for b in range(2):
                pe.wait_ge(sem("prob"), b + 1)
                for h in range(4 * b, 4 * b + 4):
                    mm = pe.transpose(T[b][:, (h % 4) * P:(h % 4 + 1) * P], prob[:, h, :], ident[:, :])
                mm.then_inc(sem("probT_psum"), 1)
            pe.wait_ge(sem("v_nat"), 2)
            for b in range(2):
                pe.wait_ge(sem("probT"), b + 1)
                for h in range(4 * b, 4 * b + 4):
                    mm = pe.matmul(A[b][:, (h % 4) * DH:(h % 4 + 1) * DH], probT[:, h, :],
                                   v_nat[:, h * DH:(h + 1) * DH], start=True, stop=True)
                mm.then_inc(sem("attn_psum"), 1)
            for half in range(2):
                pe.wait_ge(sem("attended"), half + 1)
                for c in range(HC):
                    cc = half * HC + c
                    mm = pe.transpose(G[half][:, c * P:(c + 1) * P], norm[:, cc * P:(cc + 1) * P], ident[:, :])
                mm.then_inc(sem("attnT_psum"), 1)
            pe.wait_ge(sem("attnT"), 2)
            project(U_WO, A[2:4], hidT, KC, "out_proj", "bo", 0)

            def x_transposes(n):
                for half in range(2):
                    pe.wait_ge(sem("x_ready"), 2 * n + half + 1)
                    for c in range(HC):
                        cc = half * HC + c
                        mm = pe.transpose(T[half][:, c * P:(c + 1) * P], x[:, cc * P:(cc + 1) * P], ident[:, :])
                    mm.then_inc(sem("actT_psum"), 1)
                pe.wait_ge(sem("actT"), 2 * LAYERS + 4 + 2 * (n + 1))

            x_transposes(0)
            pe.wait_ge(sem("bd"), 4)
            pe.wait_ge(sem("masks"), 2)
            pe.wait_ge(sem("w_lr"), 4)
            EB = [G[0], G[1], T[0]]
            for b in range(3):
                pe.matmul(EB[b][:, :], identb[:, :], mask1[:, :, :].rearrange("p h n -> p (h n)"),
                          start=True, stop=True)
                for h in range(4 * b, 4 * b + 4):
                    o = EB[b][:, (h % 4) * P:(h % 4 + 1) * P]
                    pe.matmul(o, w_l[:, h, :], actT[:, h // 2, :], start=False, stop=True, skip_group_check=True)
                    mm = pe.matmul(o, actT[:, h // 2, :], w_r[:, h, :], start=False, stop=True,
                                   skip_group_check=True)
                mm.then_inc(sem("b1_logits"), 1)
            for c in range(KC):
                mm = pe.matmul(A[c // HC][:, (c % HC) * P:(c % HC + 1) * P], actT[:, c, :], bd[:, 0:P],
                               start=True, stop=True)
                if c % HC == HC - 1:
                    mm.then_inc(sem("ft_psum"), 1)
            for c in range(KC):
                pe.matmul(A[2 + c // HC][:, (c % HC) * P:(c % HC + 1) * P], actT[:, c, :], bd[:, P:2 * P],
                          start=(c % HC == 0), stop=True, skip_group_check=True)
            pe.wait_ge(sem("ft"), 2)
            AB = [A[0], A[1], T[1]]
            for b in range(3):
                pe.wait_ge(sem("b1_alpha"), b + 1)
                for h in range(4 * b, 4 * b + 4):
                    mm = pe.transpose(AB[b][:, (h % 4) * P:(h % 4 + 1) * P], e12[:, h, :], ident[:, :])
                mm.then_inc(sem("b1_alphaT_psum"), 1)
            for h in range(H1):
                if h % 4 == 0:
                    pe.wait_ge(sem("b1_alphaT"), h // 4 + 1)
                mm = pe.matmul(A[2 + h // 6][:, (h % 6) * O1:(h % 6 + 1) * O1], alphaT12[:, h, :],
                               h_nat[:, h * O1:(h + 1) * O1], start=False, stop=True, skip_group_check=True)
                if h % 6 == 5:
                    mm.then_inc(sem("b1_agg"), 1)

            def logits(eb, heads, name):
                pe.matmul(eb[:, 0:heads * P], identb[:, :], mask2[:, 0:heads, :].rearrange("p h n -> p (h n)"),
                          start=True, stop=False)
                pe.wait_ge(sem(name + "_diag"), 1)
                pe.matmul(eb[:, 0:heads * P], onesf[:, :], diag4[:, 0:heads, :].rearrange("p h n -> p (h n)"),
                          start=False, stop=True).then_inc(sem(name + "_logits"), 1)

            def alpha_transposes(ab, heads, name):
                pe.wait_ge(sem(name + "_alpha"), 1)
                for h in range(heads):
                    mm = pe.transpose(ab[:, h * P:(h + 1) * P], e4[:, h, :], ident[:, :])
                mm.then_inc(sem(name + "_alphaT_psum"), 1)
                pe.wait_ge(sem(name + "_alphaT"), 1)

            x_transposes(1)
            project(U_C1, A[0:2], actT, KC, "c1_proj")
            logits(G[0], 1, "c1")
            alpha_transposes(G[1], 1, "c1")
            for c in range(KC):
                mm = pe.matmul(T[c // HC][:, (c % HC) * P:(c % HC + 1) * P], h_nat[:, c * P:(c + 1) * P],
                               alphaT4[:, 0, :], start=True, stop=True)
                if c % HC == HC - 1:
                    mm.then_inc(sem("c1_agg"), 1)
            pe.wait_ge(sem("c1_outT_a"), 1)
            pe.wait_ge(sem("c1_outT_b"), 1)
            project(U_C2, A[2:4], hidT, KC, "c2_proj")
            logits(G[0], 1, "c2")
            alpha_transposes(G[1], 1, "c2")
            for half in range(2):
                pe.matmul(A[half][:, 0:HALF], alphaT4[:, 0, :], h_nat[:, half * HALF:(half + 1) * HALF],
                          start=True, stop=False)
                add_row(A[half], "c2b", half * HALF, HALF).then_inc(sem("c2_agg"), 1)

            x_transposes(2)
            project(U_G1, A[0:2], actT, KC, "g1_proj", w=512)
            project(U_R1, A[2:4], actT, KC, "r1_proj", "r1b", w=512)
            logits(G[0], H3, "g1")
            for half in range(2):
                pe.wait_ge(sem("resid"), half + 1)
                for c in range(4):
                    mm = pe.transpose(T[half][:, c * P:(c + 1) * P], resid[:, (half * 4 + c) * P:(half * 4 + c + 1) * P],
                                      ident[:, :])
                mm.then_inc(sem("residT_psum"), 1)
            alpha_transposes(G[1], H3, "g1")
            for half in range(2):
                add_row(A[half], "g1b", half * 512, 512, start=True)
                for h in (2 * half, 2 * half + 1):
                    mm = pe.matmul(A[half][:, (h % 2) * O3:(h % 2 + 1) * O3], alphaT4[:, h, :],
                                   h_nat[:, h * O3:(h + 1) * O3], start=False, stop=True, skip_group_check=True)
                mm.then_inc(sem("g1_agg"), 1)
            for half in range(2):
                pe.wait_ge(sem("g1_norm"), half + 1)
                for c in range(4):
                    cc = half * 4 + c
                    mm = pe.transpose(G[half][:, c * P:(c + 1) * P], norm[:, cc * P:(cc + 1) * P], ident[:, :])
                mm.then_inc(sem("g1_normT_psum"), 1)
            pe.wait_ge(sem("g1_outT"), 2)
            project(U_G2, A[2:4], hidT, K3, "g2_proj")
            for half in range(2):
                for k in range(K3):
                    b = (half * K3 + k) * HALF
                    u = U_R2 + b // UNIT
                    if b % UNIT == 0:
                        arrived(u, u % REGION)
                    o = (u % RING) * UNIT + b % UNIT
                    pe.matmul(G[half][:, 0:HALF], hidT[:, k, :], ring[:, o:o + HALF], start=(k == 0), stop=False)
                add_row(G[half], "r2b", half * HALF, HALF, stop=False)
                add_row(G[half], "ln2b", half * HALF, HALF).then_inc(sem("r2_proj"), 1)
            logits(T[0], 1, "g2")
            alpha_transposes(T[1], 1, "g2")
            for half in range(2):
                pe.matmul(A[half][:, 0:HALF], alphaT4[:, 0, :], h_nat[:, half * HALF:(half + 1) * HALF],
                          start=True, stop=False)
                add_row(A[half], "g2b", half * HALF, HALF).then_inc(sem("g2_agg"), 1)

        @block.scalar
        def _(act):
            def copy_actT(n):
                for half in range(2):
                    act.wait_ge(sem("actT_psum"), n + half + 1)
                    act.copy(actT[:, half * HC:(half + 1) * HC, :].rearrange("p k n -> p (k n)"),
                             T[half][:, 0:HALF]).then_inc(sem("actT"), 1)

            copy_actT(0)
            act.wait_ge(sem("cnt"), 1)
            act.copy(edge_sum[:, :], G[0][:, P:P + DE]).then_inc(sem("edge_sum"), 1)
            act.wait_ge(sem("mixT"), 1)
            act.copy(edge_sumT[:, :, :].rearrange("p k n -> p (k n)"), T[0][:, P:3 * P]
                     ).then_inc(sem("edge_sumT"), 1)
            act.wait_ge(sem("deg_rows"), 1)
            act.copy(degB[:, :], T[1][:, 0:P]).then_inc(sem("degB"), 1)
            with act.Fori(0, LAYERS) as l:
                for half in range(2):
                    act.wait_ge(sem("actT_psum"), 2 * l + 3 + half)
                    act.copy(actT[:, half * HC:(half + 1) * HC, :].rearrange("p k n -> p (k n)"),
                             T[half][:, 0:HALF]).then_inc(sem("actT"), 1)
                act.wait_ge(sem("hidT_psum"), 2 * l + 1)
                act.wait_ge(sem("lncol"), 2 * l + 2)
                for c in range(HC):
                    ins = act.activation(hidT[:, c, :], T[0][:, c * P:(c + 1) * P], ACT.Relu,
                                         bias=lncol[:, KC + c:KC + c + 1], scale=lncol[:, c:c + 1])
                ins.then_inc(sem("hidT_a"), 1)

            copy_actT(2 * LAYERS + 2)
            for half in range(2):
                act.wait_ge(sem("k_proj"), half + 1)
                act.copy(k_nat[:, half * HALF:(half + 1) * HALF], A[2 + half][:, 0:HALF]).then_inc(sem("k_nat"), 1)
            for b in range(2):
                act.wait_ge(sem("qT_psum"), b + 1)
                act.copy(qT[0:DH, 4 * b:4 * b + 4, :].rearrange("p h n -> p (h n)"), T[b][0:DH, :]
                         ).then_inc(sem("qT"), 1)
            for half in range(2):
                act.wait_ge(sem("v_proj"), half + 1)
                act.copy(v_nat[:, half * HALF:(half + 1) * HALF], G[half][:, 0:HALF]).then_inc(sem("v_nat"), 1)
            for b in range(2):
                act.wait_ge(sem("score_shift"), b + 1)
                pb = prob[:, 4 * b:4 * b + 4, :].rearrange("p h n -> p (h n)")
                act.activation(pb, pb, ACT.Exp).then_inc(sem("prob"), 1)
            act.wait_ge(sem("probT_psum"), 1)
            act.copy(probT[:, 0:4, :].rearrange("p h n -> p (h n)"), T[0][:, :]).then_inc(sem("probT"), 1)
            act.wait_ge(sem("probT_psum"), 2)
            act.copy(probT[:, 4:8, :].rearrange("p h n -> p (h n)"), T[1][:, :]).then_inc(sem("probT"), 1)
            for half in range(2):
                act.wait_ge(sem("attnT_psum"), half + 1)
                act.copy(hidT[:, half * HC:(half + 1) * HC, :].rearrange("p k n -> p (k n)"), G[half][:, 0:HALF]
                         ).then_inc(sem("attnT"), 1)

            copy_actT(2 * LAYERS + 4)
            EB = [G[0], G[1], T[0]]
            for b in range(3):
                act.wait_ge(sem("b1_logits"), b + 1)
                act.activation(e12[:, 4 * b:4 * b + 4, :].rearrange("p h n -> p (h n)"), EB[b][:, :],
                               ACT.Copy).then_inc(sem("b1_raw"), 1)
            for half in range(2):
                act.wait_ge(sem("ft_psum"), half + 1)
                act.copy(h_nat[:, half * HALF:(half + 1) * HALF], A[half][:, 0:HALF]).then_inc(sem("ft"), 1)
            for b in range(3):
                act.wait_ge(sem("b1_shift"), b + 1)
                eb = e12[:, 4 * b:4 * b + 4, :].rearrange("p h n -> p (h n)")
                act.activation(eb, eb, ACT.Exp).then_inc(sem("b1_exp"), 1)
            AB = [A[0], A[1], T[1]]
            for b in range(3):
                act.wait_ge(sem("b1_alphaT_psum"), b + 1)
                act.copy(alphaT12[:, 4 * b:4 * b + 4, :].rearrange("p h n -> p (h n)"), AB[b][:, :]
                         ).then_inc(sem("b1_alphaT"), 1)

            def copy_h(banks, w, name):
                for half in range(2):
                    act.wait_ge(sem(name + "_proj"), half + 1)
                    act.copy(h_nat[:, half * w:(half + 1) * w], banks[half][:, 0:w]).then_inc(sem(name + "_h"), 1)

            def attend_one(eb, ab, name):
                act.wait_ge(sem(name + "_logits"), 1)
                act.wait_ge(sem(name + "_dst"), 1)
                act.activation(e4[:, 0, :], eb[:, 0:P], ACT.Identity, bias=small[:, 5:6]).then_inc(sem(name + "_raw"), 1)
                act.wait_ge(sem(name + "_max"), 1)
                act.activation(e4[:, 0, :], e4[:, 0, :], ACT.Exp, bias=small[:, 6:7]).then_inc(sem(name + "_exp"), 1)
                act.wait_ge(sem(name + "_alphaT_psum"), 1)
                act.copy(alphaT4[:, 0, :], ab[:, 0:P]).then_inc(sem(name + "_alphaT"), 1)

            copy_actT(2 * LAYERS + 6)
            copy_h(A[0:2], HALF, "c1")
            attend_one(G[0], G[1], "c1")
            act.wait_ge(sem("c1_agg"), 1)
            for c in range(HC):
                ins = act.activation(hidT[:, c, :], T[0][:, c * P:(c + 1) * P], ACT.Relu,
                                     bias=cols[:, COL_C1B + c:COL_C1B + c + 1])
            ins.then_inc(sem("c1_outT_a"), 1)
            copy_h(A[2:4], HALF, "c2")
            attend_one(G[0], G[1], "c2")

            copy_actT(2 * LAYERS + 8)
            copy_h(A[0:2], 512, "g1")
            for half in range(2):
                act.wait_ge(sem("r1_proj"), half + 1)
                act.copy(resid[:, half * 512:(half + 1) * 512], A[2 + half][:, :]).then_inc(sem("resid"), 1)
            act.wait_ge(sem("g1_logits"), 1)
            act.wait_ge(sem("g1_dst"), 1)
            for h in range(H3):
                ins = act.activation(e4[:, h, :], G[0][:, h * P:(h + 1) * P], ACT.Identity,
                                     bias=small[:, 4 + h:5 + h])
            ins.then_inc(sem("g1_raw"), 1)
            for half in range(2):
                act.wait_ge(sem("residT_psum"), half + 1)
                act.copy(residT[:, half * 4:half * 4 + 4, :].rearrange("p k n -> p (k n)"), T[half][:, :]
                         ).then_inc(sem("residT"), 1)
            act.wait_ge(sem("g1_shift"), 1)
            act.activation(e4[:, :, :].rearrange("p h n -> p (h n)"), e4[:, :, :].rearrange("p h n -> p (h n)"),
                           ACT.Exp).then_inc(sem("g1_exp"), 1)
            act.wait_ge(sem("g1_alphaT_psum"), 1)
            act.copy(alphaT4[:, :, :].rearrange("p h n -> p (h n)"), G[1][:, :]).then_inc(sem("g1_alphaT"), 1)
            for half in range(2):
                act.wait_ge(sem("g1_normT_psum"), half + 1)
                for c in range(4):
                    cc = half * 4 + c
                    ins = act.activation(hidT[:, cc, :], G[half][:, c * P:(c + 1) * P], ACT.Relu,
                                         bias=cols[:, COL_G1B + cc:COL_G1B + cc + 1],
                                         scale=cols[:, COL_G1G + cc:COL_G1G + cc + 1])
                ins.then_inc(sem("g1_relu"), 1)
            copy_h(A[2:4], HALF, "g2")
            attend_one(T[0], T[1], "g2")

        @block.vector
        def _(v):
            done = [0]

            def step(ins):
                done[0] = done[0] + 1
                ins.then_inc(sem("vector_step"), 1)
                v.wait_ge(sem("vector_step"), done[0])

            v.wait_ge(sem("iotas"), 2)
            v.tensor_scalar(ident[:, :], iota_i[:, 0:P], 0.0, None, ALU.is_equal).then_inc(sem("ident"), 1)
            step(v.tensor_copy(colf[:, :], iota_i[:, P:2 * P]))
            v.wait_ge(sem("rows_in"), 16)
            step(v.tensor_copy(parts[:, 0, :], rows_f[:, :]))
            step(v.tensor_tensor(rows_r[:, :], rows_f[:, :], parts[:, 0, :], ALU.subtract))
            step(v.tensor_copy(parts[:, 1, :], rows_r[:, :]))
            step(v.tensor_tensor(rows_f[:, :], rows_r[:, :], parts[:, 1, :], ALU.subtract))
            v.tensor_copy(parts[:, 2, :], rows_f[:, :]).then_inc(sem("row_parts"), 1)
            v.wait_ge(sem("src_in"), 16)
            v.wait_ge(sem("dst_in"), 16)
            step(v.tensor_copy(edge_f[:, :], edge_idx[:, :]))
            cb = colf[:, :].unsqueeze(1).broadcast_to([P, EC, P])
            v.tensor_tensor(dst_hot, edge_f[:, EC:2 * EC].unsqueeze(2).broadcast_to([P, EC, P]), cb,
                            ALU.is_equal).then_inc(sem("one_hots"), 1)
            v.tensor_tensor(src_edge[:, :, 0:P], edge_f[:, 0:EC].unsqueeze(2).broadcast_to([P, EC, P]), cb,
                            ALU.is_equal).then_inc(sem("one_hots"), 1)
            v.wait_ge(sem("ident"), 1)
            v.tensor_copy(identb[:, :], ident[:, :]).then_inc(sem("identb"), 1)
            v.wait_ge(sem("blk_in"), 16)
            v.wait_ge(sem("bd_zero"), 1)
            for i in range(2):
                for q in range(2):
                    v.tensor_copy(bd[q * O1:(q + 1) * O1, i * P + q * O1:i * P + (q + 1) * O1],
                                  blk[q * O1:(q + 1) * O1, i * O1:(i + 1) * O1]).then_inc(sem("bd"), 1)
            for half in range(2):
                v.wait_ge(sem("node_proj"), half + 1)
                v.tensor_copy(nodes[:, half * HALF:(half + 1) * HALF], A[half][:, 0:HALF]).then_inc(sem("nodes"), 1)
            v.wait_ge(sem("edge_sums"), 1)
            v.tensor_copy(cnt[:, :], G[0][:, 0:P]).then_inc(sem("cnt"), 1)
            v.wait_ge(sem("cnt"), 1)
            step(v.tensor_reduce(deg[:, :], cnt[:, :], AX.X, ALU.add))
            v.wait_ge(sem("graph_T"), 1)
            v.tensor_copy(cntT[:, :], T[0][:, 0:P]).then_inc(sem("cntT"), 1)
            v.wait_ge(sem("cntT"), 1)
            v.scalar_tensor_tensor(mixT[:, :], ident[:, :], deg[:, 0:1], cntT[:, :], ALU.mult, ALU.add
                                   ).then_inc(sem("mixT"), 1)
            v.wait_ge(sem("cols_in"), 16)
            v.wait_ge(sem("degB"), 1)
            v.wait_ge(sem("edge_proj"), 1)
            for c in range(KC):
                ins = v.scalar_tensor_tensor(edge_term[:, c, :], degB[:, :], cols[:, COL_BE + c:COL_BE + c + 1],
                                             G[c // HC][:, (c % HC) * P:(c % HC + 1) * P], ALU.mult, ALU.add)
            ins.then_inc(sem("edge_term"), 1)
            v.wait_ge(sem("edge_term"), 1)
            v.wait_ge(sem("wlr_psum"), 1)
            v.tensor_copy(wlr[:, :], A[2][:, 0:2 * H1]).then_inc(sem("wlr"), 1)
            step(v.tensor_tensor(cnt_self[:, :], cnt[:, :], ident[:, :], ALU.add))
            step(v.tensor_scalar(maskf[:, 0:P], cnt[:, :], 0.5, MASKED, ALU.is_lt, ALU.mult))
            step(v.tensor_scalar(maskf[:, P:2 * P], cnt_self[:, :], 0.5, MASKED, ALU.is_lt, ALU.mult))
            for i, m in enumerate((mask1, mask2)):
                v.tensor_copy(m[:, :, :], maskf[:, i * P:(i + 1) * P].unsqueeze(1).broadcast_to([P, 4, P])
                              ).then_inc(sem("masks"), 1)

            def layer_stats(halves, n):
                for i, h in enumerate(halves):
                    step(v.bn_stats(stats[:, 6 * i:6 * i + 6], h))
                step(v.bn_aggr(mv[:, :], stats[:, :]))
                v.tensor_scalar(veps[:, :], mv[:, 1:2], EPS, None, ALU.add).then_inc(sem("ln_var"), 1)
                v.wait_ge(sem("ln_rstd"), n + 1)

            def normalise(dst, src):
                return v.tensor_scalar(dst, src, mv[:, 0:1], rstd[:, 0:1], ALU.subtract, ALU.mult)

            def leaky(e):
                return v.scalar_tensor_tensor(e, e, SLOPE, e, ALU.mult, ALU.max)

            LINKS = 4
            at = done[0]
            with v.Fori(0, LAYERS) as l:
                done[0] = l * LINKS + at
                v.tensor_copy(lncol[:, 0:KC], cols[:, bass.ds(l * KC + COL_LNG, KC)]).then_inc(sem("lncol"), 1)
                v.tensor_copy(lncol[:, KC:2 * KC], cols[:, bass.ds(l * KC + COL_LNB, KC)]).then_inc(sem("lncol"), 1)
                for half in range(2):
                    v.wait_ge(sem("agg_psum"), 2 * l + half + 1)
                    ins = v.tensor_tensor(aggT[:, half * HC:(half + 1) * HC, :].rearrange("p k n -> p (k n)"),
                                          G[half][:, 0:HALF],
                                          edge_term[:, half * HC:(half + 1) * HC, :].rearrange("p k n -> p (k n)"),
                                          ALU.add).then_inc(sem("aggT"), 1)
                for half in range(2):
                    v.wait_ge(sem("hidden_proj"), 2 * l + half + 1)
                    step(v.bn_stats(stats[:, 6 * half:6 * half + 6], A[half][:, 0:HALF]))
                v.nop(nofuse=True)
                step(v.bn_aggr(mv[:, :], stats[:, :]))
                v.tensor_scalar(veps[:, :], mv[:, 1:2], EPS, None, ALU.add).then_inc(sem("ln_var"), 1)
                v.wait_ge(sem("ln_rstd"), l + 1)
                for half in range(2):
                    normalise(norm[:, half * HALF:(half + 1) * HALF], A[half][:, 0:HALF]
                              ).then_inc(sem("hidden_norm"), 1)
                v.wait_ge(sem("hidT_psum"), 2 * l + 2)
                v.wait_ge(sem("lncol"), 2 * l + 2)
                for c in range(HC):
                    cc = HC + c
                    ins = v.tensor_scalar(hidT[:, cc, :], T[1][:, c * P:(c + 1) * P], lncol[:, cc:cc + 1],
                                          lncol[:, KC + cc:KC + cc + 1], ALU.mult, ALU.add)
                step(ins)
                hb = hidT[:, HC:2 * HC, :].rearrange("p k n -> p (k n)")
                v.tensor_scalar(hb, hb, 0.0, None, ALU.max).then_inc(sem("hidT_b"), 1)
                for half in range(2):
                    v.wait_ge(sem("update_proj"), 2 * l + half + 1)
                    nh = nodes[:, half * HALF:(half + 1) * HALF]
                    v.tensor_tensor(nh, A[2 + half][:, 0:HALF], nh, ALU.add).then_inc(sem("nodes"), 1)
            done[0] = at + LAYERS * LINKS

            v.wait_ge(sem("w_zero"), 2)
            v.wait_ge(sem("wlr"), 1)
            for i, w in enumerate((w_l, w_r)):
                for q in range(2):
                    s = slice(q * O1, (q + 1) * O1)
                    v.tensor_copy(w[s, q:H1:2, :],
                                  wlr[s, i * H1 + q:(i + 1) * H1:2].unsqueeze(2).broadcast_to([O1, H1 // 2, P])
                                  ).then_inc(sem("w_lr"), 1)
            for half in range(2):
                v.wait_ge(sem("q_proj"), half + 1)
                v.tensor_scalar(q_nat[:, half * HALF:(half + 1) * HALF], A[half][:, 0:HALF], DH ** -0.5, None,
                                ALU.mult).then_inc(sem("q_nat"), 1)
            v.wait_ge(sem("nodes"), 2 * LAYERS + 2)
            step(v.tensor_tensor(x[:, :], x[:, :], nodes[:, :], ALU.add))
            for b in range(2):
                v.wait_ge(sem("kT_psum"), b + 1)
                v.tensor_copy(kT[0:DH, 4 * b:4 * b + 4, :].rearrange("p h n -> p (h n)"), A[b][0:DH, :]
                              ).then_inc(sem("kT"), 1)
            for b in range(2):
                v.wait_ge(sem("scores"), b + 1)
                sc = A[2 + b][:, :].rearrange("p (h n) -> p h n", h=4)
                step(v.tensor_reduce(small[:, 16 + 4 * b:20 + 4 * b], sc, AX.X, ALU.max))
                v.tensor_tensor(prob[:, 4 * b:4 * b + 4, :], sc,
                                small[:, 16 + 4 * b:20 + 4 * b].unsqueeze(2).broadcast_to([P, 4, P]),
                                ALU.subtract).then_inc(sem("score_shift"), 1)
            for b in range(2):
                v.wait_ge(sem("prob"), b + 1)
                step(v.tensor_reduce(small[:, 24 + 4 * b:28 + 4 * b], prob[:, 4 * b:4 * b + 4, :], AX.X, ALU.add))
            step(v.reciprocal(small[:, 32:40], small[:, 24:32]))
            for b in range(2):
                v.wait_ge(sem("attn_psum"), b + 1)
                v.tensor_tensor(norm[:, b * HALF:(b + 1) * HALF].rearrange("p (h n) -> p h n", h=4),
                                A[b][:, 0:HALF].rearrange("p (h n) -> p h n", h=4),
                                small[:, 32 + 4 * b:36 + 4 * b].unsqueeze(2).broadcast_to([P, 4, DH]),
                                ALU.mult).then_inc(sem("attended"), 1)

            def block_end(banks, name, n):
                for half in range(2):
                    v.wait_ge(sem(name), half + 1)
                    s = slice(half * HALF, (half + 1) * HALF)
                    step(v.tensor_tensor(x[:, s], banks[half][:, 0:HALF], x[:, s], ALU.add))
                layer_stats([x[:, 0:HALF], x[:, HALF:D]], n)
                for half in range(2):
                    s = slice(half * HALF, (half + 1) * HALF)
                    normalise(x[:, s], x[:, s]).then_inc(sem("x_ready"), 1)

            block_end(A[2:4], "out_proj", LAYERS)
            v.wait_ge(sem("x_ready"), 2)

            for b in range(3):
                v.wait_ge(sem("b1_raw"), b + 1)
                eb = e12[:, 4 * b:4 * b + 4, :]
                mx = small[:, 16 + 4 * b:20 + 4 * b]
                step(leaky(eb))
                step(v.tensor_reduce(mx, eb, AX.X, ALU.max))
                v.tensor_tensor(eb, eb, mx.unsqueeze(2).broadcast_to([P, 4, P]), ALU.subtract
                                ).then_inc(sem("b1_shift"), 1)
            for b in range(3):
                v.wait_ge(sem("b1_exp"), b + 1)
                eb = e12[:, 4 * b:4 * b + 4, :]
                dn = small[:, 32 + 4 * b:36 + 4 * b]
                step(v.tensor_tensor(eb, eb, cnt[:, :].unsqueeze(1).broadcast_to([P, 4, P]), ALU.mult))
                step(v.tensor_reduce(dn, eb, AX.X, ALU.add))
                step(v.tensor_scalar(dn, dn, 1e-16, None, ALU.max))
                step(v.reciprocal(dn, dn))
                v.tensor_tensor(eb, eb, dn.unsqueeze(2).broadcast_to([P, 4, P]), ALU.mult
                                ).then_inc(sem("b1_alpha"), 1)
            for half in range(2):
                v.wait_ge(sem("b1_agg"), half + 1)
                s = slice(half * HALF, (half + 1) * HALF)
                step(v.scalar_tensor_tensor(x[:, s], A[2 + half][:, 0:HALF], 0.0, x[:, s], ALU.max, ALU.add))
            layer_stats([x[:, 0:HALF], x[:, HALF:D]], LAYERS + 1)
            for half in range(2):
                s = slice(half * HALF, (half + 1) * HALF)
                normalise(x[:, s], x[:, s]).then_inc(sem("x_ready"), 1)
            v.wait_ge(sem("x_ready"), 4)

            def attend_one(src_at, dst_at, att, name, guard):
                for half in range(2):
                    v.wait_ge(sem(name + "_h"), half + 1)
                    s = slice(half * HALF, (half + 1) * HALF)
                    for i, a in enumerate((src_at, dst_at)):
                        step(v.tensor_tensor_reduce(junk[:, :], h_nat[:, s],
                                                    att[:, a + half * HALF:a + (half + 1) * HALF], 1.0, 0.0,
                                                    ALU.mult, ALU.add, small[:, 2 * half + i:2 * half + i + 1]))
                step(v.tensor_tensor(small[:, 4:6], small[:, 0:2], small[:, 2:4], ALU.add))
                v.tensor_scalar(diag4[:, 0, :], ident[:, :], small[:, 4:5], None, ALU.mult
                                ).then_inc(sem(name + "_diag"), 1)
                v.sem_inc(sem(name + "_dst"), 1)
                v.wait_ge(sem(name + "_raw"), 1)
                step(leaky(e4[:, 0, :]))
                v.tensor_reduce(small[:, 6:7], e4[:, 0, :], AX.X, ALU.max, negate=True).then_inc(sem(name + "_max"), 1)
                v.wait_ge(sem(name + "_exp"), 1)
                step(v.tensor_tensor_reduce(e4[:, 0, :], e4[:, 0, :], cnt_self[:, :], 1.0, 0.0, ALU.mult, ALU.add,
                                            small[:, 7:8]))
                if guard:
                    step(v.tensor_scalar(small[:, 7:8], small[:, 7:8], 1e-16, None, ALU.add))
                step(v.reciprocal(small[:, 8:9], small[:, 7:8]))
                v.tensor_scalar(e4[:, 0, :], e4[:, 0, :], small[:, 8:9], None, ALU.mult
                                ).then_inc(sem(name + "_alpha"), 1)

            v.wait_ge(sem("att2_in"), 64)
            attend_one(0, D, att2, "c1", False)
            v.wait_ge(sem("c1_agg"), 2)
            for c in range(HC):
                cc = HC + c
                ins = v.tensor_scalar(hidT[:, cc, :], T[1][:, c * P:(c + 1) * P],
                                      cols[:, COL_C1B + cc:COL_C1B + cc + 1], 0.0, ALU.add, ALU.max)
            ins.then_inc(sem("c1_outT_b"), 1)
            attend_one(2 * D, 3 * D, att2, "c2", False)
            block_end(A[0:2], "c2_agg", LAYERS + 2)
            v.wait_ge(sem("x_ready"), 6)

            v.wait_ge(sem("att3_in"), 16 * len(range(0, ATT3, D)))
            for h in range(H3):
                if h % 2 == 0:
                    v.wait_ge(sem("g1_h"), h // 2 + 1)
                for i in range(2):
                    s = slice(h * O3, (h + 1) * O3)
                    step(v.tensor_tensor_reduce(junk[:, 0:O3], h_nat[:, s], att3[:, i * D3 + h * O3:i * D3 + (h + 1) * O3],
                                                1.0, 0.0, ALU.mult, ALU.add, small[:, 4 * i + h:4 * i + h + 1]))
            v.tensor_tensor(diag4[:, :, :], ident[:, :].unsqueeze(1).broadcast_to([P, 4, P]),
                            small[:, 0:4].unsqueeze(2).broadcast_to([P, 4, P]), ALU.mult).then_inc(sem("g1_diag"), 1)
            v.sem_inc(sem("g1_dst"), 1)
            v.wait_ge(sem("g1_raw"), 1)
            step(leaky(e4[:, :, :]))
            step(v.tensor_reduce(small[:, 8:12], e4[:, :, :], AX.X, ALU.max))
            v.tensor_tensor(e4[:, :, :], e4[:, :, :], small[:, 8:12].unsqueeze(2).broadcast_to([P, 4, P]),
                            ALU.subtract).then_inc(sem("g1_shift"), 1)
            v.wait_ge(sem("g1_exp"), 1)
            step(v.tensor_tensor(e4[:, :, :], e4[:, :, :], cnt_self[:, :].unsqueeze(1).broadcast_to([P, 4, P]),
                                 ALU.mult))
            step(v.tensor_reduce(small[:, 12:16], e4[:, :, :], AX.X, ALU.add))
            step(v.tensor_scalar(small[:, 12:16], small[:, 12:16], 1e-16, None, ALU.add))
            step(v.reciprocal(small[:, 16:20], small[:, 12:16]))
            v.tensor_tensor(e4[:, :, :], e4[:, :, :], small[:, 16:20].unsqueeze(2).broadcast_to([P, 4, P]),
                            ALU.mult).then_inc(sem("g1_alpha"), 1)
            for half in range(2):
                v.wait_ge(sem("g1_agg"), half + 1)
                step(v.bn_stats(stats[:, 6 * half:6 * half + 6], A[half][:, :]))
            step(v.bn_aggr(mv[:, :], stats[:, :]))
            v.tensor_scalar(veps[:, :], mv[:, 1:2], EPS, None, ALU.add).then_inc(sem("ln_var"), 1)
            v.wait_ge(sem("ln_rstd"), LAYERS + 4)
            for half in range(2):
                normalise(norm[:, half * 512:(half + 1) * 512], A[half][:, :]).then_inc(sem("g1_norm"), 1)
            v.wait_ge(sem("residT"), 2)
            for half in range(2):
                v.wait_ge(sem("g1_relu"), half + 1)
                hh = hidT[:, half * 4:half * 4 + 4, :].rearrange("p k n -> p (k n)")
                v.tensor_tensor(hh, hh, residT[:, half * 4:half * 4 + 4, :].rearrange("p k n -> p (k n)"), ALU.add
                                ).then_inc(sem("g1_outT"), 1)
            attend_one(2 * D3, 2 * D3 + D, att3, "g2", True)
            for half in range(2):
                v.wait_ge(sem("r2_proj"), half + 1)
                s = slice(half * HALF, (half + 1) * HALF)
                step(v.tensor_tensor(x[:, s], G[half][:, 0:HALF], x[:, s], ALU.add))
            for half in range(2):
                v.wait_ge(sem("g2_agg"), half + 1)
                step(v.bn_stats(stats[:, 6 * half:6 * half + 6], A[half][:, 0:HALF]))
            step(v.bn_aggr(mv[:, :], stats[:, :]))
            v.tensor_scalar(veps[:, :], mv[:, 1:2], EPS, None, ALU.add).then_inc(sem("ln_var"), 1)
            v.wait_ge(sem("ln_rstd"), LAYERS + 5)
            for half in range(2):
                s = slice(half * HALF, (half + 1) * HALF)
                step(normalise(norm[:, s], A[half][:, 0:HALF]))
                step(v.tensor_tensor(norm[:, s], norm[:, s],
                                     att3[:, 2 * D3 + 2 * D + half * HALF:2 * D3 + 2 * D + (half + 1) * HALF], ALU.mult))
                step(v.tensor_tensor(x[:, s], x[:, s], norm[:, s], ALU.add))
            layer_stats([x[:, 0:HALF], x[:, HALF:D]], LAYERS + 5)
            for half in range(2):
                s = slice(half * HALF, (half + 1) * HALF)
                normalise(norm[:, s], x[:, s]).then_inc(sem("out_ready"), 1)


def _np_inputs(inputs):
    import numpy as np

    a = {k: np.asarray(v) for k, v in inputs.items()}

    def halves(wT, w):
        n_in, n_out = wT.shape
        return wT.reshape(n_in // P, P, n_out // w, w).transpose(1, 2, 0, 3).reshape(P, -1)

    mats = [halves(a["L0_gnn_Wn"].T, HALF),
            a["L0_gnn_We"].T.reshape(2, P, D).transpose(1, 0, 2).reshape(P, -1)]
    for l in range(LAYERS):
        mats += [halves(a["L0_gnn_W1"][l].T, HALF), halves(a["L0_gnn_W2"][l].T, HALF)]
    qkv = a["L0_gnn_Wqkv"]
    mats += [halves(qkv[i * D:(i + 1) * D].T, HALF) for i in range(3)]
    mats += [halves(a["L0_gnn_Wo"].T, HALF), halves(a["L2_gnn_W1"], HALF), halves(a["L2_gnn_W2"], HALF)]
    mats += [halves(a["L3_gnn_W1"], 512), halves(a["L3_gnn_Wr1"], 512),
             halves(a["L3_gnn_W2"], HALF), halves(a["L3_gnn_Wr2"], HALF)]
    stream = np.concatenate(mats, axis=1)
    stream = stream.reshape(P, -1, UNIT).transpose(1, 0, 2)

    def columns(v):
        return v.reshape(-1, P).T

    cols = np.concatenate([columns(a[n]) for n in ("L0_gnn_be", "L2_gnn_b1", "L3_gnn_g1", "L3_gnn_be1",
                                                   "L0_gnn_ln_g", "L0_gnn_ln_b")], axis=1)
    row = {"bn": "L0_gnn_bn", "b1": "L0_gnn_b1", "b2": "L0_gnn_b2", "bo": "L0_gnn_bo", "c2b": "L2_gnn_b2",
           "bqkv": "L0_gnn_bqkv", "g1b": "L3_gnn_b1", "r1b": "L3_gnn_br1", "g2b": "L3_gnn_b2",
           "r2b": "L3_gnn_br2", "ln2b": "L3_gnn_be2"}
    rows = np.concatenate([np.concatenate([a[row[n]].reshape(-1) for n, _ in g]).reshape(P, -1) for g in ROWS],
                          axis=1)
    W, Wr = a["L1_gnn_W"], a["L1_gnn_W_res"]
    wt = np.concatenate([W.T, Wr.T], axis=1)
    blk = np.concatenate([wt, wt], axis=0)
    blka = np.concatenate([W, W, a["L1_gnn_attn_l"][0].T, a["L1_gnn_attn_r"][0].T], axis=1)
    att = np.concatenate([a[n].reshape(-1) for n in (
        "L2_gnn_att_src1", "L2_gnn_att_dst1", "L2_gnn_att_src2", "L2_gnn_att_dst2",
        "L3_gnn_a_src1", "L3_gnn_a_dst1", "L3_gnn_a_src2", "L3_gnn_a_dst2", "L3_gnn_g2")]).reshape(1, -1)
    return {"x": a["x"], "src": a["src"].reshape(P, EC), "dst": a["dst"].reshape(P, EC),
            "edge": a["edge_attr_256"].reshape(P, EC, DE), "stream": stream, "cols": cols, "rows": rows,
            "blk": blk, "blka": blka, "att": att}


def kernel(**inputs):
    import numpy as np
    import concourse.bacc as bacc
    from concourse.bass_utils import run_bass_kernel_spmd as run

    nc = bacc.Bacc("TRN2", target_bir_lowering=False, num_devices=1)
    arrays, args = {}, []
    for name, a in _np_inputs(inputs).items():
        a = np.ascontiguousarray(a)
        arrays[f"in_{name}"] = a
        args.append(nc.dram_tensor(f"in_{name}", a.shape, mybir.dt.from_np(a.dtype), kind="ExternalInput").ap())
    out = nc.dram_tensor("out_x", (P, D), F32, kind="ExternalOutput").ap()
    gnn_kernel(nc, *args, out)
    return run(nc, [arrays], core_ids=[0]).results[0]["out_x"]
```

```python
import concourse.bass as bass
from concourse import mybir
from contextlib import ExitStack

F32 = mybir.dt.float32
BF16 = mybir.dt.bfloat16
I32 = mybir.dt.int32
ALU = mybir.AluOpType
ACT = mybir.ActivationFunctionType
AX = mybir.AxisListType

P = 128
D = 768
DE = 256
E = 2176
EC = E // P
KC = D // P
HALF = D // 2
HC = 3
LAYERS = 3
H0, DH = 8, 96
H1, O1 = 12, 64
H3, O3 = 4, 256
D3 = H3 * O3
K3 = D3 // P
SLOPE = 0.2
EPS = 1e-5
MASKED = -1e30

UNIT = 1536
REGION = 9
RING = 2 * REGION
U_WN, U_WE, U_LAYER, U_Q, U_K, U_V, U_WO, U_C1, U_C2 = 0, 3, 9, 36, 39, 42, 45, 48, 51
U_G1, U_R1, U_G2, U_R2, U_END = 54, 58, 62, 66, 70
PRELUDE = 4


EDGE_CUTS = [0, EC // 2, EC]


def unit_index(u):
    return u if u < PRELUDE else u - (REGION - PRELUDE)


ROWS = [
    [("bn", D)] + [("b1", LAYERS * D), ("b2", LAYERS * D)] + [("bo", D), ("c2b", D)],
    [("bqkv", 3 * D), ("g1b", D3), ("g2b", D), ("r2b", D), ("ln2b", D)],
]
ROW_BASE = [0, 32]
ROW_LEN = [sum(n for _, n in g) for g in ROWS]
ROW_COLS = [n // P for n in ROW_LEN]
ROW_AT = {}
for _g, _rows in enumerate(ROWS):
    _at = 0
    for _name, _n in _rows:
        ROW_AT[_name] = (_g, _at)
        _at += _n

COL_BE, COL_C1B, COL_G1G, COL_G1B, COL_LNG = 0, KC, 2 * KC, 2 * KC + K3, 2 * KC + 2 * K3
COL_LNB = COL_LNG + LAYERS * KC
COL_R1B = COL_LNB + LAYERS * KC
COLS = COL_R1B + K3

ATT_AT = {"c1": (0, 2 * D), "c2": (2 * D, 2 * D), "g1": (4 * D, 2 * D3), "g2": (4 * D + 2 * D3, 2 * D)}
CONV = {"c1": 0, "c2": 1, "g1": 2, "g2": 3}
W_START, W_WEIGHTS, W_HOTS, W_NORM, W_PROB, W_BLOCK, W_B1 = 6, 4, 6, 6, 3, 8, 4
DST = 32
TERMS = {"c1": 1, "c2": 2}
GAIN2_AT = 6 * D + 2 * D3


def gnn_kernel(nc, x_in, src_in, dst_in, edge_in, stream_in, cols_in, rows_in, blk_in, blka_in, att_in, out):
    ctx = ExitStack()
    with ctx:
        def sb(name, shape, dt=F32):
            return ctx.enter_context(nc.sbuf_tensor(name, shape, dt))

        sems = {}

        def sem(name):
            if name not in sems:
                sems[name] = ctx.enter_context(nc.semaphore(name))
            return sems[name]

        ring = sb("ring", [P, RING * UNIT])
        row3 = sb("row3", [P, max(ROW_LEN)], BF16)
        ones3 = sb("ones3", [P, P], BF16)
        parts = sb("parts", [P, 3, sum(ROW_COLS)], BF16)
        cols = sb("cols", [P, COLS])
        lncol = sb("lncol", [P, 2 * KC])
        warm = sb("warm", [P, 512], BF16)
        ident = sb("ident", [P, P])
        identb = sb("identb", [P, P], BF16)
        onesf = sb("onesf", [P, P])
        edge_idx = sb("edge_idx", [P, 2 * EC], I32)
        edge_f = sb("edge_f", [P, 2 * EC])
        iota_i = sb("iota_i", [P, 2 * P], I32)
        cnt = sb("cnt", [P, P])
        cnt_self = sb("cnt_self", [P, P])
        cntT = sb("cntT", [P, P])
        mixT = sb("mixT", [P, P])
        mask1 = sb("mask1", [P, 4, P], BF16)
        mask2 = sb("mask2", [P, 4, P], BF16)
        deg = sb("deg", [P, 1])
        degB = sb("degB", [P, P])
        x = sb("x", [P, D])
        nodes = sb("nodes", [P, D])
        actT = sb("actT", [P, KC, P])
        hidT = sb("hidT", [P, K3, P])
        norm = sb("norm", [P, D3])
        edge_sum = norm[:, 0:DE]
        edge_sumT = norm[:, DE:2 * DE].rearrange("p (k n) -> p k n", k=2)
        h_nat = sb("h_nat", [P, D3])
        pair = sb("pair", [P, 2, D])
        aggT = pair[:, 0, :].rearrange("p (k n) -> p k n", k=KC)
        edge_term = pair[:, 1, :].rearrange("p (k n) -> p k n", k=KC)
        stats = sb("stats", [P, 12])
        mv = sb("mv", [P, 2])
        veps = sb("veps", [P, 1])
        mhalf = sb("mhalf", [P, 1])
        mrs = sb("mrs", [P, 1])
        rstd = sb("rstd", [P, 1])
        small = sb("small", [P, 64])
        bd = sb("bd", [P, 2 * P])
        blk = sb("blk", [P, 2 * O1])
        blka = sb("blka", [O1, 2 * O1 + 2 * H1])
        wlr = sb("wlr", [P, 2 * H1])

        RG = 2 * H1 * P + 4 * D + 4 * H0 * P - D
        region = sb("region", [P, RG])

        def part(at, n):
            return region[:, at:at + n]
        dst_hot = part(0, EC * P).rearrange("p (k n) -> p k n", k=EC)
        src_edge = part(EC * P, EC * (P + DE)).rearrange("p (k n) -> p k n", k=EC)
        TAIL = EC * (2 * P + DE)
        rows_f, rows_r = part(TAIL, sum(ROW_COLS)), part(TAIL + sum(ROW_COLS), sum(ROW_COLS))
        colf, maskf = part(TAIL + 2 * sum(ROW_COLS), P), part(TAIL + 2 * sum(ROW_COLS) + P, 2 * P)
        assert TAIL + 2 * sum(ROW_COLS) + 3 * P <= RG
        junk = [nodes[:, 0:HALF], nodes[:, HALF:D]]
        w_l = part(0, H1 * P).rearrange("p (h n) -> p h n", h=H1)
        w_r = part(H1 * P, H1 * P).rearrange("p (h n) -> p h n", h=H1)
        A0 = 2 * H1 * P
        q_nat, k_nat, v_nat = (part(A0 + i * D, D) for i in range(3))
        qT, kT, prob, probT = (part(A0 + 3 * D + i * H0 * P, H0 * P).rearrange("p (h n) -> p h n", h=H0)
                               for i in range(4))
        e12 = part(A0, H1 * P).rearrange("p (h n) -> p h n", h=H1)
        alphaT12 = part(A0 + H1 * P, H1 * P).rearrange("p (h n) -> p h n", h=H1)
        e4, diag4, alphaT4 = (part(i * 4 * P, 4 * P).rearrange("p (h n) -> p h n", h=4) for i in range(3))
        V0 = 12 * P
        att = {"c1": sb("att_c1", [P, 2 * D])[:, :], "c2": pair[:, :, :].rearrange("p a n -> p (a n)")[:, 0:2 * D],
               "g1": part(V0, 2 * D3), "g2": part(V0 + 2 * D3, 2 * D)}
        gain2 = part(V0 + 2 * D3 + 2 * D, D)
        assert V0 + 2 * D3 + 3 * D <= RG
        watt = {n: sb("watt_" + n, [P, KC, DST + 1]) for n in ("c1", "c2")}
        pair_l = sb("pair_l", [DST + 1, P])
        pair_r = sb("pair_r", [DST + 1, P])
        wpart = sb("wpart", [P, 2, 2, KC])

        bank = [ctx.enter_context(nc.psum_tensor(f"bank{i}", [P, 512], F32)) for i in range(8)]
        A, T, G = bank[0:4], bank[4:6], bank[6:8]
        NB = [G[0], G[1], A[0], A[1]]

        scratch = nc.dram_tensor("row_parts", [3, sum(ROW_LEN)], BF16).ap()
        block = ctx.enter_context(nc.Block())

        @block.sync
        def _(sp):
            def load(row, region_at, j):
                sp.dma_start(ring[:, bass.ds(region_at + j * UNIT, UNIT)],
                             stream_in[bass.ds(row, 1), :, :].rearrange("o p n -> (o p) n")
                             ).then_inc(sem(f"weights{j}_in"), 16)

            def load_edges(i):
                k = slice(EDGE_CUTS[i], EDGE_CUTS[i + 1])
                sp.dma_start(src_edge[:, k, P:P + DE], edge_in[:, k, :]).then_inc(sem(f"edges{i}_in"), 16)

            def load_vectors(name):
                at, n = ATT_AT[name]
                sp.dma_start(att[name], att_in[:, at:at + n].partition_broadcast(P)).then_inc(sem(name + "_att_in"), 16)

            sp.dma_start(x[:, :], x_in).then_inc(sem("x_in"), 16)
            sp.dma_start(edge_idx[:, EC:2 * EC], dst_in).then_inc(sem("dst_in"), 16)
            sp.dma_start(edge_idx[:, 0:EC], src_in).then_inc(sem("src_in"), 16)
            load(0, 0, 0)
            sp.dma_start(rows_f, rows_in).then_inc(sem("rows_in"), 16)
            load_edges(0)
            load(1, 0, 1)
            sp.wait_ge(sem("row_parts"), 1)
            at = col = 0
            for g in range(2):
                for j in range(3):
                    sp.dma_start(scratch[j, at:at + ROW_LEN[g]].rearrange("(p c) -> p c", c=ROW_COLS[g]),
                                 parts[:, j, col:col + ROW_COLS[g]]).then_inc(sem("row_scratch"), 16)
                at += ROW_LEN[g]
                col += ROW_COLS[g]
            load(2, 0, 2)
            load_edges(1)
            sp.wait_ge(sem("row_scratch"), 96)
            for g in range(2):
                sp.dma_start(row3[ROW_BASE[g]:ROW_BASE[g] + 3, 0:ROW_LEN[g]],
                             scratch[:, g * ROW_LEN[0]:g * ROW_LEN[0] + ROW_LEN[g]]).then_inc(sem("rows_ready"), 16)
            load(3, 0, 3)
            sp.dma_start(cols[:, :], cols_in).then_inc(sem("cols_in"), 16)
            sp.dma_start(blka[:, :], blka_in).then_inc(sem("blka_in"), 16)
            sp.dma_start(blk[:, :], blk_in).then_inc(sem("blk_in"), 16)
            for j in range(REGION):
                if j < PRELUDE:
                    sp.wait_ge(sem(f"weights{j}_in"), 16)
                load(PRELUDE + j, REGION * UNIT, j)
            load_vectors("c1")
            for j in range(REGION):
                if j < 3:
                    sp.wait_ge(sem("node_products"), 1 if j == 0 else 2)
                elif j == 3:
                    sp.wait_ge(sem("edge_proj"), 2)
                sp.wait_ge(sem(f"weights{j}_in"), 32 if j < PRELUDE else 16)
                load(PRELUDE + REGION + j, 0, j)
            with sp.Fori(0, LAYERS) as l:
                for j in range(REGION):
                    if j < 6:
                        sp.wait_ge(sem("hidden_proj"), 2 * l + 1 + j // 3)
                        sp.nop(nofuse=True)
                    else:
                        sp.wait_ge(sem("update_proj"), 2 * l + 1 + (1 if j > 6 else 0))
                        sp.nop(nofuse=True)
                    sp.wait_ge(sem(f"weights{j}_in"), 16 * l + (48 if j < PRELUDE else 32))
                    sp.nop(nofuse=True)
                    load(l * REGION + (PRELUDE + 2 * REGION + j), ((l + 1) % 2) * (REGION * UNIT), j)
            load_vectors("c2")
            for u in range(U_G1, U_END):
                j = u % REGION
                if u < U_G1 + REGION:
                    sp.wait_ge(sem(["q_proj", "k_proj", "v_proj"][j // 3]), 1 if j % 3 == 0 else 2)
                elif j < 3:
                    sp.wait_ge(sem("out_proj"), 1 if j % 3 == 0 else 2)
                elif j < 6:
                    sp.wait_ge(sem("c1_proj"), 1 if j % 3 == 0 else 2)
                    sp.wait_ge(sem("c1_watt"), 1)
                else:
                    sp.wait_ge(sem("c2_proj"), 1)
                    sp.wait_ge(sem("c2_watt"), 1)
                sp.wait_ge(sem(f"weights{j}_in"), 16 * (u // REGION - (0 if j < PRELUDE else 1)))
                load(unit_index(u), (u // REGION % 2) * REGION * UNIT, j)
                if u == U_G1 + REGION + 2:
                    sp.wait_ge(sem("b1_agg"), 2)
                    load_vectors("g1")
                    load_vectors("g2")
                    sp.dma_start(gain2, att_in[:, GAIN2_AT:GAIN2_AT + D].partition_broadcast(P)
                                 ).then_inc(sem("gain2_in"), 16)
            for i in range(2):
                sp.wait_ge(sem("out_ready"), i + 1)
                sp.dma_start(out[:, i * HALF:(i + 1) * HALF], norm[:, i * HALF:(i + 1) * HALF]
                             ).then_inc(sem("out_stored"), 16)
            sp.wait_ge(sem("out_stored"), 32)

        @block.gpsimd
        def _(pool):
            pool.memset(warm[:, :], 0.0).then_inc(sem("warm"), 1)
            pool.iota(iota_i[:, 0:P], [[1, P]], base=0, channel_multiplier=-1).then_inc(sem("iotas"), 1)
            pool.iota(iota_i[:, P:2 * P], [[1, P]], base=0, channel_multiplier=0).then_inc(sem("iotas"), 1)
            pool.memset(onesf[:, :], 1.0).then_inc(sem("constants"), 1)
            pool.memset(ones3[:, :], 1.0).then_inc(sem("constants"), 1)
            pool.memset(mhalf[:, :], -0.5).then_inc(sem("mhalf"), 1)
            pool.memset(bd[:, :], 0.0).then_inc(sem("bd_zero"), 1)
            pool.wait_ge(sem("mhalf"), 1)
            for n in ("c1", "c2"):
                pool.memset(watt[n][:, :, :], 0.0).then_inc(sem("rows_zero"), 1)
            for i, t in enumerate((pair_l, pair_r)):
                pool.memset(t[:, :], 0.0).then_inc(sem("rows_zero"), 1)
                pool.wait_ge(sem("rows_zero"), 3 + i)
                r = DST * i
                pool.memset(t[r:r + 1, :], 1.0).then_inc(sem("rows_one"), 1)
                pool.wait_ge(sem("rows_one"), i + 1)
            pool.wait_ge(sem("edge_sums"), 1)
            pool.memset(w_l, 0.0).then_inc(sem("w_zero"), 1)
            pool.memset(w_r, 0.0).then_inc(sem("w_zero"), 1)
            pool.wait_ge(sem("w_zero"), 2)
            pool.wait_ge(sem("wlr"), 1)
            for i, w in enumerate((w_l, w_r)):
                for q in range(2):
                    s = slice(q * O1, (q + 1) * O1)
                    pool.tensor_copy(w[s, q:H1:2, :],
                                     wlr[s, i * H1 + q:(i + 1) * H1:2].unsqueeze(2).broadcast_to([O1, H1 // 2, P])
                                     ).then_inc(sem("w_lr"), 1)
                    pool.wait_ge(sem("w_lr"), 2 * i + q + 1)
            with pool.Fori(0, LAYERS + 6) as n:
                pool.wait_ge(sem("ln_var"), n + 1)
                pool.tensor_tensor(rstd[:, :], veps[:, :], mhalf[:, :], ALU.pow).then_inc(sem("ln_rstd"), 1)

        @block.tensor
        def _(pe):
            def keep_warm(bank_, n):
                for _ in range(n):
                    pe.matmul(bank_[:, :], warm[:, 0:P], warm[:, :], start=True, stop=True)

            def arrived(u, j):
                pe.wait_ge(sem(f"weights{j}_in"), 16 * (u // REGION + (1 if j < PRELUDE else 0)))

            def add_row(dst, name, at, n, start=False, stop=True):
                g, off = ROW_AT[name]
                b = ROW_BASE[g]
                return pe.matmul(dst[:, 0:n], ones3[b:b + 3, :], row3[b:b + 3, bass.ds(at + off, n)],
                                 start=start, stop=stop)

            def products(u0, bank_, lhsT, chunks, half, w, ks, ready=None, stop=False):
                for k in ks:
                    b = (half * chunks + k) * w
                    u = u0 + b // UNIT
                    if b % UNIT == 0 or k == ks[0]:
                        arrived(u, u % REGION)
                    if ready is not None:
                        ready(k)
                    o = (u % RING) * UNIT + b % UNIT
                    mm = pe.matmul(bank_[:, 0:w], lhsT[:, k, :], ring[:, o:o + w],
                                   start=(k == 0), stop=(stop and k == chunks - 1))
                return mm

            def project(u0, banks, lhsT, chunks, done, row=None, at=0, more=None, w=HALF, ready=None):
                for half in range(2):
                    mm = products(u0, banks[half], lhsT, chunks, half, w, range(chunks),
                                  ready if half == 0 else None, stop=row is None)
                    if row is not None:
                        mm = add_row(banks[half], row, at + half * w, w)
                    mm.then_inc(sem(done), 1)
                    if more is not None:
                        more(half)

            def halves_of_actT(n):
                def ready(k):
                    if k % HC == 0:
                        pe.wait_ge(sem("actT"), n + k // HC)
                return ready

            def transposes(src, banks, done, per=HC, n=KC):
                for c in range(n):
                    mm = pe.transpose(banks[c // per][:, (c % per) * P:(c % per + 1) * P],
                                      src[:, c * P:(c + 1) * P], ident[:, :])
                    if c % per == per - 1:
                        mm.then_inc(sem(done), 1)

            def edge_sums(i):
                pe.wait_ge(sem(f"edges{i}_in"), 16)
                for k in range(EDGE_CUTS[i], EDGE_CUTS[i + 1]):
                    mm = pe.matmul(G[0][:, 0:P + DE], dst_hot[:, k, :], src_edge[:, k, :],
                                   start=(k == 0), stop=(k == EC - 1))
                return mm

            pe.wait_ge(sem("warm"), 1)
            keep_warm(A[3], W_START)
            pe.wait_ge(sem("x_in"), 16)
            pe.wait_ge(sem("ident"), 1)
            transposes(x, T, "actT_psum")
            keep_warm(A[3], W_WEIGHTS)
            products(U_WN, A[0], actT, KC, 0, HALF, range(4), halves_of_actT(1))
            keep_warm(A[3], W_HOTS)
            pe.wait_ge(sem("one_hots"), 2)
            edge_sums(0)
            products(U_WN, A[0], actT, KC, 0, HALF, range(4, KC)).then_inc(sem("node_products"), 1)
            products(U_WN, A[1], actT, KC, 1, HALF, range(KC)).then_inc(sem("node_products"), 1)
            pe.wait_ge(sem("constants"), 2)
            edge_sums(1).then_inc(sem("edge_sums"), 1)
            pe.wait_ge(sem("rows_ready"), 32)
            for half in range(2):
                add_row(A[half], "bn", half * HALF, HALF).then_inc(sem("node_proj"), 1)
            pe.wait_ge(sem("cnt"), 1)
            pe.transpose(T[0][:, 0:P], cnt[:, :], ident[:, :]).then_inc(sem("graph_T"), 1)
            pe.wait_ge(sem("edge_sum"), 1)
            pe.transpose(T[1][:, 0:P], edge_sum[:, 0:P], ident[:, :])
            pe.transpose(T[1][:, P:2 * P], edge_sum[:, P:2 * P], ident[:, :]).then_inc(sem("graph_T"), 1)
            pe.wait_ge(sem("cntT"), 1)
            pe.wait_ge(sem("nodes"), 2)
            pe.matmul(A[0][:, 0:P], onesf[:, :], cntT[:, :], start=True, stop=True).then_inc(sem("deg_rows"), 1)
            pe.wait_ge(sem("edge_sumT"), 1)
            arrived(U_WE, U_WE)
            for c in range(KC):
                for k in range(2):
                    o = U_WE * UNIT + k * D + c * P
                    mm = pe.matmul(A[2 + c // HC][:, (c % HC) * P:(c % HC + 1) * P], ring[:, o:o + P],
                                   edge_sumT[:, k, :], start=(k == 0), stop=(k == 1))
                if c % HC == HC - 1:
                    mm.then_inc(sem("edge_proj"), 1)
            pe.wait_ge(sem("blka_in"), 16)
            pe.matmul(A[1][:, 0:2 * H1], blka[:, 0:P], blka[:, P:P + 2 * H1], start=True, stop=True
                      ).then_inc(sem("wlr_psum"), 1)
            pe.wait_ge(sem("mixT"), 1)
            pe.wait_ge(sem("degB"), 1)
            pe.wait_ge(sem("wlr"), 1)
            with pe.Fori(0, LAYERS) as l:
                base = ((l + 1) % 2) * (REGION * UNIT)

                def layer_unit(j):
                    pe.wait_ge(sem(f"weights{j}_in"), 16 * l + (32 if j < PRELUDE else 16))

                for half in range(2):
                    pe.wait_ge(sem("nodes"), 2 * l + half + 1)
                    for c in range(HC):
                        cc = half * HC + c
                        mm = pe.transpose(T[half][:, c * P:(c + 1) * P], nodes[:, cc * P:(cc + 1) * P], ident[:, :])
                    mm.then_inc(sem("actT_psum"), 1)
                    for c in range(HC):
                        cc = half * HC + c
                        mm = pe.matmul(G[half][:, c * P:(c + 1) * P], nodes[:, cc * P:(cc + 1) * P], mixT[:, :],
                                       start=True, stop=True)
                    mm.then_inc(sem("agg_psum"), 1)
                for half in range(2):
                    for k in range(2 * KC):
                        if k == 0 or k == HC:
                            pe.wait_ge(sem("actT"), 2 * l + 3 + k // HC)
                        if k == KC or k == KC + HC:
                            pe.wait_ge(sem("aggT"), 2 * l + 1 + (k - KC) // HC)
                        b = (half * 2 * KC + k) * HALF
                        if b % UNIT == 0:
                            layer_unit(b // UNIT)
                        lhsT = actT[:, k, :] if k < KC else aggT[:, k - KC, :]
                        pe.matmul(A[half][:, 0:HALF], lhsT, ring[:, bass.ds(base + b, HALF)],
                                  start=(k == 0), stop=False)
                    add_row(A[half], "b1", l * D + half * HALF, HALF).then_inc(sem("hidden_proj"), 1)
                keep_warm(A[2], W_NORM)
                for c in range(KC):
                    if c < 2:
                        pe.wait_ge(sem("hidden_norm_a"), 2 * l + c + 1)
                    if c == HC:
                        pe.wait_ge(sem("hidden_norm_b"), l + 1)
                    pe.transpose(T[c // HC][:, (c % HC) * P:(c % HC + 1) * P], norm[:, c * P:(c + 1) * P],
                                 ident[:, :]).then_inc(sem("hidT_psum"), 1)
                for half in range(2):
                    for k in range(KC):
                        if half == 0 and k < HC:
                            pe.wait_ge(sem("hidT_a"), HC * l + k + 1)
                        if half == 0 and k == HC:
                            pe.wait_ge(sem("hidT_b"), l + 1)
                        b = 6 * UNIT + (half * KC + k) * HALF
                        if b % UNIT == 0:
                            layer_unit(b // UNIT)
                        pe.matmul(A[2 + half][:, 0:HALF], hidT[:, k, :], ring[:, bass.ds(base + b, HALF)],
                                  start=(k == 0), stop=False)
                    add_row(A[2 + half], "b2", l * D + half * HALF, HALF).then_inc(sem("update_proj"), 1)

            for half in range(2):
                pe.wait_ge(sem("nodes"), 2 * LAYERS + half + 1)
                for c in range(HC):
                    cc = half * HC + c
                    mm = pe.transpose(T[half][:, c * P:(c + 1) * P], nodes[:, cc * P:(cc + 1) * P], ident[:, :])
                mm.then_inc(sem("actT_psum"), 1)
            project(U_Q, A[0:2], actT, KC, "q_proj", "bqkv", 0, ready=halves_of_actT(2 * LAYERS + 3))
            project(U_K, A[2:4], actT, KC, "k_proj", "bqkv", D)

            def head_transposes(src, banks, done):
                for h in range(H0):
                    mm = pe.transpose(banks[h // 4][0:DH, (h % 4) * P:(h % 4 + 1) * P],
                                      src[:, h * DH:(h + 1) * DH], ident[:, :])
                    if h % 4 == 3:
                        mm.then_inc(sem(done), 1)

            def between(half):
                if half == 0:
                    pe.wait_ge(sem("q_nat"), 2)
                    head_transposes(q_nat, T, "qT_psum")
                    pe.wait_ge(sem("k_nat"), 2)
                    head_transposes(k_nat, A[0:2], "kT_psum")
            project(U_V, G, actT, KC, "v_proj", "bqkv", 2 * D, more=between)
            for b in range(2):
                pe.wait_ge(sem("qT"), b + 1)
                pe.wait_ge(sem("kT"), b + 1)
                for h in range(4 * b, 4 * b + 4):
                    mm = pe.matmul(A[2 + b][:, (h % 4) * P:(h % 4 + 1) * P], qT[0:DH, h, :], kT[0:DH, h, :],
                                   start=True, stop=True)
                mm.then_inc(sem("scores"), 1)
            pe.wait_ge(sem("v_nat"), 2)
            for b in range(2):
                keep_warm(G[0], W_PROB)
                pe.wait_ge(sem("prob"), b + 1)
                for h in range(4 * b, 4 * b + 4):
                    mm = pe.transpose(T[b][:, (h % 4) * P:(h % 4 + 1) * P], prob[:, h, :], ident[:, :])
                mm.then_inc(sem("probT_psum"), 1)
            for b in range(2):
                pe.wait_ge(sem("probT"), b + 1)
                for h in range(4 * b, 4 * b + 4):
                    mm = pe.matmul(A[b][:, (h % 4) * DH:(h % 4 + 1) * DH], probT[:, h, :],
                                   v_nat[:, h * DH:(h + 1) * DH], start=True, stop=True)
                mm.then_inc(sem("attn_psum"), 1)
            for half in range(2):
                pe.wait_ge(sem("attended"), half + 1)
                for c in range(HC):
                    cc = half * HC + c
                    mm = pe.transpose(G[half][:, c * P:(c + 1) * P], norm[:, cc * P:(cc + 1) * P], ident[:, :])
                mm.then_inc(sem("attnT_psum"), 1)
            project(U_WO, A[2:4], hidT, KC, "out_proj", "bo", 0,
                    ready=lambda k: pe.wait_ge(sem("attnT"), k // HC + 1) if k % HC == 0 else None)

            def x_transposes(n):
                keep_warm(G[0], W_BLOCK)
                for half in range(2):
                    pe.wait_ge(sem("x_ready"), 2 * n + half + 1)
                    for c in range(HC):
                        cc = half * HC + c
                        mm = pe.transpose(T[half][:, c * P:(c + 1) * P], x[:, cc * P:(cc + 1) * P], ident[:, :])
                    mm.then_inc(sem("actT_psum"), 1)

            x_transposes(0)
            pe.wait_ge(sem("actT"), 2 * LAYERS + 6)
            pe.wait_ge(sem("bd"), 4)
            pe.wait_ge(sem("masks"), 2)
            pe.wait_ge(sem("w_lr"), 4)
            EB = [G[0], G[1], T[0]]
            for b in range(3):
                pe.matmul(EB[b][:, :], identb[:, :], mask1[:, :, :].rearrange("p h n -> p (h n)"),
                          start=True, stop=True)
                for h in range(4 * b, 4 * b + 4):
                    o = EB[b][:, (h % 4) * P:(h % 4 + 1) * P]
                    pe.matmul(o, w_l[:, h, :], actT[:, h // 2, :], start=False, stop=True, skip_group_check=True)
                    mm = pe.matmul(o, actT[:, h // 2, :], w_r[:, h, :], start=False, stop=True,
                                   skip_group_check=True)
                mm.then_inc(sem("b1_logits"), 1)
            for c in range(KC):
                mm = pe.matmul(A[c // HC][:, (c % HC) * P:(c % HC + 1) * P], actT[:, c, :], bd[:, 0:P],
                               start=True, stop=True)
                if c % HC == HC - 1:
                    mm.then_inc(sem("ft_psum"), 1)
            for c in range(KC):
                pe.matmul(A[2 + c // HC][:, (c % HC) * P:(c % HC + 1) * P], actT[:, c, :], bd[:, P:2 * P],
                          start=(c % HC == 0), stop=True, skip_group_check=True)
            keep_warm(T[1], W_B1)
            pe.wait_ge(sem("ft"), 2)
            AB = [A[0], A[1], T[1]]
            for b in range(3):
                if b > 0:
                    keep_warm(T[1] if b == 1 else G[0], W_B1)
                pe.wait_ge(sem("b1_alpha"), b + 1)
                for h in range(4 * b, 4 * b + 4):
                    mm = pe.transpose(AB[b][:, (h % 4) * P:(h % 4 + 1) * P], e12[:, h, :], ident[:, :])
                mm.then_inc(sem("b1_alphaT_psum"), 1)
            for h in range(H1):
                if h % 4 == 0:
                    pe.wait_ge(sem("b1_alphaT"), h // 4 + 1)
                mm = pe.matmul(A[2 + h // 6][:, (h % 6) * O1:(h % 6 + 1) * O1], alphaT12[:, h, :],
                               h_nat[:, h * O1:(h + 1) * O1], start=False, stop=True, skip_group_check=True)
                if h % 6 == 5:
                    mm.then_inc(sem("b1_agg"), 1)

            def terms(lhsT, name):
                pe.wait_ge(sem(name + "_watt"), 1)
                for k in range(KC):
                    mm = pe.matmul(G[1][0:DST + 1, 0:P], watt[name][:, k, :], lhsT[:, k, :],
                                   start=(k == 0), stop=(k == KC - 1))
                mm.then_inc(sem("conv_terms"), 1)

            def logits(eb, heads, name):
                pe.matmul(eb[:, 0:heads * P], identb[:, :], mask2[:, 0:heads, :].rearrange("p h n -> p (h n)"),
                          start=True, stop=False)
                pe.wait_ge(sem("conv_diag"), CONV[name] + 1)
                if name in watt:
                    mm = pe.matmul(eb[:, 0:P], pair_l[:, :], pair_r[:, :], start=False, stop=True)
                else:
                    mm = pe.matmul(eb[:, 0:heads * P], onesf[:, :],
                                   diag4[:, 0:heads, :].rearrange("p h n -> p (h n)"), start=False, stop=True)
                mm.then_inc(sem("conv_logits"), 1)

            def alpha_transposes(ab, heads, name):
                pe.wait_ge(sem("conv_alpha"), CONV[name] + 1)
                for h in range(heads):
                    mm = pe.transpose(ab[:, h * P:(h + 1) * P], e4[:, h, :], ident[:, :])
                mm.then_inc(sem("conv_alphaT_psum"), 1)

            def convolve(u0, banks, lhsT, name):
                products(u0, banks[0], lhsT, KC, 0, HALF, range(KC), stop=True).then_inc(sem(name + "_proj"), 1)
                logits(G[0], 1, name)
                products(u0, banks[1], lhsT, KC, 1, HALF, range(KC - 1))
                alpha_transposes(G[1], 1, name)
                products(u0, banks[1], lhsT, KC, 1, HALF, [KC - 1], stop=True).then_inc(sem(name + "_proj"), 1)
                pe.wait_ge(sem("conv_alphaT"), CONV[name] + 1)

            x_transposes(1)
            pe.wait_ge(sem("actT"), 2 * LAYERS + 8)
            terms(actT, "c1")
            convolve(U_C1, A[0:2], actT, "c1")
            for c in range(KC):
                if c % HC == 0:
                    pe.wait_ge(sem("conv_h"), 2 * CONV["c1"] + c // HC + 1)
                pe.matmul(T[c // HC][:, (c % HC) * P:(c % HC + 1) * P], h_nat[:, c * P:(c + 1) * P],
                          alphaT4[:, 0, :], start=True, stop=True).then_inc(sem("c1_agg"), 1)

            def c1_out(k):
                pe.wait_ge(sem("c1_outT_a" if k < HC else "c1_outT_b"), k % HC + 1)
            for k in range(KC):
                c1_out(k)
            terms(hidT, "c2")
            convolve(U_C2, A[2:4], hidT, "c2")
            for half in range(2):
                pe.wait_ge(sem("conv_h"), 2 * CONV["c2"] + half + 1)
                pe.matmul(A[half][:, 0:HALF], alphaT4[:, 0, :], h_nat[:, half * HALF:(half + 1) * HALF],
                          start=True, stop=False)
                add_row(A[half], "c2b", half * HALF, HALF).then_inc(sem("c2_agg"), 1)

            x_transposes(2)
            pe.wait_ge(sem("actT"), 2 * LAYERS + 10)
            project(U_G1, A[0:2], actT, KC, "g1_proj", w=512)

            def residual(cs):
                for c in cs:
                    for k in range(KC):
                        b = (c // 4 * KC + k) * 512
                        if c % 4 == 0 and b % UNIT == 0:
                            arrived(U_R1 + b // UNIT, (U_R1 + b // UNIT) % REGION)
                        o = (U_R1 % RING) * UNIT + b + c % 4 * P
                        mm = pe.matmul(A[2 + c // 4][:, (c % 4) * P:(c % 4 + 1) * P], ring[:, o:o + P],
                                       actT[:, k, :], start=(k == 0), stop=(k == KC - 1))
                    if c % 4 == 3:
                        mm.then_inc(sem("r1_proj"), 1)

            residual(range(2))
            logits(G[0], H3, "g1")
            residual(range(2, 7))
            alpha_transposes(G[1], H3, "g1")
            residual([7])
            pe.wait_ge(sem("conv_alphaT"), CONV["g1"] + 1)
            for half in range(2):
                add_row(T[half], "g1b", half * 512, 512, start=True)
                pe.wait_ge(sem("conv_h"), 2 * CONV["g1"] + half + 1)
                for h in (2 * half, 2 * half + 1):
                    mm = pe.matmul(T[half][:, (h % 2) * O3:(h % 2 + 1) * O3], alphaT4[:, h, :],
                                   h_nat[:, h * O3:(h + 1) * O3], start=False, stop=True, skip_group_check=True)
                mm.then_inc(sem("g1_agg"), 1)
            keep_warm(A[0], W_NORM)
            for c in range(K3):
                if c % 4 == 0:
                    pe.wait_ge(sem("g1_norm"), c // 4 + 1)
                mm = pe.transpose(NB[c // 2][:, (c % 2) * P:(c % 2 + 1) * P], norm[:, c * P:(c + 1) * P],
                                  ident[:, :])
                if c % 2 == 1:
                    mm.then_inc(sem("g1_normT_psum"), 1)
            project(U_G2, T, hidT, K3, "g2_proj", ready=lambda k: pe.wait_ge(sem("g1_outT"), k + 1))

            products(U_R2, A[2], hidT, K3, 0, HALF, range(4))
            logits(G[0], 1, "g2")
            products(U_R2, A[2], hidT, K3, 0, HALF, range(4, K3))
            add_row(A[2], "r2b", 0, HALF, stop=False)
            add_row(A[2], "ln2b", 0, HALF).then_inc(sem("r2_proj"), 1)
            products(U_R2, A[3], hidT, K3, 1, HALF, range(2))
            alpha_transposes(G[1], 1, "g2")
            products(U_R2, A[3], hidT, K3, 1, HALF, range(2, 3))
            pe.wait_ge(sem("conv_alphaT"), CONV["g2"] + 1)
            for i in range(2):
                pe.wait_ge(sem("conv_h"), 2 * CONV["g2"] + i + 1)
                pe.matmul(A[i][:, 0:HALF], alphaT4[:, 0, :], h_nat[:, i * HALF:(i + 1) * HALF],
                          start=True, stop=False)
                add_row(A[i], "g2b", i * HALF, HALF).then_inc(sem("g2_agg"), 1)
            products(U_R2, A[3], hidT, K3, 1, HALF, range(3, K3))
            add_row(A[3], "r2b", HALF, HALF, stop=False)
            add_row(A[3], "ln2b", HALF, HALF).then_inc(sem("r2_proj"), 1)

        @block.scalar
        def _(act):
            def copy_actT(n):
                for half in range(2):
                    act.wait_ge(sem("actT_psum"), n + half + 1)
                    act.copy(actT[:, half * HC:(half + 1) * HC, :].rearrange("p k n -> p (k n)"),
                             T[half][:, 0:HALF]).then_inc(sem("actT"), 1)

            copy_actT(0)
            act.wait_ge(sem("cnt"), 1)
            act.copy(edge_sum[:, :], G[0][:, P:P + DE]).then_inc(sem("edge_sum"), 1)
            act.wait_ge(sem("graph_T"), 2)
            act.copy(edge_sumT[:, :, :].rearrange("p k n -> p (k n)"), T[1][:, 0:2 * P]
                     ).then_inc(sem("edge_sumT"), 1)
            act.wait_ge(sem("deg_rows"), 1)
            act.copy(degB[:, :], A[0][:, 0:P]).then_inc(sem("degB"), 1)
            act.wait_ge(sem("wlr_psum"), 1)
            act.copy(wlr[:, :], A[1][:, 0:2 * H1]).then_inc(sem("wlr"), 1)
            with act.Fori(0, LAYERS) as l:
                for half in range(2):
                    act.wait_ge(sem("actT_psum"), 2 * l + 3 + half)
                    act.copy(actT[:, half * HC:(half + 1) * HC, :].rearrange("p k n -> p (k n)"),
                             T[half][:, 0:HALF]).then_inc(sem("actT"), 1)
                act.wait_ge(sem("ln_shift"), l + 1)
                act.activation(norm[:, HALF:D], A[1][:, 0:HALF], ACT.Identity, bias=mrs[:, 0:1],
                               scale=rstd[:, 0:1]).then_inc(sem("hidden_norm_b"), 1)
                act.wait_ge(sem("lncol"), 2 * l + 2)
                for c in range(HC):
                    act.wait_ge(sem("hidT_psum"), KC * l + HC)
                    act.activation(hidT[:, c, :], T[0][:, c * P:(c + 1) * P], ACT.Relu,
                                   bias=lncol[:, KC + c:KC + c + 1], scale=lncol[:, c:c + 1]
                                   ).then_inc(sem("hidT_a"), 1)

            copy_actT(2 * LAYERS + 2)
            for half in range(2):
                act.wait_ge(sem("k_proj"), half + 1)
                act.copy(k_nat[:, half * HALF:(half + 1) * HALF], A[2 + half][:, 0:HALF]).then_inc(sem("k_nat"), 1)
            for b in range(2):
                act.wait_ge(sem("qT_psum"), b + 1)
                act.copy(qT[0:DH, 4 * b:4 * b + 4, :].rearrange("p h n -> p (h n)"), T[b][0:DH, :]
                         ).then_inc(sem("qT"), 1)
            for half in range(2):
                act.wait_ge(sem("v_proj"), half + 1)
                act.copy(v_nat[:, half * HALF:(half + 1) * HALF], G[half][:, 0:HALF]).then_inc(sem("v_nat"), 1)
            for b in range(2):
                act.wait_ge(sem("score_shift"), b + 1)
                pb = prob[:, 4 * b:4 * b + 4, :].rearrange("p h n -> p (h n)")
                act.activation(pb, pb, ACT.Exp).then_inc(sem("prob"), 1)
            act.wait_ge(sem("probT_psum"), 1)
            act.copy(probT[:, 0:4, :].rearrange("p h n -> p (h n)"), T[0][:, :]).then_inc(sem("probT"), 1)
            act.wait_ge(sem("probT_psum"), 2)
            act.copy(probT[:, 4:8, :].rearrange("p h n -> p (h n)"), T[1][:, :]).then_inc(sem("probT"), 1)
            for half in range(2):
                act.wait_ge(sem("attnT_psum"), half + 1)
                act.copy(hidT[:, half * HC:(half + 1) * HC, :].rearrange("p k n -> p (k n)"), G[half][:, 0:HALF]
                         ).then_inc(sem("attnT"), 1)

            copy_actT(2 * LAYERS + 4)
            EB = [G[0], G[1], T[0]]
            for b in range(3):
                act.wait_ge(sem("b1_logits"), b + 1)
                act.activation(e12[:, 4 * b:4 * b + 4, :].rearrange("p h n -> p (h n)"), EB[b][:, :],
                               ACT.Copy).then_inc(sem("b1_raw"), 1)
            for b in range(3):
                act.wait_ge(sem("b1_max"), b + 1)
                for h in range(4 * b, 4 * b + 4):
                    ins = act.activation(e12[:, h, :], e12[:, h, :], ACT.Exp, bias=small[:, 16 + h:17 + h])
                ins.then_inc(sem("b1_exp"), 1)
                if b < 2:
                    act.wait_ge(sem("ft_psum"), b + 1)
                    act.copy(h_nat[:, b * HALF:(b + 1) * HALF], A[b][:, 0:HALF]).then_inc(sem("ft"), 1)
            AB = [A[0], A[1], T[1]]
            for b in range(3):
                act.wait_ge(sem("b1_alphaT_psum"), b + 1)
                act.copy(alphaT12[:, 4 * b:4 * b + 4, :].rearrange("p h n -> p (h n)"), AB[b][:, :]
                         ).then_inc(sem("b1_alphaT"), 1)

            def copy_h(banks, w, half, name):
                act.wait_ge(sem(name + "_proj"), half + 1)
                act.copy(h_nat[:, half * w:(half + 1) * w], banks[half][:, 0:w]).then_inc(sem("conv_h"), 1)

            def raw_logits(heads, name):
                act.wait_ge(sem("conv_logits"), CONV[name] + 1)
                for h in range(heads):
                    if name in watt:
                        ins = act.copy(e4[:, h, :], G[0][:, h * P:(h + 1) * P])
                    else:
                        ins = act.activation(e4[:, h, :], G[0][:, h * P:(h + 1) * P], ACT.Identity,
                                             bias=small[:, heads + h:heads + h + 1])
                ins.then_inc(sem("conv_raw"), 1)

            def exponentials(heads, name):
                act.wait_ge(sem("conv_max"), CONV[name] + 1)
                for h in range(heads):
                    ins = act.activation(e4[:, h, :], e4[:, h, :], ACT.Exp, bias=small[:, 8 + h:9 + h])
                ins.then_inc(sem("conv_exp"), 1)

            def copy_alphaT(heads, name):
                act.wait_ge(sem("conv_alphaT_psum"), CONV[name] + 1)
                act.copy(alphaT4[:, 0:heads, :].rearrange("p h n -> p (h n)"), G[1][:, 0:heads * P]
                         ).then_inc(sem("conv_alphaT"), 1)

            copy_actT(2 * LAYERS + 6)
            copy_h(A[0:2], HALF, 0, "c1")
            raw_logits(1, "c1")
            exponentials(1, "c1")
            copy_alphaT(1, "c1")
            copy_h(A[0:2], HALF, 1, "c1")
            for c in range(HC):
                act.wait_ge(sem("c1_agg"), HC)
                act.activation(hidT[:, c, :], T[0][:, c * P:(c + 1) * P], ACT.Relu,
                               bias=cols[:, COL_C1B + c:COL_C1B + c + 1]).then_inc(sem("c1_outT_a"), 1)
            copy_h(A[2:4], HALF, 0, "c2")
            raw_logits(1, "c2")
            exponentials(1, "c2")
            copy_alphaT(1, "c2")
            copy_h(A[2:4], HALF, 1, "c2")

            copy_actT(2 * LAYERS + 8)
            copy_h(A[0:2], 512, 0, "g1")
            copy_h(A[0:2], 512, 1, "g1")
            raw_logits(H3, "g1")
            exponentials(H3, "g1")
            copy_alphaT(H3, "g1")
            for c in range(K3):
                if c % 2 == 0:
                    act.wait_ge(sem("g1_normT_psum"), c // 2 + 1)
                act.activation(hidT[:, c, :], NB[c // 2][:, (c % 2) * P:(c % 2 + 1) * P], ACT.Relu,
                               bias=cols[:, COL_G1B + c:COL_G1B + c + 1],
                               scale=cols[:, COL_G1G + c:COL_G1G + c + 1]).then_inc(sem("g1_relu"), 1)
            copy_h(T, HALF, 0, "g2")
            copy_h(T, HALF, 1, "g2")
            raw_logits(1, "g2")
            exponentials(1, "g2")
            copy_alphaT(1, "g2")

        @block.vector
        def _(v):
            done = [0]

            def step(ins):
                done[0] = done[0] + 1
                ins.then_inc(sem("vector_step"), 1)
                v.wait_ge(sem("vector_step"), done[0])

            v.wait_ge(sem("iotas"), 2)
            v.tensor_scalar(ident[:, :], iota_i[:, 0:P], 0.0, None, ALU.is_equal).then_inc(sem("ident"), 1)
            step(v.tensor_copy(colf[:, :], iota_i[:, P:2 * P]))
            v.wait_ge(sem("rows_in"), 16)
            step(v.tensor_copy(parts[:, 0, :], rows_f[:, :]))
            step(v.tensor_tensor(rows_r[:, :], rows_f[:, :], parts[:, 0, :], ALU.subtract))
            step(v.tensor_copy(parts[:, 1, :], rows_r[:, :]))
            step(v.tensor_tensor(rows_f[:, :], rows_r[:, :], parts[:, 1, :], ALU.subtract))
            v.tensor_copy(parts[:, 2, :], rows_f[:, :]).then_inc(sem("row_parts"), 1)
            v.wait_ge(sem("src_in"), 16)
            v.wait_ge(sem("dst_in"), 16)
            step(v.tensor_copy(edge_f[:, :], edge_idx[:, :]))
            cb = colf[:, :].unsqueeze(1).broadcast_to([P, EC, P])
            v.tensor_tensor(dst_hot, edge_f[:, EC:2 * EC].unsqueeze(2).broadcast_to([P, EC, P]), cb,
                            ALU.is_equal).then_inc(sem("one_hots"), 1)
            v.tensor_tensor(src_edge[:, :, 0:P], edge_f[:, 0:EC].unsqueeze(2).broadcast_to([P, EC, P]), cb,
                            ALU.is_equal).then_inc(sem("one_hots"), 1)
            v.wait_ge(sem("ident"), 1)
            v.tensor_copy(identb[:, :], ident[:, :]).then_inc(sem("identb"), 1)
            v.wait_ge(sem("blk_in"), 16)
            v.wait_ge(sem("bd_zero"), 1)
            for i in range(2):
                for q in range(2):
                    v.tensor_copy(bd[q * O1:(q + 1) * O1, i * P + q * O1:i * P + (q + 1) * O1],
                                  blk[q * O1:(q + 1) * O1, i * O1:(i + 1) * O1]).then_inc(sem("bd"), 1)
            for half in range(2):
                v.wait_ge(sem("node_proj"), half + 1)
                v.tensor_copy(nodes[:, half * HALF:(half + 1) * HALF], A[half][:, 0:HALF]).then_inc(sem("nodes"), 1)
            v.wait_ge(sem("edge_sums"), 1)
            v.tensor_copy(cnt[:, :], G[0][:, 0:P]).then_inc(sem("cnt"), 1)
            v.wait_ge(sem("cnt"), 1)
            step(v.tensor_reduce(deg[:, :], cnt[:, :], AX.X, ALU.add))
            v.wait_ge(sem("graph_T"), 1)
            v.tensor_copy(cntT[:, :], T[0][:, 0:P]).then_inc(sem("cntT"), 1)
            v.wait_ge(sem("cntT"), 1)
            v.scalar_tensor_tensor(mixT[:, :], ident[:, :], deg[:, 0:1], cntT[:, :], ALU.mult, ALU.add
                                   ).then_inc(sem("mixT"), 1)
            v.wait_ge(sem("cols_in"), 16)
            v.wait_ge(sem("degB"), 1)
            for c in range(KC):
                if c % HC == 0:
                    v.wait_ge(sem("edge_proj"), c // HC + 1)
                ins = v.scalar_tensor_tensor(edge_term[:, c, :], degB[:, :], cols[:, COL_BE + c:COL_BE + c + 1],
                                             A[2 + c // HC][:, (c % HC) * P:(c % HC + 1) * P], ALU.mult, ALU.add)
            ins.then_inc(sem("edge_term"), 1)
            v.wait_ge(sem("edge_term"), 1)
            step(v.tensor_tensor(cnt_self[:, :], cnt[:, :], ident[:, :], ALU.add))
            step(v.tensor_scalar(maskf[:, 0:P], cnt[:, :], 0.5, MASKED, ALU.is_lt, ALU.mult))
            step(v.tensor_scalar(maskf[:, P:2 * P], cnt_self[:, :], 0.5, MASKED, ALU.is_lt, ALU.mult))
            for i, m in enumerate((mask1, mask2)):
                v.tensor_copy(m[:, :, :], maskf[:, i * P:(i + 1) * P].unsqueeze(1).broadcast_to([P, 4, P])
                              ).then_inc(sem("masks"), 1)

            def row_stats(n):
                step(v.bn_aggr(mv[:, :], stats[:, :]))
                v.tensor_scalar(veps[:, :], mv[:, 1:2], EPS, None, ALU.add).then_inc(sem("ln_var"), 1)
                v.wait_ge(sem("ln_rstd"), n + 1)

            def normalise(dst, src):
                return v.tensor_scalar(dst, src, mv[:, 0:1], rstd[:, 0:1], ALU.subtract, ALU.mult)

            def leaky(e):
                return v.scalar_tensor_tensor(e, e, SLOPE, e, ALU.mult, ALU.max)

            LINKS = 4
            at = done[0]
            with v.Fori(0, LAYERS) as l:
                done[0] = l * LINKS + at
                v.tensor_copy(lncol[:, 0:KC], cols[:, bass.ds(l * KC + COL_LNG, KC)]).then_inc(sem("lncol"), 1)
                v.tensor_copy(lncol[:, KC:2 * KC], cols[:, bass.ds(l * KC + COL_LNB, KC)]).then_inc(sem("lncol"), 1)
                for half in range(2):
                    v.wait_ge(sem("agg_psum"), 2 * l + half + 1)
                    ins = v.tensor_tensor(aggT[:, half * HC:(half + 1) * HC, :].rearrange("p k n -> p (k n)"),
                                          G[half][:, 0:HALF],
                                          edge_term[:, half * HC:(half + 1) * HC, :].rearrange("p k n -> p (k n)"),
                                          ALU.add).then_inc(sem("aggT"), 1)
                for half in range(2):
                    v.wait_ge(sem("hidden_proj"), 2 * l + half + 1)
                    step(v.bn_stats(stats[:, 6 * half:6 * half + 6], A[half][:, 0:HALF]))
                v.nop(nofuse=True)
                step(v.bn_aggr(mv[:, :], stats[:, :]))
                v.tensor_scalar(veps[:, :], mv[:, 1:2], EPS, None, ALU.add).then_inc(sem("ln_var"), 1)
                v.wait_ge(sem("ln_rstd"), l + 1)
                v.tensor_scalar(mrs[:, :], mv[:, 0:1], rstd[:, 0:1], -1.0, ALU.mult, ALU.mult
                                ).then_inc(sem("ln_shift"), 1)
                normalise(norm[:, 0:P], A[0][:, 0:P]).then_inc(sem("hidden_norm_a"), 1)
                normalise(norm[:, P:HALF], A[0][:, P:HALF]).then_inc(sem("hidden_norm_a"), 1)
                v.wait_ge(sem("hidT_psum"), KC * l + KC)
                v.wait_ge(sem("lncol"), 2 * l + 2)
                for c in range(HC):
                    cc = HC + c
                    ins = v.tensor_scalar(hidT[:, cc, :], T[1][:, c * P:(c + 1) * P], lncol[:, cc:cc + 1],
                                          lncol[:, KC + cc:KC + cc + 1], ALU.mult, ALU.add)
                step(ins)
                hb = hidT[:, HC:2 * HC, :].rearrange("p k n -> p (k n)")
                v.tensor_scalar(hb, hb, 0.0, None, ALU.max).then_inc(sem("hidT_b"), 1)
                for half in range(2):
                    v.wait_ge(sem("update_proj"), 2 * l + half + 1)
                    nh = nodes[:, half * HALF:(half + 1) * HALF]
                    v.tensor_tensor(nh, A[2 + half][:, 0:HALF], nh, ALU.add).then_inc(sem("nodes"), 1)
            done[0] = at + LAYERS * LINKS

            weighed = [0]

            def junk_of_two():
                if weighed[0] >= 2:
                    v.wait_ge(sem("weighed"), weighed[0] - 1)
                return junk[weighed[0] % 2]

            def weigh(name, u0):
                v.wait_ge(sem(name + "_att_in"), 16)
                for b in range(2 * KC):
                    half, k = b // KC, b % KC
                    if b * HALF % UNIT == 0:
                        u = u0 + b * HALF // UNIT
                        v.wait_ge(sem(f"weights{u % REGION}_in"),
                                  16 * (u // REGION + (1 if u % REGION < PRELUDE else 0)))
                    at = (u % RING) * UNIT + b * HALF % UNIT
                    for i in range(2):
                        v.tensor_tensor_reduce(junk_of_two(), ring[:, at:at + HALF],
                                               att[name][:, i * D + half * HALF:i * D + (half + 1) * HALF], 1.0, 0.0,
                                               ALU.mult, ALU.add, wpart[:, i, half, k:k + 1]
                                               ).then_inc(sem("weighed"), 1)
                        weighed[0] += 1
                v.wait_ge(sem("weighed"), weighed[0])
                v.wait_ge(sem("rows_zero"), 4)
                v.tensor_tensor(watt[name][:, :, 0:DST + 1:DST].rearrange("p k i -> p i k"), wpart[:, :, 0, :],
                                wpart[:, :, 1, :], ALU.add).then_inc(sem(name + "_watt"), 1)
                v.wait_ge(sem(name + "_watt"), 1)

            v.wait_ge(sem("nodes"), 2 * LAYERS + 2)
            step(v.tensor_tensor(x[:, :], x[:, :], nodes[:, :], ALU.add))
            v.wait_ge(sem("actT_psum"), 2 * LAYERS + 4)
            weigh("c1", U_C1)
            for half in range(2):
                v.wait_ge(sem("q_proj"), half + 1)
                v.tensor_scalar(q_nat[:, half * HALF:(half + 1) * HALF], A[half][:, 0:HALF], DH ** -0.5, None,
                                ALU.mult).then_inc(sem("q_nat"), 1)
            weigh("c2", U_C2)
            for b in range(2):
                v.wait_ge(sem("kT_psum"), b + 1)
                v.tensor_copy(kT[0:DH, 4 * b:4 * b + 4, :].rearrange("p h n -> p (h n)"), A[b][0:DH, :]
                              ).then_inc(sem("kT"), 1)
            for b in range(2):
                v.wait_ge(sem("scores"), b + 1)
                sc = A[2 + b][:, :].rearrange("p (h n) -> p h n", h=4)
                step(v.tensor_reduce(small[:, 16 + 4 * b:20 + 4 * b], sc, AX.X, ALU.max))
                v.tensor_tensor(prob[:, 4 * b:4 * b + 4, :], sc,
                                small[:, 16 + 4 * b:20 + 4 * b].unsqueeze(2).broadcast_to([P, 4, P]),
                                ALU.subtract).then_inc(sem("score_shift"), 1)
            for b in range(2):
                v.wait_ge(sem("prob"), b + 1)
                step(v.tensor_reduce(small[:, 24 + 4 * b:28 + 4 * b], prob[:, 4 * b:4 * b + 4, :], AX.X, ALU.add))
            step(v.reciprocal(small[:, 32:40], small[:, 24:32]))
            for b in range(2):
                v.wait_ge(sem("attn_psum"), b + 1)
                v.tensor_tensor(norm[:, b * HALF:(b + 1) * HALF].rearrange("p (h n) -> p h n", h=4),
                                A[b][:, 0:HALF].rearrange("p (h n) -> p h n", h=4),
                                small[:, 32 + 4 * b:36 + 4 * b].unsqueeze(2).broadcast_to([P, 4, DH]),
                                ALU.mult).then_inc(sem("attended"), 1)

            def block_end(banks, name, n, dst=x, ready="x_ready"):
                for half in range(2):
                    v.wait_ge(sem(name), half + 1)
                    s = slice(half * HALF, (half + 1) * HALF)
                    step(v.tensor_tensor(x[:, s], banks[half][:, 0:HALF], x[:, s], ALU.add))
                    step(v.bn_stats(stats[:, 6 * half:6 * half + 6], x[:, s]))
                row_stats(n)
                for half in range(2):
                    s = slice(half * HALF, (half + 1) * HALF)
                    normalise(dst[:, s], x[:, s]).then_inc(sem(ready), 1)

            block_end(A[2:4], "out_proj", LAYERS)
            v.wait_ge(sem("x_ready"), 2)

            for b in range(3):
                v.wait_ge(sem("b1_raw"), b + 1)
                eb = e12[:, 4 * b:4 * b + 4, :]
                step(leaky(eb))
                v.tensor_reduce(small[:, 16 + 4 * b:20 + 4 * b], eb, AX.X, ALU.max, negate=True
                                ).then_inc(sem("b1_max"), 1)
            for b in range(3):
                v.wait_ge(sem("b1_exp"), b + 1)
                dn = small[:, 32 + 4 * b:36 + 4 * b]
                for h in range(4 * b, 4 * b + 4):
                    ins = v.tensor_tensor_reduce(e12[:, h, :], e12[:, h, :], cnt[:, :], 1.0, 0.0, ALU.mult, ALU.add,
                                                 small[:, 32 + h:33 + h])
                    done[0] += 1
                    ins.then_inc(sem("vector_step"), 1)
                v.wait_ge(sem("vector_step"), done[0])
                step(v.tensor_scalar(dn, dn, 1e-16, None, ALU.max))
                step(v.reciprocal(dn, dn))
                for h in range(4 * b, 4 * b + 4):
                    ins = v.tensor_scalar(e12[:, h, :], e12[:, h, :], small[:, 32 + h:33 + h], None, ALU.mult)
                ins.then_inc(sem("b1_alpha"), 1)
            for half in range(2):
                v.wait_ge(sem("b1_agg"), half + 1)
                s = slice(half * HALF, (half + 1) * HALF)
                step(v.scalar_tensor_tensor(x[:, s], A[2 + half][:, 0:HALF], 0.0, x[:, s], ALU.max, ALU.add))
                step(v.bn_stats(stats[:, 6 * half:6 * half + 6], x[:, s]))
            row_stats(LAYERS + 1)
            for half in range(2):
                s = slice(half * HALF, (half + 1) * HALF)
                normalise(x[:, s], x[:, s]).then_inc(sem("x_ready"), 1)
            v.wait_ge(sem("x_ready"), 4)

            def attention(heads, name, guard):
                if name in watt:
                    v.wait_ge(sem("rows_one"), 2)
                    v.wait_ge(sem("conv_terms"), TERMS[name])
                    step(v.tensor_copy(pair_r[0:1, :], G[1][0:1, 0:P]))
                    ins = v.tensor_copy(pair_l[DST:DST + 1, :], G[1][DST:DST + 1, 0:P])
                elif heads == 1:
                    ins = v.tensor_scalar(diag4[:, 0, :], ident[:, :], small[:, 0:1], None, ALU.mult)
                else:
                    ins = v.tensor_tensor(diag4[:, :, :], ident[:, :].unsqueeze(1).broadcast_to([P, heads, P]),
                                          small[:, 0:heads].unsqueeze(2).broadcast_to([P, heads, P]), ALU.mult)
                ins.then_inc(sem("conv_diag"), 1)
                v.wait_ge(sem("conv_raw"), CONV[name] + 1)
                e = e4[:, 0:heads, :]
                step(leaky(e))
                v.tensor_reduce(small[:, 8:8 + heads], e, AX.X, ALU.max, negate=True).then_inc(sem("conv_max"), 1)
                v.wait_ge(sem("conv_exp"), CONV[name] + 1)
                for h in range(heads):
                    ins = v.tensor_tensor_reduce(e4[:, h, :], e4[:, h, :], cnt_self[:, :], 1.0, 0.0, ALU.mult,
                                                 ALU.add, small[:, 12 + h:13 + h])
                    done[0] += 1
                    ins.then_inc(sem("vector_step"), 1)
                v.wait_ge(sem("vector_step"), done[0])
                if guard:
                    step(v.tensor_scalar(small[:, 12:12 + heads], small[:, 12:12 + heads], 1e-16, None, ALU.add))
                step(v.reciprocal(small[:, 16:16 + heads], small[:, 12:12 + heads]))
                for h in range(heads):
                    ins = v.tensor_scalar(e4[:, h, :], e4[:, h, :], small[:, 16 + h:17 + h], None, ALU.mult)
                ins.then_inc(sem("conv_alpha"), 1)

            def terms_of(heads, name, w):
                v.wait_ge(sem(name + "_att_in"), 16)
                o = 2 * w // heads if heads > 1 else w
                for half in range(2):
                    v.wait_ge(sem("conv_h"), 2 * CONV[name] + half + 1)
                    for i in range(2):
                        for h in range(w // o):
                            at = half * (w // o) + h
                            v.tensor_tensor_reduce(junk_of_two()[:, 0:o], h_nat[:, at * o:(at + 1) * o],
                                                   att[name][:, 2 * w * i + at * o:2 * w * i + (at + 1) * o],
                                                   1.0, 0.0, ALU.mult, ALU.add,
                                                   small[:, i * heads + at:i * heads + at + 1] if heads > 1 else
                                                   small[:, 20 + 2 * half + i:21 + 2 * half + i]
                                                   ).then_inc(sem("weighed"), 1)
                            weighed[0] += 1
                v.wait_ge(sem("weighed"), weighed[0])
                if heads == 1:
                    step(v.tensor_tensor(small[:, 0:2], small[:, 20:22], small[:, 22:24], ALU.add))

            attention(1, "c1", False)
            for c in range(HC):
                cc = HC + c
                v.wait_ge(sem("c1_agg"), KC)
                v.tensor_scalar(hidT[:, cc, :], T[1][:, c * P:(c + 1) * P],
                                cols[:, COL_C1B + cc:COL_C1B + cc + 1], 0.0, ALU.add, ALU.max
                                ).then_inc(sem("c1_outT_b"), 1)
            attention(1, "c2", False)
            block_end(A[0:2], "c2_agg", LAYERS + 2)
            v.wait_ge(sem("x_ready"), 6)

            terms_of(H3, "g1", 512)
            attention(H3, "g1", True)
            for half in range(2):
                v.wait_ge(sem("g1_agg"), half + 1)
                step(v.bn_stats(stats[:, 6 * half:6 * half + 6], T[half][:, :]))
            row_stats(LAYERS + 3)
            for half in range(2):
                normalise(norm[:, half * 512:(half + 1) * 512], T[half][:, :]).then_inc(sem("g1_norm"), 1)
            for c in range(K3):
                if c % 4 == 0:
                    v.wait_ge(sem("r1_proj"), c // 4 + 1)
                v.wait_ge(sem("g1_relu"), c + 1)
                v.scalar_tensor_tensor(hidT[:, c, :], A[2 + c // 4][:, (c % 4) * P:(c % 4 + 1) * P],
                                       cols[:, COL_R1B + c:COL_R1B + c + 1], hidT[:, c, :], ALU.add, ALU.add
                                       ).then_inc(sem("g1_outT"), 1)
            terms_of(1, "g2", HALF)
            attention(1, "g2", True)
            for half in range(2):
                v.wait_ge(sem("g2_agg"), half + 1)
                step(v.bn_stats(stats[:, 6 * half:6 * half + 6], A[half][:, 0:HALF]))
            row_stats(LAYERS + 4)
            v.wait_ge(sem("gain2_in"), 16)
            for half in range(2):
                s = slice(half * HALF, (half + 1) * HALF)
                step(v.scalar_tensor_tensor(norm[:, s], A[half][:, 0:HALF], mv[:, 0:1], gain2[:, s],
                                            ALU.subtract, ALU.mult))
                step(v.scalar_tensor_tensor(x[:, s], norm[:, s], rstd[:, 0:1], x[:, s], ALU.mult, ALU.add))
            block_end(A[2:4], "r2_proj", LAYERS + 5, norm, "out_ready")


def _np_inputs(inputs):
    import numpy as np

    a = {k: np.asarray(v) for k, v in inputs.items()}

    def halves(wT, w):
        n_in, n_out = wT.shape
        return wT.reshape(n_in // P, P, n_out // w, w).transpose(1, 2, 0, 3).reshape(P, -1)

    mats = [halves(a["L0_gnn_Wn"].T, HALF),
            a["L0_gnn_We"].T.reshape(2, P, D).transpose(1, 0, 2).reshape(P, -1)]
    for l in range(LAYERS):
        mats += [halves(a["L0_gnn_W1"][l].T, HALF), halves(a["L0_gnn_W2"][l].T, HALF)]
    qkv = a["L0_gnn_Wqkv"]
    mats += [halves(qkv[i * D:(i + 1) * D].T, HALF) for i in range(3)]
    mats += [halves(a["L0_gnn_Wo"].T, HALF), halves(a["L2_gnn_W1"], HALF), halves(a["L2_gnn_W2"], HALF)]
    mats += [halves(a["L3_gnn_W1"], 512), halves(a["L3_gnn_Wr1"], 512),
             halves(a["L3_gnn_W2"], HALF), halves(a["L3_gnn_Wr2"], HALF)]
    stream = np.concatenate(mats, axis=1)
    stream = stream.reshape(P, -1, UNIT).transpose(1, 0, 2)

    def columns(v):
        return v.reshape(-1, P).T

    cols = np.concatenate([columns(a[n]) for n in ("L0_gnn_be", "L2_gnn_b1", "L3_gnn_g1", "L3_gnn_be1",
                                                   "L0_gnn_ln_g", "L0_gnn_ln_b", "L3_gnn_br1")], axis=1)
    row = {"bn": "L0_gnn_bn", "b1": "L0_gnn_b1", "b2": "L0_gnn_b2", "bo": "L0_gnn_bo", "c2b": "L2_gnn_b2",
           "bqkv": "L0_gnn_bqkv", "g1b": "L3_gnn_b1", "g2b": "L3_gnn_b2",
           "r2b": "L3_gnn_br2", "ln2b": "L3_gnn_be2"}
    rows = np.concatenate([np.concatenate([a[row[n]].reshape(-1) for n, _ in g]).reshape(P, -1) for g in ROWS],
                          axis=1)
    W, Wr = a["L1_gnn_W"], a["L1_gnn_W_res"]
    wt = np.concatenate([W.T, Wr.T], axis=1)
    blk = np.concatenate([wt, wt], axis=0)
    blka = np.concatenate([W, W, a["L1_gnn_attn_l"][0].T, a["L1_gnn_attn_r"][0].T], axis=1)
    att = np.concatenate([a[n].reshape(-1) for n in (
        "L2_gnn_att_src1", "L2_gnn_att_dst1", "L2_gnn_att_src2", "L2_gnn_att_dst2",
        "L3_gnn_a_src1", "L3_gnn_a_dst1", "L3_gnn_a_src2", "L3_gnn_a_dst2", "L3_gnn_g2")]).reshape(1, -1)
    return {"x": a["x"], "src": a["src"].reshape(P, EC), "dst": a["dst"].reshape(P, EC),
            "edge": a["edge_attr_256"].reshape(P, EC, DE), "stream": stream, "cols": cols, "rows": rows,
            "blk": blk, "blka": blka, "att": att}


def kernel(**inputs):
    import numpy as np
    import concourse.bacc as bacc
    from concourse.bass_utils import run_bass_kernel_spmd as run

    nc = bacc.Bacc("TRN2", target_bir_lowering=False, num_devices=1)
    arrays, args = {}, []
    for name, a in _np_inputs(inputs).items():
        a = np.ascontiguousarray(a)
        arrays[f"in_{name}"] = a
        args.append(nc.dram_tensor(f"in_{name}", a.shape, mybir.dt.from_np(a.dtype), kind="ExternalInput").ap())
    out = nc.dram_tensor("out_x", (P, D), F32, kind="ExternalOutput").ap()
    gnn_kernel(nc, *args, out)
    return run(nc, [arrays], core_ids=[0]).results[0]["out_x"]
```

```python
import concourse.bass as bass
from concourse import mybir
from contextlib import ExitStack

F32 = mybir.dt.float32
BF16 = mybir.dt.bfloat16
F32R = mybir.dt.float32r
I32 = mybir.dt.int32
ALU = mybir.AluOpType
ACT = mybir.ActivationFunctionType
AX = mybir.AxisListType

P = 128
D = 768
DE = 256
E = 2176
EC = E // P
KC = D // P
HALF = D // 2
HC = 3
LAYERS = 3
H0, DH = 8, 96
H1, O1 = 12, 64
H3, O3 = 4, 256
D3 = H3 * O3
K3 = D3 // P
SLOPE = 0.2
EPS = 1e-5
MASKED = -1e30

UNIT = 1536
REGION = 9
RING = 2 * REGION
U_WN, U_WE, U_LAYERS, U_Q, U_K, U_V, U_WO, U_C1, U_C2 = 0, 3, 9, 36, 39, 42, 45, 48, 51
U_G1, U_R1, U_G2, U_R2, U_END = 54, 58, 62, 66, 70
assert U_Q == U_LAYERS + REGION * LAYERS
PRELUDE = 4
VECTOR_LOW = [0, 1, 2, 4, 5, 7, 8]
POOL_LOW = [3, 6]
EDGE_CUTS = [0, EC // 2, EC]


def place(u):
    if u < PRELUDE:
        return (RING - PRELUDE + u) * UNIT
    return (0 if u < U_Q else u // REGION % 2) * REGION * UNIT + u % REGION * UNIT


LATE = [*range(U_V, U_V + 3), *range(U_WO, U_WO + 3), *range(U_G1, U_R1), *range(U_G2, U_END)]


def high_place(u):
    if U_V <= u < U_V + 3:
        return (u - U_V) * UNIT
    if U_WO <= u < U_WO + 3:
        return (3 + u - U_WO) * UNIT
    if U_G1 <= u < U_R1:
        return (REGION + u - U_G1) * UNIT
    if U_G2 <= u < U_END:
        return (u - U_G2) * UNIT
    return (REGION + u % REGION) * UNIT


def unit_index(u):
    return u if u < PRELUDE else u - (REGION - PRELUDE)


ROWS = [
    [("bn", D)] + [("b1", LAYERS * D), ("b2", LAYERS * D)] + [("bo", D), ("c2b", D)],
    [("bqkv", 3 * D), ("g1b", D3), ("g2b", D), ("r2b", D), ("ln2b", D)],
]
ROW_BASE = [0, 32]
ROW_LEN = [sum(n for _, n in g) for g in ROWS]
ROW_COLS = [n // P for n in ROW_LEN]
ROW_AT = {}
for _g, _rows in enumerate(ROWS):
    _at = 0
    for _name, _n in _rows:
        ROW_AT[_name] = (_g, _at)
        _at += _n

COL_BE, COL_C1B, COL_G1G, COL_G1B, COL_LNG = 0, KC, 2 * KC, 2 * KC + K3, 2 * KC + 2 * K3
COL_LNB = COL_LNG + LAYERS * KC
COL_R1B = COL_LNB + LAYERS * KC
COLS = COL_R1B + K3

ATT_AT = {"c1": (0, 2 * D), "c2": (2 * D, 2 * D), "g1": (4 * D, 2 * D3), "g2": (4 * D + 2 * D3, 2 * D)}
CONV = {"c1": 0, "c2": 1, "g1": 2, "g2": 3}
DST = 32
TERMS = {"c1": 1, "c2": 2}
GAIN2_AT = 6 * D + 2 * D3
WARM = {"start": 8, "weights": 12, "hots": 8, "norm": 10, "prob": 4, "block": 12, "copy": 2, "b1": 6}


def gnn_kernel(nc, x_in, src_in, dst_in, edge_in, stream_in, cols_in, rows_in, blk_in, blka_in, att_in, out):
    ctx = ExitStack()
    with ctx:
        def sb(name, shape, dt=F32):
            return ctx.enter_context(nc.sbuf_tensor(name, shape, dt))

        sems = {}

        def sem(name):
            if name not in sems:
                sems[name] = ctx.enter_context(nc.semaphore(name))
            return sems[name]

        def sb_under(name, shape, parts):
            with nc.sbuf_tensor(name, shape, F32) as whole:
                pass
            return whole, [sb(*p) for p in parts]

        ring, (lows_r, highs_r) = sb_under("ring", [P, RING * UNIT], [("lows", [P, REGION * UNIT], F32R),
                                                                      ("highs", [P, REGION * UNIT], F32R)])

        def rounded(at, n):
            if at < REGION * UNIT:
                return lows_r[:, at:at + n]
            return highs_r[:, at - REGION * UNIT:at - REGION * UNIT + n]

        row3 = sb("row3", [P, max(ROW_LEN)], BF16)
        ones3 = sb("ones3", [P, P], BF16)
        parts = sb("parts", [P, 3, sum(ROW_COLS)], BF16)
        cols = sb("cols", [P, COLS])
        lncol = sb("lncol", [P, 2 * KC])
        warm = sb("warm", [P, 512], BF16)
        ident = sb("ident", [P, P])
        identb = sb("identb", [P, P], BF16)
        onesf = sb("onesf", [P, P])
        edge_idx = sb("edge_idx", [P, 2 * EC], I32)
        edge_f = sb("edge_f", [P, 2 * EC])
        iota_i = sb("iota_i", [P, 2 * P], I32)
        cnt = sb("cnt", [P, P])
        cnt_self = sb("cnt_self", [P, P])
        cntT = sb("cntT", [P, P])
        mixT = sb("mixT", [P, P])
        mask1 = sb("mask1", [P, 4, P], BF16)
        mask2 = sb("mask2", [P, 4, P], BF16)
        deg = sb("deg", [P, 1])
        degB = sb("degB", [P, P])
        x = sb("x", [P, D])
        nodes = sb("nodes", [P, D])
        actT = sb("actT", [P, KC, P])
        hidT = sb("hidT", [P, K3, P])
        norm = sb("norm", [P, D3])
        edge_sum = norm[:, 0:DE]
        edge_sumT = norm[:, DE:2 * DE].rearrange("p (k n) -> p k n", k=2)
        h_nat = sb("h_nat", [P, D3])
        pair = sb("pair", [P, 2, D])
        agg_full = pair[:, 0, :].rearrange("p (k n) -> p k n", k=KC)
        edge_term = pair[:, 1, :].rearrange("p (k n) -> p k n", k=KC)
        stats = sb("stats", [P, 12])
        mv = sb("mv", [P, 2])
        veps = sb("veps", [P, 1])
        mhalf = sb("mhalf", [P, 1])
        mrs = sb("mrs", [P, 1])
        rstd = sb("rstd", [P, 1])
        small = sb("small", [P, 64])
        bd = sb("bd", [P, 2 * P])
        blk = sb("blk", [P, 2 * O1])
        blka = sb("blka", [O1, 2 * O1 + 2 * H1])
        wlr = sb("wlr", [P, 2 * H1])

        RG = 2 * H1 * P + 4 * D + 4 * H0 * P - D
        with nc.sbuf_tensor("edge_parts", [P, EC * (2 * P + DE)], F32R) as edge_parts:
            pass
        region, (_, act_parts) = sb_under("region", [P, RG], [
            ("region_head", [P, RG - 6 * D], F32), ("act_parts", [P, 6 * D], F32R)])
        deep_high, deep_low = (act_parts[:, i * D3:(i + 1) * D3].rearrange("p (k n) -> p k n", k=K3) for i in (1, 2))
        assert 3 * D3 <= 4 * D
        agg_high, agg_low, hid_high, hid_low, act_high, act_low = (
            act_parts[:, i * D:(i + 1) * D].rearrange("p (k n) -> p k n", k=KC) for i in range(6))

        def part(at, n):
            return region[:, at:at + n]
        dst_hot = edge_parts[:, 0:EC * P].rearrange("p (k n) -> p k n", k=EC)
        src_edge = edge_parts[:, EC * P:EC * (2 * P + DE)].rearrange("p (k n) -> p k n", k=EC)
        E0 = (REGION - 3) * UNIT
        features = ring[:, E0:E0 + EC * DE].rearrange("p (k n) -> p k n", k=EC)
        features_low = lows_r[:, E0:E0 + EC * DE].rearrange("p (k n) -> p k n", k=EC)
        assert EC * DE <= 3 * UNIT
        TAIL = EC * (2 * P + DE)
        rows_f, rows_r = part(TAIL, sum(ROW_COLS)), part(TAIL + sum(ROW_COLS), sum(ROW_COLS))
        colf, maskf = part(TAIL + 2 * sum(ROW_COLS), P), part(TAIL + 2 * sum(ROW_COLS) + P, 2 * P)
        assert TAIL + 2 * sum(ROW_COLS) + 3 * P <= RG
        junk = [nodes[:, 0:HALF], nodes[:, HALF:D]]
        w_l = part(0, H1 * P).rearrange("p (h n) -> p h n", h=H1)
        w_r = part(H1 * P, H1 * P).rearrange("p (h n) -> p h n", h=H1)
        A0 = 2 * H1 * P
        q_nat, k_nat, v_nat = (part(A0 + i * D, D) for i in range(3))
        qT, kT, prob, probT = (part(A0 + 3 * D + i * H0 * P, H0 * P).rearrange("p (h n) -> p h n", h=H0)
                               for i in range(4))
        e12 = part(A0, H1 * P).rearrange("p (h n) -> p h n", h=H1)
        alphaT12 = part(A0 + H1 * P, H1 * P).rearrange("p (h n) -> p h n", h=H1)
        e4, diag4, alphaT4 = (part(i * 4 * P, 4 * P).rearrange("p (h n) -> p h n", h=4) for i in range(3))
        V0 = 12 * P
        att = {"c1": sb("att_c1", [P, 2 * D])[:, :], "c2": pair[:, :, :].rearrange("p a n -> p (a n)")[:, 0:2 * D],
               "g1": part(V0, 2 * D3), "g2": part(V0 + 2 * D3, 2 * D)}
        gain2 = part(V0 + 2 * D3 + 2 * D, D)
        assert V0 + 2 * D3 + 3 * D <= RG - 6 * D + D3
        watt = {n: sb("watt_" + n, [P, KC, DST + 1]) for n in ("c1", "c2")}
        pair_l = sb("pair_l", [DST + 1, P])
        pair_r = sb("pair_r", [DST + 1, P])
        wpart = sb("wpart", [P, 2, 2, KC])

        bank = [ctx.enter_context(nc.psum_tensor(f"bank{i}", [P, 512], F32)) for i in range(8)]
        A, T, G = bank[0:4], bank[4:6], bank[6:8]
        NB = [G[0], G[1], A[0], A[1]]

        scratch = nc.dram_tensor("row_parts", [3, sum(ROW_LEN)], BF16).ap()
        block = ctx.enter_context(nc.Block())

        @block.sync
        def _(sp):
            def load(row, at, j):
                sp.dma_start(ring[:, at:at + UNIT],
                             stream_in[bass.ds(row, 1), :, :].rearrange("o p n -> (o p) n")
                             ).then_inc(sem(f"weights{j}_in"), 16)

            def load_edges(i):
                k = slice(EDGE_CUTS[i], EDGE_CUTS[i + 1])
                sp.dma_start(features[:, k, :], edge_in[:, k, :]).then_inc(sem(f"edges{i}_in"), 16)

            def load_vectors(name):
                at, n = ATT_AT[name]
                sp.dma_start(att[name], att_in[:, at:at + n].partition_broadcast(P)).then_inc(sem(name + "_att_in"), 16)

            sp.dma_start(edge_idx[:, EC:2 * EC], dst_in).then_inc(sem("dst_in"), 16)
            sp.dma_start(edge_idx[:, 0:EC], src_in).then_inc(sem("src_in"), 16)
            sp.dma_start(x[:, :], x_in).then_inc(sem("x_in"), 16)
            load_edges(0)
            load(0, place(0), 0)
            sp.dma_start(rows_f, rows_in).then_inc(sem("rows_in"), 16)
            load_edges(1)
            load(1, place(1), 1)
            sp.wait_ge(sem("row_parts"), 1)
            at = col = 0
            for g in range(2):
                for j in range(3):
                    sp.dma_start(scratch[j, at:at + ROW_LEN[g]].rearrange("(p c) -> p c", c=ROW_COLS[g]),
                                 parts[:, j, col:col + ROW_COLS[g]]).then_inc(sem("row_scratch"), 16)
                at += ROW_LEN[g]
                col += ROW_COLS[g]
            load(2, place(2), 2)
            sp.wait_ge(sem("row_scratch"), 96)
            for g in range(2):
                sp.dma_start(row3[ROW_BASE[g]:ROW_BASE[g] + 3, 0:ROW_LEN[g]],
                             scratch[:, g * ROW_LEN[0]:g * ROW_LEN[0] + ROW_LEN[g]]).then_inc(sem("rows_ready"), 16)
            load(3, place(3), 3)
            sp.dma_start(cols[:, :], cols_in).then_inc(sem("cols_in"), 16)
            sp.dma_start(blka[:, :], blka_in).then_inc(sem("blka_in"), 16)
            sp.dma_start(blk[:, :], blk_in).then_inc(sem("blk_in"), 16)
            for j in range(REGION):
                if j < PRELUDE:
                    sp.wait_ge(sem(f"weights{j}_in"), 16)
                if j == REGION - 3:
                    sp.wait_ge(sem("edge_sums"), 1)
                load(PRELUDE + j, j * UNIT, j)
            load_vectors("c1")

            def layer_read(l, j):
                sp.wait_ge(sem("hidden_proj" if j < 6 else "update_proj"),
                           2 * l + 1 + (j // 3 if j < 6 else int(j > 6)))
                sp.nop(nofuse=True)
                sp.wait_ge(sem(f"weights{j}_in"), 16 * l + (32 if j < PRELUDE else 16))
                sp.nop(nofuse=True)

            with sp.Fori(0, LAYERS - 1) as l:
                for j in range(REGION):
                    layer_read(l, j)
                    load(l * REGION + (PRELUDE + REGION + j), j * UNIT, j)

            def follow(u):
                j = u % REGION
                sp.wait_ge(sem(f"weights{j}_in"), 16 * (u // REGION - (0 if j < PRELUDE else 1)))
                load(unit_index(u), place(u), j)

            for u in range(U_Q, U_V):
                layer_read(LAYERS - 1, u % REGION)
                load(unit_index(u), place(u), u % REGION)
            load_vectors("c2")
            for u in range(U_C1, U_C2):
                sp.wait_ge(sem(f"weights{u % REGION}_in"), 16 * (U_Q // REGION + (1 if u % REGION < PRELUDE else 0)))
                load(unit_index(u), place(u), u % REGION)
            for u in range(U_V, U_V + 3):
                layer_read(LAYERS - 1, u % REGION)
                load(unit_index(u), place(u), u % REGION)
            for u in range(U_C2, U_C2 + 3):
                follow(u)
            sp.wait_ge(sem("q_proj"), 2)
            for u in range(U_WO, U_WO + 3):
                follow(u)
            sp.wait_ge(sem("v_proj"), 2)
            for u in (*range(U_G1, U_G1 + 3), *range(U_G1 + 6, U_G1 + REGION)):
                follow(u)
            sp.wait_ge(sem("out_proj"), 2)
            for u in range(U_G1 + 3, U_G1 + 6):
                follow(u)
            sp.wait_ge(sem("b1_agg"), 2)
            load_vectors("g1")
            load_vectors("g2")
            sp.dma_start(gain2, att_in[:, GAIN2_AT:GAIN2_AT + D].partition_broadcast(P)).then_inc(sem("gain2_in"), 16)
            sp.wait_ge(sem("c1_proj"), 2)
            sp.wait_ge(sem("c1_watt"), 1)
            for u in range(U_R2 + 1, U_R2 + 3):
                follow(u)
            sp.wait_ge(sem("c2_proj"), 1)
            sp.wait_ge(sem("c2_watt"), 1)
            follow(U_R2 + 3)
            sp.wait_ge(sem("g1_proj"), 2)
            for u in range(U_G1 + REGION, U_R2 + 1):
                follow(u)
            for i in range(2):
                sp.wait_ge(sem("out_ready"), i + 1)
                sp.dma_start(out[:, i * HALF:(i + 1) * HALF], norm[:, i * HALF:(i + 1) * HALF]
                             ).then_inc(sem("out_stored"), 16)
            sp.wait_ge(sem("out_stored"), 32)

        @block.gpsimd
        def _(pool):
            pool.memset(warm[:, :], 0.0).then_inc(sem("warm"), 1)
            pool.iota(iota_i[:, 0:P], [[1, P]], base=0, channel_multiplier=-1).then_inc(sem("iotas"), 1)
            pool.iota(iota_i[:, P:2 * P], [[1, P]], base=0, channel_multiplier=0).then_inc(sem("iotas"), 1)
            pool.memset(onesf[:, :], 1.0).then_inc(sem("constants"), 1)
            pool.memset(ones3[:, :], 1.0).then_inc(sem("constants"), 1)
            pool.memset(mhalf[:, :], -0.5).then_inc(sem("mhalf"), 1)
            pool.memset(bd[:, :], 0.0).then_inc(sem("bd_zero"), 1)
            pool.wait_ge(sem("mhalf"), 1)
            for n in ("c1", "c2"):
                pool.memset(watt[n][:, :, :], 0.0).then_inc(sem("rows_zero"), 1)
            for i, t in enumerate((pair_l, pair_r)):
                pool.memset(t[:, :], 0.0).then_inc(sem("rows_zero"), 1)
                pool.wait_ge(sem("rows_zero"), 3 + i)
                r = DST * i
                pool.memset(t[r:r + 1, :], 1.0).then_inc(sem("rows_one"), 1)
                pool.wait_ge(sem("rows_one"), i + 1)

            def low_parts(l):
                for i, j in enumerate(POOL_LOW):
                    pool.wait_ge(sem("weight_high"), REGION * l + (j + 1))
                    pool.nop(nofuse=True)
                    u = slice(j * UNIT, (j + 1) * UNIT)
                    pool.tensor_tensor(lows_r[:, u], ring[:, u], highs_r[:, u].bitcast(F32), ALU.subtract
                                       ).then_inc(sem("weight_low_pool"), 1)
                    pool.wait_ge(sem("weight_low_pool"), len(POOL_LOW) * l + (i + 1))
                    pool.nop(nofuse=True)

            low_parts(0)

            def reciprocal_deviation(n):
                pool.wait_ge(sem("ln_var"), n + 1)
                pool.tensor_tensor(rstd[:, :], veps[:, :], mhalf[:, :], ALU.pow).then_inc(sem("ln_rstd"), 1)

            with pool.Fori(0, LAYERS - 1) as l:
                reciprocal_deviation(l)
                pool.wait_ge(sem("ln_rstd"), l + 1)
                pool.nop(nofuse=True)
                low_parts(l + 1)
            reciprocal_deviation(LAYERS - 1)
            pool.wait_ge(sem("edge_sums"), 1)
            pool.memset(w_l, 0.0).then_inc(sem("w_zero"), 1)
            pool.memset(w_r, 0.0).then_inc(sem("w_zero"), 1)
            pool.wait_ge(sem("w_zero"), 2)
            pool.wait_ge(sem("wlr"), 1)
            for i, w in enumerate((w_l, w_r)):
                for q in range(2):
                    s = slice(q * O1, (q + 1) * O1)
                    pool.tensor_copy(w[s, q:H1:2, :],
                                     wlr[s, i * H1 + q:(i + 1) * H1:2].unsqueeze(2).broadcast_to([O1, H1 // 2, P])
                                     ).then_inc(sem("w_lr"), 1)
                    pool.wait_ge(sem("w_lr"), 2 * i + q + 1)

            def late_low(u):
                n = LATE.index(u)
                pool.wait_ge(sem("late_high"), n + 1)
                pool.tensor_tensor(rounded(place(u), UNIT), ring[:, place(u):place(u) + UNIT],
                                   rounded(high_place(u), UNIT).bitcast(F32), ALU.subtract
                                   ).then_inc(sem("late_low"), 1)
                pool.wait_ge(sem("late_low"), n + 1)

            for u in range(U_V, U_V + 3):
                late_low(u)
            for u in range(U_WO, U_WO + 3):
                late_low(u)
            reciprocal_deviation(LAYERS)
            reciprocal_deviation(LAYERS + 1)
            for u in range(U_G1, U_R1):
                late_low(u)
            reciprocal_deviation(LAYERS + 2)
            for u in range(U_G2, U_G2 + 3):
                late_low(u)
            reciprocal_deviation(LAYERS + 3)
            for u in range(U_G2 + 3, U_END):
                late_low(u)
            reciprocal_deviation(LAYERS + 4)
            reciprocal_deviation(LAYERS + 5)

        @block.tensor
        def _(pe):
            def keep_warm(bank_, n):
                for _ in range(n):
                    pe.matmul(bank_[:, :], warm[:, 0:P], warm[:, :], start=True, stop=True)

            def arrived(u, j):
                pe.wait_ge(sem(f"weights{j}_in"), 16 * (u // REGION + (1 if j < PRELUDE else 0)))

            def add_row(dst, name, at, n, start=False, stop=True):
                g, off = ROW_AT[name]
                b = ROW_BASE[g]
                return pe.matmul(dst[:, 0:n], ones3[b:b + 3, :], row3[b:b + 3, bass.ds(at + off, n)],
                                 start=start, stop=stop)

            def products(u0, bank_, lhsT, chunks, half, w, ks, ready=None, stop=False):
                for k in ks:
                    b = (half * chunks + k) * w
                    u = u0 + b // UNIT
                    if b % UNIT == 0 or k == ks[0]:
                        arrived(u, u % REGION)
                    if ready is not None:
                        ready(k)
                    o = place(u) + b % UNIT
                    mm = pe.matmul(bank_[:, 0:w], lhsT[:, k, :], ring[:, o:o + w],
                                   start=(k == 0), stop=(stop and k == chunks - 1))
                return mm

            def project(u0, banks, lhsT, chunks, done, row=None, at=0, more=None, w=HALF, ready=None):
                for half in range(2):
                    mm = products(u0, banks[half], lhsT, chunks, half, w, range(chunks),
                                  ready if half == 0 else None, stop=row is None)
                    if row is not None:
                        mm = add_row(banks[half], row, at + half * w, w)
                    mm.then_inc(sem(done), 1)
                    if more is not None:
                        more(half)

            def layer_unit(l, j):
                if j in POOL_LOW:
                    pe.wait_ge(sem("weight_low_pool"), len(POOL_LOW) * l + (POOL_LOW.index(j) + 1))
                else:
                    pe.wait_ge(sem("weight_low"), len(VECTOR_LOW) * l + (VECTOR_LOW.index(j) + 1))

            def late_products(u0, bank_, parts_, chunks, half, w, passes=("high", "low"), ready=None, ks=None,
                              stop=False):
                high, low = parts_
                ks = range(chunks) if ks is None else ks
                for which in passes:
                    for k in ks:
                        b = (half * chunks + k) * w
                        u = u0 + b // UNIT
                        wh, wl = high_place(u) + b % UNIT, place(u) + b % UNIT
                        if ready is not None:
                            ready(which, k)
                        if which == "high":
                            if (b % UNIT == 0 or k == ks[0]) and u in LATE:
                                pe.wait_ge(sem("late_low"), LATE.index(u) + 1)
                            elif b % UNIT == 0 or k == ks[0]:
                                layer_unit(LAYERS, u % REGION)
                            pe.matmul(bank_[:, 0:w], high[:, k, :], rounded(wh, w), start=(k == 0), stop=False)
                            mm = pe.matmul(bank_[:, 0:w], high[:, k, :], rounded(wl, w), start=False, stop=False)
                        else:
                            mm = pe.matmul(bank_[:, 0:w], low[:, k, :], rounded(wh, w), start=False,
                                           stop=(stop and k == chunks - 1))
                return mm

            def late_project(u0, banks, parts_, done, row, at, ready=None, more=None):
                for half in range(2):
                    late_products(u0, banks[half], parts_, KC, half, HALF, ready=ready if half == 0 else None)
                    add_row(banks[half], row, at + half * HALF, HALF).then_inc(sem(done), 1)
                    if more is not None:
                        more(half)

            def halves_of_actT(n):
                def ready(k):
                    if k % HC == 0:
                        pe.wait_ge(sem("actT"), n + k // HC)
                return ready

            def transposes(src, banks, done, per=HC, n=KC):
                for c in range(n):
                    mm = pe.transpose(banks[c // per][:, (c % per) * P:(c % per + 1) * P],
                                      src[:, c * P:(c + 1) * P], ident[:, :])
                    if c % per == per - 1:
                        mm.then_inc(sem(done), 1)

            def edge_sums(i, low=False):
                for k in range(EDGE_CUTS[i], EDGE_CUTS[i + 1]):
                    o, moving = (P, features_low) if low else (0, src_edge)
                    mm = pe.matmul(G[0][:, o:P + DE], dst_hot[:, k, :], moving[:, k, :],
                                   start=(k == 0 and not low), stop=True, skip_group_check=True)
                return mm

            pe.wait_ge(sem("warm"), 1)
            keep_warm(A[3], WARM["start"])
            pe.wait_ge(sem("x_in"), 16)
            pe.wait_ge(sem("ident"), 1)
            transposes(x, T, "actT_psum")
            keep_warm(A[3], WARM["weights"])
            products(U_WN, A[0], actT, KC, 0, HALF, range(4), halves_of_actT(1))
            keep_warm(A[3], WARM["hots"])
            for i in range(2):
                pe.wait_ge(sem("one_hots"), 2)
                pe.wait_ge(sem("features_high"), i + 1)
                edge_sums(i)
            for i in range(2):
                pe.wait_ge(sem("features_low"), i + 1)
                mm = edge_sums(i, low=True)
            mm.then_inc(sem("edge_sums"), 1)
            products(U_WN, A[0], actT, KC, 0, HALF, range(4, KC))
            pe.wait_ge(sem("constants"), 2)
            pe.wait_ge(sem("rows_ready"), 32)
            add_row(A[0], "bn", 0, HALF).then_inc(sem("node_proj"), 1)
            pe.wait_ge(sem("cnt"), 1)
            pe.transpose(T[0][:, 0:P], cnt[:, :], ident[:, :]).then_inc(sem("graph_T"), 1)
            pe.wait_ge(sem("edge_sum"), 1)
            pe.transpose(T[1][:, 0:P], edge_sum[:, 0:P], ident[:, :])
            pe.transpose(T[1][:, P:2 * P], edge_sum[:, P:2 * P], ident[:, :]).then_inc(sem("graph_T"), 1)
            products(U_WN, A[1], actT, KC, 1, HALF, range(KC))
            add_row(A[1], "bn", HALF, HALF).then_inc(sem("node_proj"), 1)
            pe.wait_ge(sem("cntT"), 1)
            pe.wait_ge(sem("nodes"), 1)
            pe.matmul(A[0][:, 0:P], onesf[:, :], cntT[:, :], start=True, stop=True).then_inc(sem("deg_rows"), 1)
            pe.wait_ge(sem("edge_sumT"), 1)
            arrived(U_WE, U_WE)
            for c in range(KC):
                for k in range(2):
                    o = place(U_WE) + k * D + c * P
                    mm = pe.matmul(A[2 + c // HC][:, (c % HC) * P:(c % HC + 1) * P], ring[:, o:o + P],
                                   edge_sumT[:, k, :], start=(k == 0), stop=(k == 1))
                if c % HC == HC - 1:
                    mm.then_inc(sem("edge_proj"), 1)
            pe.wait_ge(sem("blka_in"), 16)
            pe.wait_ge(sem("degB"), 1)
            pe.matmul(A[0][:, 0:2 * H1], blka[:, 0:P], blka[:, P:P + 2 * H1], start=True, stop=True
                      ).then_inc(sem("wlr_psum"), 1)
            pe.wait_ge(sem("mixT"), 1)
            pe.wait_ge(sem("wlr"), 1)
            def split_products(l, bank_, b0, xs, bias, done):
                for k, (high, _, ready, _) in enumerate(xs):
                    b = b0 + k * HALF
                    ready()
                    if b % UNIT == 0 or k == 0:
                        layer_unit(l, b // UNIT)
                    pe.matmul(bank_[:, 0:HALF], high, highs_r[:, b:b + HALF],
                              start=(k == 0), stop=False)
                    pe.matmul(bank_[:, 0:HALF], high, lows_r[:, b:b + HALF],
                              start=False, stop=False)
                for k, (_, low, _, ready) in enumerate(xs):
                    b = b0 + k * HALF
                    ready()
                    pe.matmul(bank_[:, 0:HALF], low, highs_r[:, b:b + HALF],
                              start=False, stop=False)
                add_row(bank_, *bias).then_inc(sem(done), 1)

            def after(*waits):
                def ready():
                    for name, value in waits:
                        pe.wait_ge(sem(name), value)
                return ready

            def layer(l):
                for half in range(2):
                    pe.wait_ge(sem("nodes"), 2 * l + (half + 1))
                    for c in range(HC):
                        cc = half * HC + c
                        mm = pe.transpose(T[half][:, c * P:(c + 1) * P], nodes[:, cc * P:(cc + 1) * P], ident[:, :])
                    mm.then_inc(sem("actT_psum"), 1)
                    for c in range(HC):
                        cc = half * HC + c
                        mm = pe.matmul(G[half][:, c * P:(c + 1) * P], nodes[:, cc * P:(cc + 1) * P], mixT[:, :],
                                       start=True, stop=True)
                    mm.then_inc(sem("agg_psum"), 1)
                xs = [(act_high[:, k, :], act_low[:, k, :],
                       after(*([("act_high", 2 * l + (1 + k // HC))] if k % HC == 0 else [])),
                       after(*([("act_low", 2 * l + (1 + k // HC))] if k % HC == 0 else []))) for k in range(KC)]
                xs += [(agg_high[:, k, :], agg_low[:, k, :],
                        after(*([("agg_high", 2 * l + (1 + k // HC))] if k % HC == 0 else [])),
                        after(*([("agg_low", 2 * l + (1 + k // HC))] if k % HC == 0 else []))) for k in range(KC)]
                for half in range(2):
                    split_products(l, A[half], half * 2 * KC * HALF, xs, ("b1", l * D + half * HALF, HALF),
                                   "hidden_proj")
                keep_warm(A[2], WARM["norm"])
                for c in range(KC):
                    if c < 2:
                        pe.wait_ge(sem("hidden_norm_a"), 2 * l + (c + 1))
                    if c == HC:
                        pe.wait_ge(sem("hidden_norm_b"), l + 1)
                    pe.transpose(T[c // HC][:, (c % HC) * P:(c % HC + 1) * P], norm[:, c * P:(c + 1) * P],
                                 ident[:, :]).then_inc(sem("hidT_psum"), 1)
                xs = [(hid_high[:, k, :], hid_low[:, k, :],
                       after(("hid_high_a", HC * l + (k + 1)) if k < HC else ("hid_high_b", l + 1)),
                       after(("hid_low", 2 * l + (1 + k // HC)))) for k in range(KC)]
                for half in range(2):
                    split_products(l, A[2 + half], (2 * 2 * KC + half * KC) * HALF, xs,
                                   ("b2", l * D + half * HALF, HALF), "update_proj")

            with pe.Fori(0, LAYERS) as l:
                layer(l)

            for half in range(2):
                pe.wait_ge(sem("nodes"), 2 * LAYERS + half + 1)
                for c in range(HC):
                    cc = half * HC + c
                    mm = pe.transpose(T[half][:, c * P:(c + 1) * P], nodes[:, cc * P:(cc + 1) * P], ident[:, :])
                mm.then_inc(sem("actT_psum"), 1)
            late_project(U_Q, A[0:2], (act_high, act_low), "q_proj", "bqkv", 0,
                         lambda which, k: pe.wait_ge(sem("act_" + which), 2 * LAYERS + k // HC + 1)
                         if k % HC == 0 else None)
            project(U_K, A[2:4], actT, KC, "k_proj", "bqkv", D, ready=halves_of_actT(3))

            def head_transposes(src, banks, done):
                for h in range(H0):
                    mm = pe.transpose(banks[h // 4][0:DH, (h % 4) * P:(h % 4 + 1) * P],
                                      src[:, h * DH:(h + 1) * DH], ident[:, :])
                    if h % 4 == 3:
                        mm.then_inc(sem(done), 1)

            def between(half):
                if half == 0:
                    pe.wait_ge(sem("q_nat"), 2)
                    head_transposes(q_nat, T, "qT_psum")
                    pe.wait_ge(sem("k_nat"), 2)
                    head_transposes(k_nat, A[0:2], "kT_psum")
            late_project(U_V, G, (act_high, act_low), "v_proj", "bqkv", 2 * D, more=between)
            for b in range(2):
                pe.wait_ge(sem("qT"), b + 1)
                pe.wait_ge(sem("kT"), b + 1)
                for h in range(4 * b, 4 * b + 4):
                    mm = pe.matmul(A[2 + b][:, (h % 4) * P:(h % 4 + 1) * P], qT[0:DH, h, :], kT[0:DH, h, :],
                                   start=True, stop=True)
                mm.then_inc(sem("scores"), 1)
            pe.wait_ge(sem("v_nat"), 2)
            for b in range(2):
                keep_warm(G[0], WARM["prob"])
                pe.wait_ge(sem("prob"), b + 1)
                for h in range(4 * b, 4 * b + 4):
                    mm = pe.transpose(T[b][:, (h % 4) * P:(h % 4 + 1) * P], prob[:, h, :], ident[:, :])
                mm.then_inc(sem("probT_psum"), 1)
            for b in range(2):
                pe.wait_ge(sem("probT"), b + 1)
                for h in range(4 * b, 4 * b + 4):
                    mm = pe.matmul(A[b][:, (h % 4) * DH:(h % 4 + 1) * DH], probT[:, h, :],
                                   v_nat[:, h * DH:(h + 1) * DH], start=True, stop=True)
                mm.then_inc(sem("attn_psum"), 1)
            for half in range(2):
                pe.wait_ge(sem("attended"), half + 1)
                for c in range(HC):
                    cc = half * HC + c
                    mm = pe.transpose(G[half][:, c * P:(c + 1) * P], norm[:, cc * P:(cc + 1) * P], ident[:, :])
                mm.then_inc(sem("attnT_psum"), 1)
            late_project(U_WO, A[2:4], (hid_high, hid_low), "out_proj", "bo", 0,
                         lambda which, k: pe.wait_ge(sem("attnT_" + which), k // HC + 1) if k % HC == 0 else None)

            def x_transposes(n):
                keep_warm(G[0], WARM["block"])
                for half in range(2):
                    pe.wait_ge(sem("x_ready"), 2 * n + half + 1)
                    for c in range(HC):
                        cc = half * HC + c
                        mm = pe.transpose(T[half][:, c * P:(c + 1) * P], x[:, cc * P:(cc + 1) * P], ident[:, :])
                    mm.then_inc(sem("actT_psum"), 1)
                keep_warm(G[0], WARM["copy"])

            x_transposes(0)
            pe.wait_ge(sem("actT"), 6)
            pe.wait_ge(sem("bd"), 4)
            pe.wait_ge(sem("masks"), 2)
            pe.wait_ge(sem("w_lr"), 4)
            EB = [G[0], G[1], T[0]]
            for b in range(3):
                pe.matmul(EB[b][:, :], identb[:, :], mask1[:, :, :].rearrange("p h n -> p (h n)"),
                          start=True, stop=True)
                for h in range(4 * b, 4 * b + 4):
                    o = EB[b][:, (h % 4) * P:(h % 4 + 1) * P]
                    pe.matmul(o, w_l[:, h, :], actT[:, h // 2, :], start=False, stop=True, skip_group_check=True)
                    mm = pe.matmul(o, actT[:, h // 2, :], w_r[:, h, :], start=False, stop=True,
                                   skip_group_check=True)
                mm.then_inc(sem("b1_logits"), 1)
            for c in range(KC):
                mm = pe.matmul(A[c // HC][:, (c % HC) * P:(c % HC + 1) * P], actT[:, c, :], bd[:, 0:P],
                               start=True, stop=True)
                if c % HC == HC - 1:
                    mm.then_inc(sem("ft_psum"), 1)
            for c in range(KC):
                pe.matmul(A[2 + c // HC][:, (c % HC) * P:(c % HC + 1) * P], actT[:, c, :], bd[:, P:2 * P],
                          start=(c % HC == 0), stop=True, skip_group_check=True)
            keep_warm(T[1], WARM["b1"])
            pe.wait_ge(sem("ft"), 2)
            AB = [A[0], A[1], T[1]]
            for b in range(3):
                if b > 0:
                    keep_warm(T[1] if b == 1 else G[0], WARM["b1"])
                pe.wait_ge(sem("b1_alpha"), b + 1)
                for h in range(4 * b, 4 * b + 4):
                    mm = pe.transpose(AB[b][:, (h % 4) * P:(h % 4 + 1) * P], e12[:, h, :], ident[:, :])
                mm.then_inc(sem("b1_alphaT_psum"), 1)
            for h in range(H1):
                if h % 4 == 0:
                    pe.wait_ge(sem("b1_alphaT"), h // 4 + 1)
                mm = pe.matmul(A[2 + h // 6][:, (h % 6) * O1:(h % 6 + 1) * O1], alphaT12[:, h, :],
                               h_nat[:, h * O1:(h + 1) * O1], start=False, stop=True, skip_group_check=True)
                if h % 6 == 5:
                    mm.then_inc(sem("b1_agg"), 1)

            def terms(lhsT, name, ready=None):
                pe.wait_ge(sem(name + "_watt"), 1)
                for k in range(KC):
                    if ready is not None:
                        ready(k)
                    mm = pe.matmul(G[1][0:DST + 1, 0:P], watt[name][:, k, :], lhsT[:, k, :],
                                   start=(k == 0), stop=(k == KC - 1))
                mm.then_inc(sem("conv_terms"), 1)

            def logits(eb, heads, name):
                pe.matmul(eb[:, 0:heads * P], identb[:, :], mask2[:, 0:heads, :].rearrange("p h n -> p (h n)"),
                          start=True, stop=False)
                pe.wait_ge(sem("conv_diag"), CONV[name] + 1)
                if name in watt:
                    mm = pe.matmul(eb[:, 0:P], pair_l[:, :], pair_r[:, :], start=False, stop=True)
                else:
                    mm = pe.matmul(eb[:, 0:heads * P], onesf[:, :],
                                   diag4[:, 0:heads, :].rearrange("p h n -> p (h n)"), start=False, stop=True)
                mm.then_inc(sem("conv_logits"), 1)

            def alpha_transposes(ab, heads, name):
                pe.wait_ge(sem("conv_alpha"), CONV[name] + 1)
                for h in range(heads):
                    mm = pe.transpose(ab[:, h * P:(h + 1) * P], e4[:, h, :], ident[:, :])
                mm.then_inc(sem("conv_alphaT_psum"), 1)

            def convolve(u0, banks, lhsT, name):
                products(u0, banks[0], lhsT, KC, 0, HALF, range(KC), stop=True).then_inc(sem(name + "_proj"), 1)
                logits(G[0], 1, name)
                products(u0, banks[1], lhsT, KC, 1, HALF, range(KC - 1))
                alpha_transposes(G[1], 1, name)
                products(u0, banks[1], lhsT, KC, 1, HALF, [KC - 1], stop=True).then_inc(sem(name + "_proj"), 1)
                pe.wait_ge(sem("conv_alphaT"), CONV[name] + 1)

            x_transposes(1)
            pe.wait_ge(sem("actT"), 8)
            terms(actT, "c1")
            convolve(U_C1, A[0:2], actT, "c1")
            for c in range(KC):
                if c % HC == 0:
                    pe.wait_ge(sem("conv_h"), 2 * CONV["c1"] + c // HC + 1)
                pe.matmul(T[c // HC][:, (c % HC) * P:(c % HC + 1) * P], h_nat[:, c * P:(c + 1) * P],
                          alphaT4[:, 0, :], start=True, stop=True).then_inc(sem("c1_agg"), 1)

            def c1_out(k):
                pe.wait_ge(sem("c1_outT_a" if k < HC else "c1_outT_b"), k % HC + 1)
            terms(hidT, "c2", c1_out)
            convolve(U_C2, A[2:4], hidT, "c2")
            for half in range(2):
                pe.wait_ge(sem("conv_h"), 2 * CONV["c2"] + half + 1)
                pe.matmul(A[half][:, 0:HALF], alphaT4[:, 0, :], h_nat[:, half * HALF:(half + 1) * HALF],
                          start=True, stop=False)
                add_row(A[half], "c2b", half * HALF, HALF).then_inc(sem("c2_agg"), 1)

            x_transposes(2)
            for half in range(2):
                late_products(U_G1, A[half], (act_high, act_low), KC, half, 512, stop=True, ready=None if half else (
                    lambda which, k: pe.wait_ge(sem("act_" + which), 2 * LAYERS + 3 + k // HC)
                    if k % HC == 0 else None)).then_inc(sem("g1_proj"), 1)
            pe.wait_ge(sem("actT"), 10)

            def residual(cs):
                for c in cs:
                    for k in range(KC):
                        b = (c // 4 * KC + k) * 512
                        if c % 4 == 0 and b % UNIT == 0:
                            arrived(U_R1 + b // UNIT, (U_R1 + b // UNIT) % REGION)
                        o = place(U_R1 + b // UNIT) + b % UNIT + c % 4 * P
                        mm = pe.matmul(A[2 + c // 4][:, (c % 4) * P:(c % 4 + 1) * P], ring[:, o:o + P],
                                       actT[:, k, :], start=(k == 0), stop=(k == KC - 1))
                    if c % 4 == 3:
                        mm.then_inc(sem("r1_proj"), 1)

            residual(range(2))
            logits(G[0], H3, "g1")
            residual(range(2, 7))
            alpha_transposes(G[1], H3, "g1")
            residual([7])
            pe.wait_ge(sem("conv_alphaT"), CONV["g1"] + 1)
            for half in range(2):
                add_row(T[half], "g1b", half * 512, 512, start=True)
                pe.wait_ge(sem("conv_h"), 2 * CONV["g1"] + half + 1)
                for h in (2 * half, 2 * half + 1):
                    mm = pe.matmul(T[half][:, (h % 2) * O3:(h % 2 + 1) * O3], alphaT4[:, h, :],
                                   h_nat[:, h * O3:(h + 1) * O3], start=False, stop=True, skip_group_check=True)
                mm.then_inc(sem("g1_agg"), 1)
            keep_warm(A[0], WARM["norm"])
            for c in range(K3):
                if c % 4 == 0:
                    pe.wait_ge(sem("g1_norm"), c // 4 + 1)
                mm = pe.transpose(NB[c // 2][:, (c % 2) * P:(c % 2 + 1) * P], norm[:, c * P:(c + 1) * P],
                                  ident[:, :])
                if c % 2 == 1:
                    mm.then_inc(sem("g1_normT_psum"), 1)
            deep = (deep_high, deep_low)
            for half in range(2):
                late_products(U_G2, T[half], deep, K3, half, HALF, ["high"],
                              None if half else lambda which, k: pe.wait_ge(sem("g1_outT"), k + 1))
            for half in range(2):
                late_products(U_G2, T[half], deep, K3, half, HALF, ["low"], stop=True, ready=None if half else (
                    lambda which, k: pe.wait_ge(sem("deep_low"), k // 4 + 1) if k % 4 == 0 else None)
                              ).then_inc(sem("g2_proj"), 1)

            def second_residual(half, passes, ks=range(K3)):
                late_products(U_R2, A[2 + half], deep, K3, half, HALF, passes, ks=ks)

            def residual_rows(half):
                add_row(A[2 + half], "r2b", half * HALF, HALF, stop=False)
                add_row(A[2 + half], "ln2b", half * HALF, HALF).then_inc(sem("r2_proj"), 1)

            second_residual(0, ["high"])
            logits(G[0], 1, "g2")
            second_residual(0, ["low"])
            residual_rows(0)
            second_residual(1, ["high"], range(4))
            alpha_transposes(G[1], 1, "g2")
            second_residual(1, ["low"], range(4))
            pe.wait_ge(sem("conv_alphaT"), CONV["g2"] + 1)
            for i in range(2):
                pe.wait_ge(sem("conv_h"), 2 * CONV["g2"] + i + 1)
                pe.matmul(A[i][:, 0:HALF], alphaT4[:, 0, :], h_nat[:, i * HALF:(i + 1) * HALF],
                          start=True, stop=False)
                add_row(A[i], "g2b", i * HALF, HALF).then_inc(sem("g2_agg"), 1)
            second_residual(1, ["high", "low"], range(4, K3))
            residual_rows(1)

        @block.scalar
        def _(act):
            def copy_actT(n):
                for half in range(2):
                    act.wait_ge(sem("actT_psum"), n + half + 1)
                    act.copy(actT[:, half * HC:(half + 1) * HC, :].rearrange("p k n -> p (k n)"),
                             T[half][:, 0:HALF]).then_inc(sem("actT"), 1)

            def high_part(l, j):
                act.wait_ge(sem(f"weights{j}_in"), 16 * l + (32 if j < PRELUDE else 16))
                act.nop(nofuse=True)
                u = slice(j * UNIT, (j + 1) * UNIT)
                act.copy(highs_r[:, u], ring[:, u]).then_inc(sem("weight_high"), 1)

            copy_actT(0)
            for i in range(2):
                k = slice(EDGE_CUTS[i], EDGE_CUTS[i + 1])
                act.wait_ge(sem(f"edges{i}_in"), 16)
                act.copy(src_edge[:, k, P:P + DE], features[:, k, :]).then_inc(sem("features_high"), 1)
            act.wait_ge(sem("cnt"), 1)
            act.copy(edge_sum[:, :], G[0][:, P:P + DE]).then_inc(sem("edge_sum"), 1)
            act.wait_ge(sem("graph_T"), 2)
            act.copy(edge_sumT[:, :, :].rearrange("p k n -> p (k n)"), T[1][:, 0:2 * P]
                     ).then_inc(sem("edge_sumT"), 1)
            high_part(0, 0)
            high_part(0, 1)
            act.wait_ge(sem("deg_rows"), 1)
            act.copy(degB[:, :], A[0][:, 0:P]).then_inc(sem("degB"), 1)
            act.wait_ge(sem("wlr_psum"), 1)
            act.copy(wlr[:, :], A[0][:, 0:2 * H1]).then_inc(sem("wlr"), 1)
            high_part(0, 2)

            def layer(l):
                for half in range(2):
                    s = slice(half * HC, (half + 1) * HC)
                    act.wait_ge(sem("actT_psum"), 2 * l + (3 + half))
                    act.copy(act_high[:, s, :].rearrange("p k n -> p (k n)"), T[half][:, 0:HALF]
                             ).then_inc(sem("act_high"), 1)
                for half in range(2):
                    s = slice(half * HC, (half + 1) * HC)
                    act.wait_ge(sem("agg_full"), 2 * l + (half + 1))
                    act.copy(agg_high[:, s, :].rearrange("p k n -> p (k n)"),
                             agg_full[:, s, :].rearrange("p k n -> p (k n)")).then_inc(sem("agg_high"), 1)
                for j in range(3, REGION):
                    high_part(l, j)
                act.wait_ge(sem("hidden_proj"), 2 * l + 1)
                act.nop(nofuse=True)
                high_part(l + 1, 0)
                act.wait_ge(sem("ln_shift"), l + 1)
                act.activation(norm[:, HALF:D], A[1][:, 0:HALF], ACT.Identity, bias=mrs[:, 0:1],
                               scale=rstd[:, 0:1]).then_inc(sem("hidden_norm_b"), 1)
                act.wait_ge(sem("lncol"), 2 * l + 2)
                act.wait_ge(sem("hidT_psum"), KC * l + HC)
                for dst, done in ((hid_high, "hid_high_a"), (hidT, "hid_full")):
                    for c in range(HC):
                        act.activation(dst[:, c, :], T[0][:, c * P:(c + 1) * P], ACT.Relu,
                                       bias=lncol[:, KC + c:KC + c + 1], scale=lncol[:, c:c + 1]
                                       ).then_inc(sem(done), 1)
                for j in (1, 2):
                    high_part(l + 1, j)

            with act.Fori(0, LAYERS) as l:
                layer(l)

            def high_copies(n, banks, dst, src_ready, done):
                for half in range(2):
                    act.wait_ge(sem(src_ready), n + half + 1)
                    act.copy(dst[:, half * HC:(half + 1) * HC, :].rearrange("p k n -> p (k n)"),
                             banks[half][:, 0:HALF]).then_inc(sem(done), 1)

            def late_high(u):
                act.wait_ge(sem(f"weights{u % REGION}_in"), 16 * (u // REGION + (1 if u % REGION < PRELUDE else 0)))
                act.copy(rounded(high_place(u), UNIT), ring[:, place(u):place(u) + UNIT]
                         ).then_inc(sem("late_high"), 1)

            high_copies(2 * LAYERS + 2, T, act_high, "actT_psum", "act_high")
            copy_actT(2 * LAYERS + 2)
            act.wait_ge(sem("q_proj"), 2)
            for u in range(U_V, U_V + 3):
                late_high(u)
            for half in range(2):
                act.wait_ge(sem("k_proj"), half + 1)
                act.copy(k_nat[:, half * HALF:(half + 1) * HALF], A[2 + half][:, 0:HALF]).then_inc(sem("k_nat"), 1)
            for b in range(2):
                act.wait_ge(sem("qT_psum"), b + 1)
                act.copy(qT[0:DH, 4 * b:4 * b + 4, :].rearrange("p h n -> p (h n)"), T[b][0:DH, :]
                         ).then_inc(sem("qT"), 1)
            for b in range(2):
                act.wait_ge(sem("kT_psum"), b + 1)
                act.copy(kT[0:DH, 4 * b:4 * b + 4, :].rearrange("p h n -> p (h n)"), A[b][0:DH, :]
                         ).then_inc(sem("kT"), 1)
            late_high(U_WO)
            for half in range(2):
                act.wait_ge(sem("v_proj"), half + 1)
                act.copy(v_nat[:, half * HALF:(half + 1) * HALF], G[half][:, 0:HALF]).then_inc(sem("v_nat"), 1)
            late_high(U_WO + 1)
            for b in range(2):
                act.wait_ge(sem("score_shift"), b + 1)
                pb = prob[:, 4 * b:4 * b + 4, :].rearrange("p h n -> p (h n)")
                act.activation(pb, pb, ACT.Exp).then_inc(sem("prob"), 1)
            act.wait_ge(sem("probT_psum"), 1)
            act.copy(probT[:, 0:4, :].rearrange("p h n -> p (h n)"), T[0][:, :]).then_inc(sem("probT"), 1)
            act.wait_ge(sem("probT_psum"), 2)
            act.copy(probT[:, 4:8, :].rearrange("p h n -> p (h n)"), T[1][:, :]).then_inc(sem("probT"), 1)
            late_high(U_WO + 2)
            high_copies(0, G, hid_high, "attnT_psum", "attnT_high")

            copy_actT(2 * LAYERS + 4)
            EB = [G[0], G[1], T[0]]
            for b in range(3):
                act.wait_ge(sem("b1_logits"), b + 1)
                act.activation(e12[:, 4 * b:4 * b + 4, :].rearrange("p h n -> p (h n)"), EB[b][:, :],
                               ACT.Copy).then_inc(sem("b1_raw"), 1)
            for b in range(3):
                act.wait_ge(sem("b1_max"), b + 1)
                for h in range(4 * b, 4 * b + 4):
                    ins = act.activation(e12[:, h, :], e12[:, h, :], ACT.Exp, bias=small[:, 16 + h:17 + h])
                ins.then_inc(sem("b1_exp"), 1)
                if b < 2:
                    act.wait_ge(sem("ft_psum"), b + 1)
                    act.copy(h_nat[:, b * HALF:(b + 1) * HALF], A[b][:, 0:HALF]).then_inc(sem("ft"), 1)
            AB = [A[0], A[1], T[1]]
            for b in range(3):
                act.wait_ge(sem("b1_alphaT_psum"), b + 1)
                act.copy(alphaT12[:, 4 * b:4 * b + 4, :].rearrange("p h n -> p (h n)"), AB[b][:, :]
                         ).then_inc(sem("b1_alphaT"), 1)

            def copy_h(banks, w, half, name):
                act.wait_ge(sem(name + "_proj"), half + 1)
                act.copy(h_nat[:, half * w:(half + 1) * w], banks[half][:, 0:w]).then_inc(sem("conv_h"), 1)

            def raw_logits(heads, name):
                act.wait_ge(sem("conv_logits"), CONV[name] + 1)
                for h in range(heads):
                    if name in watt:
                        ins = act.copy(e4[:, h, :], G[0][:, h * P:(h + 1) * P])
                    else:
                        ins = act.activation(e4[:, h, :], G[0][:, h * P:(h + 1) * P], ACT.Identity,
                                             bias=small[:, heads + h:heads + h + 1])
                ins.then_inc(sem("conv_raw"), 1)

            def exponentials(heads, name):
                act.wait_ge(sem("conv_max"), CONV[name] + 1)
                for h in range(heads):
                    ins = act.activation(e4[:, h, :], e4[:, h, :], ACT.Exp, bias=small[:, 8 + h:9 + h])
                ins.then_inc(sem("conv_exp"), 1)

            def copy_alphaT(heads, name):
                act.wait_ge(sem("conv_alphaT_psum"), CONV[name] + 1)
                act.copy(alphaT4[:, 0:heads, :].rearrange("p h n -> p (h n)"), G[1][:, 0:heads * P]
                         ).then_inc(sem("conv_alphaT"), 1)

            copy_actT(2 * LAYERS + 6)
            late_high(U_G1)
            late_high(U_G1 + 1)
            copy_h(A[0:2], HALF, 0, "c1")
            raw_logits(1, "c1")
            exponentials(1, "c1")
            copy_alphaT(1, "c1")
            copy_h(A[0:2], HALF, 1, "c1")
            for c in range(HC):
                act.wait_ge(sem("c1_agg"), HC)
                act.activation(hidT[:, c, :], T[0][:, c * P:(c + 1) * P], ACT.Relu,
                               bias=cols[:, COL_C1B + c:COL_C1B + c + 1]).then_inc(sem("c1_outT_a"), 1)
            late_high(U_G1 + 2)
            late_high(U_G1 + 3)
            copy_h(A[2:4], HALF, 0, "c2")
            raw_logits(1, "c2")
            exponentials(1, "c2")
            copy_alphaT(1, "c2")
            copy_h(A[2:4], HALF, 1, "c2")

            high_copies(2 * LAYERS + 8, T, act_high, "actT_psum", "act_high")
            copy_actT(2 * LAYERS + 8)
            copy_h(A[0:2], 512, 0, "g1")
            copy_h(A[0:2], 512, 1, "g1")
            late_high(U_G2)
            raw_logits(H3, "g1")
            late_high(U_G2 + 1)
            exponentials(H3, "g1")
            late_high(U_G2 + 2)
            copy_alphaT(H3, "g1")
            late_high(U_G2 + 3)
            act.wait_ge(sem("r1_proj"), 2)
            late_high(U_R2)
            for c in range(K3):
                if c % 2 == 0:
                    act.wait_ge(sem("g1_normT_psum"), c // 2 + 1)
                act.activation(hidT[:, c, :], NB[c // 2][:, (c % 2) * P:(c % 2 + 1) * P], ACT.Relu,
                               bias=cols[:, COL_G1B + c:COL_G1B + c + 1],
                               scale=cols[:, COL_G1G + c:COL_G1G + c + 1]).then_inc(sem("g1_relu"), 1)
            for u in range(U_R2 + 1, U_END):
                late_high(u)
            copy_h(T, HALF, 0, "g2")
            copy_h(T, HALF, 1, "g2")
            raw_logits(1, "g2")
            exponentials(1, "g2")
            copy_alphaT(1, "g2")

        @block.vector
        def _(v):
            done = [0]

            def step(ins):
                done[0] = done[0] + 1
                ins.then_inc(sem("vector_step"), 1)
                v.wait_ge(sem("vector_step"), done[0])

            v.wait_ge(sem("iotas"), 2)
            v.tensor_scalar(ident[:, :], iota_i[:, 0:P], 0.0, None, ALU.is_equal).then_inc(sem("ident"), 1)
            step(v.tensor_copy(colf[:, :], iota_i[:, P:2 * P]))
            v.wait_ge(sem("src_in"), 16)
            v.wait_ge(sem("dst_in"), 16)
            step(v.tensor_copy(edge_f[:, :], edge_idx[:, :]))
            cb = colf[:, :].unsqueeze(1).broadcast_to([P, EC, P])
            v.tensor_tensor(dst_hot, edge_f[:, EC:2 * EC].unsqueeze(2).broadcast_to([P, EC, P]), cb,
                            ALU.is_equal).then_inc(sem("one_hots"), 1)
            v.tensor_tensor(src_edge[:, :, 0:P], edge_f[:, 0:EC].unsqueeze(2).broadcast_to([P, EC, P]), cb,
                            ALU.is_equal).then_inc(sem("one_hots"), 1)
            v.wait_ge(sem("rows_in"), 16)
            step(v.tensor_copy(parts[:, 0, :], rows_f[:, :]))
            step(v.tensor_tensor(rows_r[:, :], rows_f[:, :], parts[:, 0, :], ALU.subtract))
            step(v.tensor_copy(parts[:, 1, :], rows_r[:, :]))
            step(v.tensor_tensor(rows_f[:, :], rows_r[:, :], parts[:, 1, :], ALU.subtract))
            v.tensor_copy(parts[:, 2, :], rows_f[:, :]).then_inc(sem("row_parts"), 1)
            for i in range(2):
                k = slice(EDGE_CUTS[i], EDGE_CUTS[i + 1])
                v.wait_ge(sem("features_high"), i + 1)
                v.tensor_tensor(features_low[:, k, :], features[:, k, :], src_edge[:, k, P:P + DE].bitcast(F32),
                                ALU.subtract).then_inc(sem("features_low"), 1)
            v.wait_ge(sem("ident"), 1)
            v.tensor_copy(identb[:, :], ident[:, :]).then_inc(sem("identb"), 1)
            def low_part(l, j):
                v.wait_ge(sem("weight_high"), REGION * l + (j + 1))
                u = slice(j * UNIT, (j + 1) * UNIT)
                v.tensor_tensor(lows_r[:, u], ring[:, u], highs_r[:, u].bitcast(F32), ALU.subtract
                                ).then_inc(sem("weight_low"), 1)

            v.wait_ge(sem("edge_sums"), 1)
            v.tensor_copy(cnt[:, :], G[0][:, 0:P]).then_inc(sem("cnt"), 1)
            v.wait_ge(sem("cnt"), 1)
            step(v.tensor_reduce(deg[:, :], cnt[:, :], AX.X, ALU.add))

            def copy_nodes(half):
                v.wait_ge(sem("node_proj"), half + 1)
                v.tensor_copy(nodes[:, half * HALF:(half + 1) * HALF], A[half][:, 0:HALF]).then_inc(sem("nodes"), 1)

            copy_nodes(0)
            v.wait_ge(sem("graph_T"), 1)
            v.tensor_copy(cntT[:, :], T[0][:, 0:P]).then_inc(sem("cntT"), 1)
            v.wait_ge(sem("cntT"), 1)
            v.scalar_tensor_tensor(mixT[:, :], ident[:, :], deg[:, 0:1], cntT[:, :], ALU.mult, ALU.add
                                   ).then_inc(sem("mixT"), 1)
            step(v.tensor_tensor(cnt_self[:, :], cnt[:, :], ident[:, :], ALU.add))
            step(v.tensor_scalar(maskf[:, 0:P], cnt[:, :], 0.5, MASKED, ALU.is_lt, ALU.mult))
            step(v.tensor_scalar(maskf[:, P:2 * P], cnt_self[:, :], 0.5, MASKED, ALU.is_lt, ALU.mult))
            for i, m in enumerate((mask1, mask2)):
                v.tensor_copy(m[:, :, :], maskf[:, i * P:(i + 1) * P].unsqueeze(1).broadcast_to([P, 4, P])
                              ).then_inc(sem("masks"), 1)
            v.wait_ge(sem("blk_in"), 16)
            v.wait_ge(sem("bd_zero"), 1)
            for i in range(2):
                for q in range(2):
                    v.tensor_copy(bd[q * O1:(q + 1) * O1, i * P + q * O1:i * P + (q + 1) * O1],
                                  blk[q * O1:(q + 1) * O1, i * O1:(i + 1) * O1]).then_inc(sem("bd"), 1)
            copy_nodes(1)
            low_part(0, 0)
            low_part(0, 1)
            v.wait_ge(sem("cols_in"), 16)
            v.wait_ge(sem("degB"), 1)
            for c in range(KC):
                if c % HC == 0:
                    v.wait_ge(sem("edge_proj"), c // HC + 1)
                ins = v.scalar_tensor_tensor(edge_term[:, c, :], degB[:, :], cols[:, COL_BE + c:COL_BE + c + 1],
                                             A[2 + c // HC][:, (c % HC) * P:(c % HC + 1) * P], ALU.mult, ALU.add)
            ins.then_inc(sem("edge_term"), 1)
            v.wait_ge(sem("edge_term"), 1)

            def row_variance():
                step(v.bn_aggr(mv[:, :], stats[:, :]))
                v.tensor_scalar(veps[:, :], mv[:, 1:2], EPS, None, ALU.add).then_inc(sem("ln_var"), 1)

            def row_stats(n):
                row_variance()
                v.wait_ge(sem("ln_rstd"), n + 1)

            def normalise(dst, src):
                return v.tensor_scalar(dst, src, mv[:, 0:1], rstd[:, 0:1], ALU.subtract, ALU.mult)

            def leaky(e):
                return v.scalar_tensor_tensor(e, e, SLOPE, e, ALU.mult, ALU.max)

            def half_of(t, half):
                return t[:, half * HC:(half + 1) * HC, :].rearrange("p k n -> p (k n)")

            def low_copies(n, banks, high, low, high_ready, done):
                for half in range(2):
                    v.wait_ge(sem(high_ready), n + half + 1)
                    v.tensor_tensor(half_of(low, half), banks[half][:, 0:HALF], half_of(high, half).bitcast(F32),
                                    ALU.subtract).then_inc(sem(done), 1)

            def layer(l):
                v.tensor_copy(lncol[:, 0:KC], cols[:, bass.ds(l * KC + COL_LNG, KC)]).then_inc(sem("lncol"), 1)
                v.tensor_copy(lncol[:, KC:2 * KC], cols[:, bass.ds(l * KC + COL_LNB, KC)]).then_inc(sem("lncol"), 1)

                for half in range(2):
                    v.wait_ge(sem("agg_psum"), 2 * l + (half + 1))
                    v.tensor_tensor(half_of(agg_full, half), G[half][:, 0:HALF], half_of(edge_term, half), ALU.add
                                    ).then_inc(sem("agg_full"), 1)
                low_part(l, 2)
                for half in range(2):
                    v.wait_ge(sem("act_high"), 2 * l + (1 + half))
                    v.tensor_tensor(half_of(act_low, half), T[half][:, 0:HALF],
                                    half_of(act_high, half).bitcast(F32),
                                    ALU.subtract).then_inc(sem("act_low"), 1)
                for half in range(2):
                    v.wait_ge(sem("agg_high"), 2 * l + (half + 1))
                    v.tensor_tensor(half_of(agg_low, half), half_of(agg_full, half),
                                    half_of(agg_high, half).bitcast(F32), ALU.subtract).then_inc(sem("agg_low"), 1)
                for j in (4, 5):
                    low_part(l, j)
                for half in range(2):
                    v.wait_ge(sem("hidden_proj"), 2 * l + (half + 1))
                    step(v.bn_stats(stats[:, 6 * half:6 * half + 6], A[half][:, 0:HALF]))
                    if half == 0:
                        low_part(l, 7)
                        low_part(l, 8)
                v.nop(nofuse=True)
                step(v.bn_aggr(mv[:, :], stats[:, :]))
                v.tensor_scalar(veps[:, :], mv[:, 1:2], EPS, None, ALU.add).then_inc(sem("ln_var"), 1)
                v.wait_ge(sem("ln_rstd"), l + 1)
                v.tensor_scalar(mrs[:, :], mv[:, 0:1], rstd[:, 0:1], -1.0, ALU.mult, ALU.mult
                                ).then_inc(sem("ln_shift"), 1)
                normalise(norm[:, 0:P], A[0][:, 0:P]).then_inc(sem("hidden_norm_a"), 1)
                normalise(norm[:, P:HALF], A[0][:, P:HALF]).then_inc(sem("hidden_norm_a"), 1)
                v.wait_ge(sem("hidT_psum"), KC * l + KC)
                v.wait_ge(sem("lncol"), 2 * l + 2)
                for c in range(HC):
                    cc = HC + c
                    ins = v.tensor_scalar(hidT[:, cc, :], T[1][:, c * P:(c + 1) * P], lncol[:, cc:cc + 1],
                                          lncol[:, KC + cc:KC + cc + 1], ALU.mult, ALU.add)
                step(ins)
                full, high = hidT[:, HC:2 * HC, :].rearrange("p k n -> p (k n)"), half_of(hid_high, 1)
                v.tensor_scalar(high, full, 0.0, None, ALU.max).then_inc(sem("hid_high_b"), 1)
                v.wait_ge(sem("hid_full"), HC * l + HC)
                v.tensor_tensor(half_of(hid_low, 0), half_of(hidT, 0), half_of(hid_high, 0).bitcast(F32),
                                ALU.subtract).then_inc(sem("hid_low"), 1)
                v.wait_ge(sem("hid_high_b"), l + 1)
                v.scalar_tensor_tensor(half_of(hid_low, 1), full, 0.0, high.bitcast(F32), ALU.max,
                                       ALU.subtract
                                       ).then_inc(sem("hid_low"), 1)
                for half in range(2):
                    low_part(l + 1, half)
                    v.wait_ge(sem("update_proj"), 2 * l + (half + 1))
                    nh = nodes[:, half * HALF:(half + 1) * HALF]
                    v.tensor_tensor(nh, A[2 + half][:, 0:HALF], nh, ALU.add).then_inc(sem("nodes"), 1)

            LINKS = 4
            at = done[0]
            with v.Fori(0, LAYERS) as l:
                done[0] = l * LINKS + at
                layer(l)
            done[0] = at + LAYERS * LINKS

            weighed = [0]

            def junk_of_two():
                if weighed[0] >= 2:
                    v.wait_ge(sem("weighed"), weighed[0] - 1)
                return junk[weighed[0] % 2]

            def weigh(name, u0, blocks=range(2 * KC)):
                v.wait_ge(sem(name + "_att_in"), 16)
                for b in blocks:
                    half, k = b // KC, b % KC
                    u = u0 + b * HALF // UNIT
                    if b * HALF % UNIT == 0 or b == blocks[0]:
                        v.wait_ge(sem(f"weights{u % REGION}_in"),
                                  16 * (u // REGION + (1 if u % REGION < PRELUDE else 0)))
                    at = place(u) + b * HALF % UNIT
                    for i in range(2):
                        v.tensor_tensor_reduce(junk_of_two(), ring[:, at:at + HALF],
                                               att[name][:, i * D + half * HALF:i * D + (half + 1) * HALF], 1.0, 0.0,
                                               ALU.mult, ALU.add, wpart[:, i, half, k:k + 1]
                                               ).then_inc(sem("weighed"), 1)
                        weighed[0] += 1
                v.wait_ge(sem("weighed"), weighed[0])
                if blocks[-1] != 2 * KC - 1:
                    return
                v.wait_ge(sem("rows_zero"), 4)
                v.tensor_tensor(watt[name][:, :, 0:DST + 1:DST].rearrange("p k i -> p i k"), wpart[:, :, 0, :],
                                wpart[:, :, 1, :], ALU.add).then_inc(sem(name + "_watt"), 1)
                v.wait_ge(sem(name + "_watt"), 1)

            low_part(LAYERS, 2)
            v.wait_ge(sem("actT"), 4)
            low_copies(2 * LAYERS, T, act_high, act_low, "act_high", "act_low")
            v.wait_ge(sem("nodes"), 2 * LAYERS + 2)
            step(v.tensor_tensor(x[:, :], x[:, :], nodes[:, :], ALU.add))
            v.wait_ge(sem("actT_psum"), 2 * LAYERS + 4)
            weigh("c1", U_C1)
            for half in range(2):
                v.wait_ge(sem("q_proj"), half + 1)
                v.tensor_scalar(q_nat[:, half * HALF:(half + 1) * HALF], A[half][:, 0:HALF], DH ** -0.5, None,
                                ALU.mult).then_inc(sem("q_nat"), 1)
            weigh("c2", U_C2, range(KC))
            for b in range(2):
                v.wait_ge(sem("scores"), b + 1)
                sc = A[2 + b][:, :].rearrange("p (h n) -> p h n", h=4)
                step(v.tensor_reduce(small[:, 16 + 4 * b:20 + 4 * b], sc, AX.X, ALU.max))
                v.tensor_tensor(prob[:, 4 * b:4 * b + 4, :], sc,
                                small[:, 16 + 4 * b:20 + 4 * b].unsqueeze(2).broadcast_to([P, 4, P]),
                                ALU.subtract).then_inc(sem("score_shift"), 1)
            for b in range(2):
                v.wait_ge(sem("prob"), b + 1)
                step(v.tensor_reduce(small[:, 24 + 4 * b:28 + 4 * b], prob[:, 4 * b:4 * b + 4, :], AX.X, ALU.add))
            step(v.reciprocal(small[:, 32:40], small[:, 24:32]))
            for b in range(2):
                v.wait_ge(sem("attn_psum"), b + 1)
                v.tensor_tensor(norm[:, b * HALF:(b + 1) * HALF].rearrange("p (h n) -> p h n", h=4),
                                A[b][:, 0:HALF].rearrange("p (h n) -> p h n", h=4),
                                small[:, 32 + 4 * b:36 + 4 * b].unsqueeze(2).broadcast_to([P, 4, DH]),
                                ALU.mult).then_inc(sem("attended"), 1)

            def block_end(banks, name, n):
                for half in range(2):
                    v.wait_ge(sem(name), half + 1)
                    s = slice(half * HALF, (half + 1) * HALF)
                    step(v.tensor_tensor(x[:, s], banks[half][:, 0:HALF], x[:, s], ALU.add))
                    step(v.bn_stats(stats[:, 6 * half:6 * half + 6], x[:, s]))
                row_stats(n)
                for half in range(2):
                    s = slice(half * HALF, (half + 1) * HALF)
                    normalise(x[:, s], x[:, s]).then_inc(sem("x_ready"), 1)

            low_copies(0, G, hid_high, hid_low, "attnT_high", "attnT_low")
            weigh("c2", U_C2, range(KC, KC + HC))
            block_end(A[2:4], "out_proj", LAYERS)
            v.wait_ge(sem("x_ready"), 2)

            for b in range(3):
                v.wait_ge(sem("b1_raw"), b + 1)
                eb = e12[:, 4 * b:4 * b + 4, :]
                step(leaky(eb))
                v.tensor_reduce(small[:, 16 + 4 * b:20 + 4 * b], eb, AX.X, ALU.max, negate=True
                                ).then_inc(sem("b1_max"), 1)
            for b in range(3):
                v.wait_ge(sem("b1_exp"), b + 1)
                dn = small[:, 32 + 4 * b:36 + 4 * b]
                for h in range(4 * b, 4 * b + 4):
                    ins = v.tensor_tensor_reduce(e12[:, h, :], e12[:, h, :], cnt[:, :], 1.0, 0.0, ALU.mult, ALU.add,
                                                 small[:, 32 + h:33 + h])
                    done[0] += 1
                    ins.then_inc(sem("vector_step"), 1)
                v.wait_ge(sem("vector_step"), done[0])
                step(v.tensor_scalar(dn, dn, 1e-16, None, ALU.max))
                step(v.reciprocal(dn, dn))
                for h in range(4 * b, 4 * b + 4):
                    ins = v.tensor_scalar(e12[:, h, :], e12[:, h, :], small[:, 32 + h:33 + h], None, ALU.mult)
                ins.then_inc(sem("b1_alpha"), 1)
            for half in range(2):
                v.wait_ge(sem("b1_agg"), half + 1)
                s = slice(half * HALF, (half + 1) * HALF)
                step(v.scalar_tensor_tensor(x[:, s], A[2 + half][:, 0:HALF], 0.0, x[:, s], ALU.max, ALU.add))
                step(v.bn_stats(stats[:, 6 * half:6 * half + 6], x[:, s]))
            row_stats(LAYERS + 1)
            for half in range(2):
                s = slice(half * HALF, (half + 1) * HALF)
                normalise(x[:, s], x[:, s]).then_inc(sem("x_ready"), 1)
            v.wait_ge(sem("x_ready"), 4)

            def attention(heads, name, guard):
                if name in watt:
                    v.wait_ge(sem("rows_one"), 2)
                    v.wait_ge(sem("conv_terms"), TERMS[name])
                    step(v.tensor_copy(pair_r[0:1, :], G[1][0:1, 0:P]))
                    ins = v.tensor_copy(pair_l[DST:DST + 1, :], G[1][DST:DST + 1, 0:P])
                elif heads == 1:
                    ins = v.tensor_scalar(diag4[:, 0, :], ident[:, :], small[:, 0:1], None, ALU.mult)
                else:
                    ins = v.tensor_tensor(diag4[:, :, :], ident[:, :].unsqueeze(1).broadcast_to([P, heads, P]),
                                          small[:, 0:heads].unsqueeze(2).broadcast_to([P, heads, P]), ALU.mult)
                ins.then_inc(sem("conv_diag"), 1)
                v.wait_ge(sem("conv_raw"), CONV[name] + 1)
                e = e4[:, 0:heads, :]
                step(leaky(e))
                v.tensor_reduce(small[:, 8:8 + heads], e, AX.X, ALU.max, negate=True).then_inc(sem("conv_max"), 1)
                v.wait_ge(sem("conv_exp"), CONV[name] + 1)
                for h in range(heads):
                    ins = v.tensor_tensor_reduce(e4[:, h, :], e4[:, h, :], cnt_self[:, :], 1.0, 0.0, ALU.mult,
                                                 ALU.add, small[:, 12 + h:13 + h])
                    done[0] += 1
                    ins.then_inc(sem("vector_step"), 1)
                v.wait_ge(sem("vector_step"), done[0])
                if guard:
                    step(v.tensor_scalar(small[:, 12:12 + heads], small[:, 12:12 + heads], 1e-16, None, ALU.add))
                step(v.reciprocal(small[:, 16:16 + heads], small[:, 12:12 + heads]))
                for h in range(heads):
                    ins = v.tensor_scalar(e4[:, h, :], e4[:, h, :], small[:, 16 + h:17 + h], None, ALU.mult)
                ins.then_inc(sem("conv_alpha"), 1)

            def terms_of(heads, name, w):
                v.wait_ge(sem(name + "_att_in"), 16)
                o = 2 * w // heads if heads > 1 else w
                for half in range(2):
                    v.wait_ge(sem("conv_h"), 2 * CONV[name] + half + 1)
                    for i in range(2):
                        for h in range(w // o):
                            at = half * (w // o) + h
                            v.tensor_tensor_reduce(junk_of_two()[:, 0:o], h_nat[:, at * o:(at + 1) * o],
                                                   att[name][:, 2 * w * i + at * o:2 * w * i + (at + 1) * o],
                                                   1.0, 0.0, ALU.mult, ALU.add,
                                                   small[:, i * heads + at:i * heads + at + 1] if heads > 1 else
                                                   small[:, 20 + 2 * half + i:21 + 2 * half + i]
                                                   ).then_inc(sem("weighed"), 1)
                            weighed[0] += 1
                v.wait_ge(sem("weighed"), weighed[0])
                if heads == 1:
                    step(v.tensor_tensor(small[:, 0:2], small[:, 20:22], small[:, 22:24], ALU.add))

            attention(1, "c1", False)
            weigh("c2", U_C2, range(KC + HC, 2 * KC))
            for c in range(HC):
                cc = HC + c
                v.wait_ge(sem("c1_agg"), KC)
                v.tensor_scalar(hidT[:, cc, :], T[1][:, c * P:(c + 1) * P],
                                cols[:, COL_C1B + cc:COL_C1B + cc + 1], 0.0, ALU.add, ALU.max
                                ).then_inc(sem("c1_outT_b"), 1)
            attention(1, "c2", False)
            block_end(A[0:2], "c2_agg", LAYERS + 2)
            v.wait_ge(sem("x_ready"), 6)

            v.wait_ge(sem("actT"), 10)
            low_copies(2 * LAYERS + 2, T, act_high, act_low, "act_high", "act_low")
            terms_of(H3, "g1", 512)
            attention(H3, "g1", True)
            for half in range(2):
                v.wait_ge(sem("g1_agg"), half + 1)
                step(v.bn_stats(stats[:, 6 * half:6 * half + 6], T[half][:, :]))
            row_stats(LAYERS + 3)
            for half in range(2):
                normalise(norm[:, half * 512:(half + 1) * 512], T[half][:, :]).then_inc(sem("g1_norm"), 1)
            def deep_sum(dst, c):
                return v.scalar_tensor_tensor(dst, A[2 + c // 4][:, (c % 4) * P:(c % 4 + 1) * P],
                                              cols[:, COL_R1B + c:COL_R1B + c + 1], hidT[:, c, :], ALU.add, ALU.add)

            for c in range(K3):
                if c % 4 == 0:
                    v.wait_ge(sem("r1_proj"), c // 4 + 1)
                v.wait_ge(sem("g1_relu"), c + 1)
                deep_sum(deep_high[:, c, :], c).then_inc(sem("g1_outT"), 1)
            for half in range(2):
                for c in range(4 * half, 4 * half + 4):
                    ins = deep_sum(norm[:, c * P:(c + 1) * P], c)
                step(ins)
                v.wait_ge(sem("g1_outT"), 4 * half + 4)
                v.tensor_tensor(deep_low[:, 4 * half:4 * half + 4, :].rearrange("p k n -> p (k n)"),
                                norm[:, half * 512:(half + 1) * 512],
                                deep_high[:, 4 * half:4 * half + 4, :].rearrange("p k n -> p (k n)").bitcast(F32),
                                ALU.subtract).then_inc(sem("deep_low"), 1)
            terms_of(1, "g2", HALF)
            attention(1, "g2", True)
            def add_residual(half):
                v.wait_ge(sem("r2_proj"), half + 1)
                s = slice(half * HALF, (half + 1) * HALF)
                step(v.tensor_tensor(x[:, s], A[2 + half][:, 0:HALF], x[:, s], ALU.add))

            add_residual(0)
            for half in range(2):
                v.wait_ge(sem("g2_agg"), half + 1)
                step(v.bn_stats(stats[:, 6 * half:6 * half + 6], A[half][:, 0:HALF]))
            row_variance()
            v.wait_ge(sem("gain2_in"), 16)
            for half in range(2):
                s = slice(half * HALF, (half + 1) * HALF)
                ins = v.scalar_tensor_tensor(norm[:, s], A[half][:, 0:HALF], mv[:, 0:1], gain2[:, s],
                                             ALU.subtract, ALU.mult)
            step(ins)
            v.wait_ge(sem("ln_rstd"), LAYERS + 5)
            for half in range(2):
                s = slice(half * HALF, (half + 1) * HALF)
                if half == 1:
                    add_residual(1)
                step(v.scalar_tensor_tensor(x[:, s], norm[:, s], rstd[:, 0:1], x[:, s], ALU.mult, ALU.add))
                step(v.bn_stats(stats[:, 6 * half:6 * half + 6], x[:, s]))
            row_stats(LAYERS + 5)
            for half in range(2):
                s = slice(half * HALF, (half + 1) * HALF)
                normalise(norm[:, s], x[:, s]).then_inc(sem("out_ready"), 1)


def _np_inputs(inputs):
    import numpy as np

    a = {k: np.asarray(v) for k, v in inputs.items()}

    def halves(wT, w):
        n_in, n_out = wT.shape
        return wT.reshape(n_in // P, P, n_out // w, w).transpose(1, 2, 0, 3).reshape(P, -1)

    mats = [halves(a["L0_gnn_Wn"].T, HALF),
            a["L0_gnn_We"].T.reshape(2, P, D).transpose(1, 0, 2).reshape(P, -1)]
    for l in range(LAYERS):
        mats += [halves(a["L0_gnn_W1"][l].T, HALF), halves(a["L0_gnn_W2"][l].T, HALF)]
    qkv = a["L0_gnn_Wqkv"]
    mats += [halves(qkv[i * D:(i + 1) * D].T, HALF) for i in range(3)]
    mats += [halves(a["L0_gnn_Wo"].T, HALF), halves(a["L2_gnn_W1"], HALF), halves(a["L2_gnn_W2"], HALF)]
    mats += [halves(a["L3_gnn_W1"], 512), halves(a["L3_gnn_Wr1"], 512),
             halves(a["L3_gnn_W2"], HALF), halves(a["L3_gnn_Wr2"], HALF)]
    stream = np.concatenate(mats, axis=1)
    stream = stream.reshape(P, -1, UNIT).transpose(1, 0, 2)

    def columns(v):
        return v.reshape(-1, P).T

    cols = np.concatenate([columns(a[n]) for n in ("L0_gnn_be", "L2_gnn_b1", "L3_gnn_g1", "L3_gnn_be1",
                                                   "L0_gnn_ln_g", "L0_gnn_ln_b", "L3_gnn_br1")], axis=1)
    row = {"bn": "L0_gnn_bn", "b1": "L0_gnn_b1", "b2": "L0_gnn_b2", "bo": "L0_gnn_bo", "c2b": "L2_gnn_b2",
           "bqkv": "L0_gnn_bqkv", "g1b": "L3_gnn_b1", "g2b": "L3_gnn_b2",
           "r2b": "L3_gnn_br2", "ln2b": "L3_gnn_be2"}
    rows = np.concatenate([np.concatenate([a[row[n]].reshape(-1) for n, _ in g]).reshape(P, -1) for g in ROWS],
                          axis=1)
    W, Wr = a["L1_gnn_W"], a["L1_gnn_W_res"]
    wt = np.concatenate([W.T, Wr.T], axis=1)
    blk = np.concatenate([wt, wt], axis=0)
    blka = np.concatenate([W, W, a["L1_gnn_attn_l"][0].T, a["L1_gnn_attn_r"][0].T], axis=1)
    att = np.concatenate([a[n].reshape(-1) for n in (
        "L2_gnn_att_src1", "L2_gnn_att_dst1", "L2_gnn_att_src2", "L2_gnn_att_dst2",
        "L3_gnn_a_src1", "L3_gnn_a_dst1", "L3_gnn_a_src2", "L3_gnn_a_dst2", "L3_gnn_g2")]).reshape(1, -1)
    return {"x": a["x"], "src": a["src"].reshape(P, EC), "dst": a["dst"].reshape(P, EC),
            "edge": a["edge_attr_256"].reshape(P, EC, DE), "stream": stream, "cols": cols, "rows": rows,
            "blk": blk, "blka": blka, "att": att}


def kernel(**inputs):
    import numpy as np
    import concourse.bacc as bacc
    from concourse.bass_utils import run_bass_kernel_spmd as run

    nc = bacc.Bacc("TRN2", target_bir_lowering=False, num_devices=1)
    arrays, args = {}, []
    for name, a in _np_inputs(inputs).items():
        a = np.ascontiguousarray(a)
        arrays[f"in_{name}"] = a
        args.append(nc.dram_tensor(f"in_{name}", a.shape, mybir.dt.from_np(a.dtype), kind="ExternalInput").ap())
    out = nc.dram_tensor("out_x", (P, D), F32, kind="ExternalOutput").ap()
    gnn_kernel(nc, *args, out)
    return run(nc, [arrays], core_ids=[0]).results[0]["out_x"]
```
